# Optimizing a Trainium2 kernel written in Bass

```python
import numpy as np
import jax
import jax.numpy as jnp

def _softmax(x, axis=-1):
    return jax.nn.softmax(x, axis=axis)

def _gelu(x):
    return jax.nn.gelu(x, approximate=True)

def _silu(x):
    return jax.nn.silu(x)

def _sigmoid(x):
    return jax.nn.sigmoid(x)

def _layernorm(x, axis=-1, eps=1e-05):
    m = jnp.mean(x, axis=axis, keepdims=True)
    v = jnp.var(x, axis=axis, keepdims=True)
    return (x - m) / jnp.sqrt(v + eps)

def _scatter_add(tgt, idx, src, axis=0):
    return tgt.at[idx].add(src)

def _segment_sum(src, seg, n):
    return jax.ops.segment_sum(src, seg, n)
kernel_name = 'mk_lm_tower_d1_tok_ids768_r4_ca64c2'

def setup_inputs(seed: int=0):
    np.random.seed(seed)
    _w = jnp.asarray

    def _rec_inputs():
        import jax
        import jax.numpy as jnp
        _rk = jax.random.key(seed)
        x = jax.random.randint(jax.random.fold_in(_rk, 1), (8, 256), 0, 31993, jnp.int32)
        return x
    x = _rec_inputs()

    def _L0_tok_setup():
        import jax, jax.numpy as jnp
        import numpy as np
        B, S, D, L, K, V = (8, 256, 192, 4, 4, 8000)
        N = D
        EPS = 1e-05

        def _layernorm(x, g, b):
            m = jnp.mean(x, axis=-1, keepdims=True)
            v = jnp.mean(jnp.square(x - m), axis=-1, keepdims=True)
            return (x - m) * jax.lax.rsqrt(v + EPS) * g + b

        def _dwconv_causal(u, w, b):
            lhs = u.transpose(0, 2, 1)
            rhs = w[:, None, :]
            out = jax.lax.conv_general_dilated(lhs, rhs, window_strides=(1,), padding=[(K - 1, 0)], dimension_numbers=('NCH', 'OIH', 'NCH'), feature_group_count=D)
            return out.transpose(0, 2, 1) + b

        def _selective_scan(u, delta, Bm, Cm):
            decay = jnp.exp(-delta)
            inp = u * Bm
            h0 = jnp.zeros((u.shape[0], N), u.dtype)
            xs = (decay.transpose(1, 0, 2), inp.transpose(1, 0, 2), Cm.transpose(1, 0, 2))

            def step(h, x):
                d, i, c = x
                h = h * d + i
                return (h, jnp.sum(h * c, axis=-1))
            _, ys = jax.lax.scan(step, h0, xs)
            return ys.T[..., None]

        def _block(x, g, bt, Wi, bi, cw, cb, wd, bd_, wB, bB_, wC, bC_, wo, bo):
            h = _layernorm(x, g, bt)
            uv = h @ Wi.T + bi
            u, v = (uv[..., :D], uv[..., D:])
            uc = _dwconv_causal(u, cw, cb)
            delta = jax.nn.softplus(uc @ wd.T + bd_)
            Bm = uc @ wB.T + bB_
            Cm = uc @ wC.T + bC_
            y = _selective_scan(uc, delta, Bm, Cm)
            y = y * jax.nn.sigmoid(v)
            return x + (y @ wo.T + bo)
        key = jax.random.key(seed)
        ks = jax.random.split(key, 12)
        rn = lambda k, shp, s=0.02: jax.random.normal(k, shp, jnp.float32) * s
        return dict(tokens=jax.random.randint(ks[0], (B, S), 0, V), embedding=rn(ks[1], (V, D)), pos_enc=rn(ks[2], (256, D)), ln_g=jnp.ones((L, D), jnp.float32), ln_b=jnp.zeros((L, D), jnp.float32), Win=rn(ks[3], (L, 2 * D, D)), b_in=jnp.zeros((L, 2 * D), jnp.float32), convw=rn(ks[4], (L, D, K), 0.1), convb=jnp.zeros((L, D), jnp.float32), Wd=rn(ks[5], (L, N, D)), bd=jnp.zeros((L, N), jnp.float32), WB=rn(ks[6], (L, N, D)), bB=jnp.zeros((L, N), jnp.float32), WC=rn(ks[7], (L, N, D)), bC=jnp.zeros((L, N), jnp.float32), Wout=rn(ks[8], (L, D, D)), bout=jnp.zeros((L, D), jnp.float32))
    _L0_tok_all = _L0_tok_setup()
    _L0_tok_in = {k: v for k, v in _L0_tok_all.items() if k in ('embedding', 'pos_enc', 'ln_g', 'ln_b', 'Win', 'b_in', 'convw', 'convb', 'Wd', 'bd', 'WB', 'bB', 'WC', 'bC', 'Wout', 'bout')}
    del _L0_tok_all

    def _L0_attn_setup():
        import jax, jax.numpy as jnp
        import numpy as np
        B, L, D, M = (1, 512, 192, 64)
        key = jax.random.key(seed)
        ks = jax.random.split(key, 9)

        def w(k, shape):
            return jax.random.normal(k, shape, jnp.float32) * shape[0] ** (-0.5)
        x = jax.random.normal(ks[0], (B, L, D), jnp.float32)
        Wq = w(ks[1], (D, M))
        Wk = w(ks[2], (D, M))
        Wv = w(ks[3], (D, D))
        Wf = w(ks[4], (D, M))
        bf = jnp.zeros((M,), jnp.float32)
        Wo = w(ks[5], (D, D))
        gamma = jnp.ones((D,), jnp.float32)
        beta = jnp.zeros((D,), jnp.float32)
        return {'x': x, 'Wq': Wq, 'Wk': Wk, 'Wv': Wv, 'Wf': Wf, 'bf': bf, 'Wo': Wo, 'gamma': gamma, 'beta': beta}
    _L0_attn_all = _L0_attn_setup()
    _L0_attn_in = {k: v for k, v in _L0_attn_all.items() if k in ('Wq', 'Wk', 'Wv', 'Wf', 'bf', 'Wo', 'gamma', 'beta')}
    del _L0_attn_all

    def _L0_ffn_setup():
        import jax, jax.numpy as jnp
        import numpy as np
        DIM = 192
        GROUP = 64
        E1, S1, E2 = (8, 16, 4)
        MULT = 4
        HID = int(DIM * MULT * 2 / 3)
        B, N = (4, 1024)

        def _l2norm(t, eps=1e-06):
            return t * jax.lax.rsqrt(jnp.sum(t * t, axis=-1, keepdims=True) + eps)

        def _forward(x, gamma_in, slots1, gamma2, w_slot2, w1, b1, w2, b2):
            b, n, d = x.shape
            G, g = (n // GROUP, GROUP)
            scale = d ** 0.5
            xn = _l2norm(x) * scale * gamma_in
            xg = xn.reshape(b, G, g, d)
            phi = _l2norm(slots1) * scale
            logits1 = jnp.einsum('bGgd,esd->bGges', xg, phi)
            disp1 = jax.nn.softmax(logits1, axis=2)
            comb1 = jax.nn.softmax(logits1.reshape(b, G, g, E1 * S1), -1)
            slots = jnp.einsum('bGgd,bGges->bGesd', xg, disp1)
            yn = _l2norm(slots) * scale * gamma2[None, None, :, None, :]
            ns = S1 // E2
            m = S1 // ns
            means = yn.reshape(b, G, E1, m, ns, d).mean(axis=4)
            se2 = jnp.einsum('bGkmd,kdf->bGkmf', means, w_slot2)
            se2 = se2.reshape(b, G, E1, m, E2, d).transpose(0, 1, 2, 4, 3, 5)
            se2 = _l2norm(se2) * scale
            logits2 = jnp.einsum('bGksd,bGkemd->bGksem', yn, se2)
            disp2 = jax.nn.softmax(logits2, axis=3)
            comb2 = jax.nn.softmax(logits2.reshape(b, G, E1, S1, E2 * m), -1)
            slots2 = jnp.einsum('bGksd,bGksem->bGkemd', yn, disp2)
            u = jnp.einsum('bGkemd,kedh->bGkemh', slots2, w1) + b1[None, None, :, :, None, :]
            v, gate = jnp.split(u, 2, axis=-1)
            act = v * jax.nn.gelu(gate)
            o = jnp.einsum('bGkemh,kehd->bGkemd', act, w2) + b2[None, None, :, :, None, :]
            out2 = jnp.einsum('bGkpd,bGksp->bGksd', o.reshape(b, G, E1, E2 * m, d), comb2)
            out = jnp.einsum('bGPd,bGgP->bGgd', out2.reshape(b, G, E1 * S1, d), comb1)
            return out.reshape(b, n, d)
        key = jax.random.key(seed)
        ks = jax.random.split(key, 8)
        p = lambda k, shape, s=0.02: jax.random.normal(k, shape, dtype=jnp.float32) * s
        return {'x': jax.random.normal(ks[0], (B, N, DIM), dtype=jnp.float32), 'gamma_in': jnp.ones((DIM,), jnp.float32), 'slots1': p(ks[1], (E1, S1, DIM), 1.0 / DIM ** 0.5), 'gamma2': jnp.ones((E1, DIM), jnp.float32), 'w_slot2': p(ks[2], (E1, DIM, E2 * DIM)), 'w1': p(ks[3], (E1, E2, DIM, 2 * HID)), 'b1': jnp.zeros((E1, E2, 2 * HID), jnp.float32), 'w2': p(ks[4], (E1, E2, HID, DIM)), 'b2': jnp.zeros((E1, E2, DIM), jnp.float32)}
    _L0_ffn_all = _L0_ffn_setup()
    _L0_ffn_in = {k: v for k, v in _L0_ffn_all.items() if k in ('gamma_in', 'slots1', 'gamma2', 'w_slot2', 'w1', 'b1', 'w2', 'b2')}
    del _L0_ffn_all
    return {'x': x, 'L0_tok_embedding': _L0_tok_in['embedding'], 'L0_tok_pos_enc': _L0_tok_in['pos_enc'], 'L0_tok_ln_g': _L0_tok_in['ln_g'], 'L0_tok_ln_b': _L0_tok_in['ln_b'], 'L0_tok_Win': _L0_tok_in['Win'], 'L0_tok_b_in': _L0_tok_in['b_in'], 'L0_tok_convw': _L0_tok_in['convw'], 'L0_tok_convb': _L0_tok_in['convb'], 'L0_tok_Wd': _L0_tok_in['Wd'], 'L0_tok_bd': _L0_tok_in['bd'], 'L0_tok_WB': _L0_tok_in['WB'], 'L0_tok_bB': _L0_tok_in['bB'], 'L0_tok_WC': _L0_tok_in['WC'], 'L0_tok_bC': _L0_tok_in['bC'], 'L0_tok_Wout': _L0_tok_in['Wout'], 'L0_tok_bout': _L0_tok_in['bout'], 'L0_attn_Wq': _L0_attn_in['Wq'], 'L0_attn_Wk': _L0_attn_in['Wk'], 'L0_attn_Wv': _L0_attn_in['Wv'], 'L0_attn_Wf': _L0_attn_in['Wf'], 'L0_attn_bf': _L0_attn_in['bf'], 'L0_attn_Wo': _L0_attn_in['Wo'], 'L0_attn_gamma': _L0_attn_in['gamma'], 'L0_attn_beta': _L0_attn_in['beta'], 'L0_ffn_gamma_in': _L0_ffn_in['gamma_in'], 'L0_ffn_slots1': _L0_ffn_in['slots1'], 'L0_ffn_gamma2': _L0_ffn_in['gamma2'], 'L0_ffn_w_slot2': _L0_ffn_in['w_slot2'], 'L0_ffn_w1': _L0_ffn_in['w1'], 'L0_ffn_b1': _L0_ffn_in['b1'], 'L0_ffn_w2': _L0_ffn_in['w2'], 'L0_ffn_b2': _L0_ffn_in['b2']}

def reference(x, L0_tok_embedding, L0_tok_pos_enc, L0_tok_ln_g, L0_tok_ln_b, L0_tok_Win, L0_tok_b_in, L0_tok_convw, L0_tok_convb, L0_tok_Wd, L0_tok_bd, L0_tok_WB, L0_tok_bB, L0_tok_WC, L0_tok_bC, L0_tok_Wout, L0_tok_bout, L0_attn_Wq, L0_attn_Wk, L0_attn_Wv, L0_attn_Wf, L0_attn_bf, L0_attn_Wo, L0_attn_gamma, L0_attn_beta, L0_ffn_gamma_in, L0_ffn_slots1, L0_ffn_gamma2, L0_ffn_w_slot2, L0_ffn_w1, L0_ffn_b1, L0_ffn_w2, L0_ffn_b2):
    import jax
    import jax.numpy as jnp

    def _L0_tok_ref(tokens, embedding, pos_enc, ln_g, ln_b, Win, b_in, convw, convb, Wd, bd, WB, bB, WC, bC, Wout, bout):
        import jax, jax.numpy as jnp
        import numpy as np
        B, S, D, L, K, V = (8, 256, 192, 4, 4, 8000)
        N = D
        EPS = 1e-05

        def _layernorm(x, g, b):
            m = jnp.mean(x, axis=-1, keepdims=True)
            v = jnp.mean(jnp.square(x - m), axis=-1, keepdims=True)
            return (x - m) * jax.lax.rsqrt(v + EPS) * g + b

        def _dwconv_causal(u, w, b):
            lhs = u.transpose(0, 2, 1)
            rhs = w[:, None, :]
            out = jax.lax.conv_general_dilated(lhs, rhs, window_strides=(1,), padding=[(K - 1, 0)], dimension_numbers=('NCH', 'OIH', 'NCH'), feature_group_count=D)
            return out.transpose(0, 2, 1) + b

        def _selective_scan(u, delta, Bm, Cm):
            decay = jnp.exp(-delta)
            inp = u * Bm
            h0 = jnp.zeros((u.shape[0], N), u.dtype)
            xs = (decay.transpose(1, 0, 2), inp.transpose(1, 0, 2), Cm.transpose(1, 0, 2))

            def step(h, x):
                d, i, c = x
                h = h * d + i
                return (h, jnp.sum(h * c, axis=-1))
            _, ys = jax.lax.scan(step, h0, xs)
            return ys.T[..., None]

        def _block(x, g, bt, Wi, bi, cw, cb, wd, bd_, wB, bB_, wC, bC_, wo, bo):
            h = _layernorm(x, g, bt)
            uv = h @ Wi.T + bi
            u, v = (uv[..., :D], uv[..., D:])
            uc = _dwconv_causal(u, cw, cb)
            delta = jax.nn.softplus(uc @ wd.T + bd_)
            Bm = uc @ wB.T + bB_
            Cm = uc @ wC.T + bC_
            y = _selective_scan(uc, delta, Bm, Cm)
            y = y * jax.nn.sigmoid(v)
            return x + (y @ wo.T + bo)
        x = embedding[tokens] + pos_enc[:S][None]
        for l in range(L):
            x = _block(x, ln_g[l], ln_b[l], Win[l], b_in[l], convw[l], convb[l], Wd[l], bd[l], WB[l], bB[l], WC[l], bC[l], Wout[l], bout[l])
        return x

    def _L0_attn_ref(x, Wq, Wk, Wv, Wf, bf, Wo, gamma, beta):
        import jax, jax.numpy as jnp
        import numpy as np
        B, L, D, M = (1, 512, 192, 64)
        m_dim = Wq.shape[1]
        scale = m_dim ** (-0.5)
        q = (jax.nn.elu(x @ Wq) + 1.0) * scale
        k = jax.nn.elu(x @ Wk) + 1.0
        v = x @ Wv
        forget = jax.nn.sigmoid(x @ Wf + bf)
        log_f = jnp.log(jnp.clip(forget, 1e-06, None))
        log_f_cum = jnp.clip(jnp.cumsum(log_f, axis=1), -20.0, 20.0)
        exp_neg = jnp.exp(-log_f_cum)
        exp_pos = jnp.exp(log_f_cum)
        kv = k[..., :, None] * v[..., None, :]
        cum_kv = jnp.cumsum(exp_neg[..., None] * kv, axis=1)
        Mstate = exp_pos[..., None] * cum_kv
        z = exp_pos * jnp.cumsum(exp_neg * k, axis=1)
        numerator = jnp.einsum('blm,blmd->bld', q, Mstate)
        denominator = jnp.einsum('blm,blm->bl', q, z)[..., None] + 1e-06
        h = numerator / denominator
        mu = jnp.mean(h, axis=-1, keepdims=True)
        var = jnp.var(h, axis=-1, keepdims=True)
        normed = (h - mu) / jnp.sqrt(var + 1e-05) * gamma + beta
        return normed @ Wo

    def _L0_ffn_ref(x, gamma_in, slots1, gamma2, w_slot2, w1, b1, w2, b2):
        import jax, jax.numpy as jnp
        import numpy as np
        DIM = 192
        GROUP = 64
        E1, S1, E2 = (8, 16, 4)
        MULT = 4
        HID = int(DIM * MULT * 2 / 3)
        B, N = (4, 1024)

        def _l2norm(t, eps=1e-06):
            return t * jax.lax.rsqrt(jnp.sum(t * t, axis=-1, keepdims=True) + eps)

        def _forward(x, gamma_in, slots1, gamma2, w_slot2, w1, b1, w2, b2):
            b, n, d = x.shape
            G, g = (n // GROUP, GROUP)
            scale = d ** 0.5
            xn = _l2norm(x) * scale * gamma_in
            xg = xn.reshape(b, G, g, d)
            phi = _l2norm(slots1) * scale
            logits1 = jnp.einsum('bGgd,esd->bGges', xg, phi)
            disp1 = jax.nn.softmax(logits1, axis=2)
            comb1 = jax.nn.softmax(logits1.reshape(b, G, g, E1 * S1), -1)
            slots = jnp.einsum('bGgd,bGges->bGesd', xg, disp1)
            yn = _l2norm(slots) * scale * gamma2[None, None, :, None, :]
            ns = S1 // E2
            m = S1 // ns
            means = yn.reshape(b, G, E1, m, ns, d).mean(axis=4)
            se2 = jnp.einsum('bGkmd,kdf->bGkmf', means, w_slot2)
            se2 = se2.reshape(b, G, E1, m, E2, d).transpose(0, 1, 2, 4, 3, 5)
            se2 = _l2norm(se2) * scale
            logits2 = jnp.einsum('bGksd,bGkemd->bGksem', yn, se2)
            disp2 = jax.nn.softmax(logits2, axis=3)
            comb2 = jax.nn.softmax(logits2.reshape(b, G, E1, S1, E2 * m), -1)
            slots2 = jnp.einsum('bGksd,bGksem->bGkemd', yn, disp2)
            u = jnp.einsum('bGkemd,kedh->bGkemh', slots2, w1) + b1[None, None, :, :, None, :]
            v, gate = jnp.split(u, 2, axis=-1)
            act = v * jax.nn.gelu(gate)
            o = jnp.einsum('bGkemh,kehd->bGkemd', act, w2) + b2[None, None, :, :, None, :]
            out2 = jnp.einsum('bGkpd,bGksp->bGksd', o.reshape(b, G, E1, E2 * m, d), comb2)
            out = jnp.einsum('bGPd,bGgP->bGgd', out2.reshape(b, G, E1 * S1, d), comb1)
            return out.reshape(b, n, d)
        return _forward(x, gamma_in, slots1, gamma2, w_slot2, w1, b1, w2, b2)
    h = _L0_tok_ref(x, L0_tok_embedding, L0_tok_pos_enc, L0_tok_ln_g, L0_tok_ln_b, L0_tok_Win, L0_tok_b_in, L0_tok_convw, L0_tok_convb, L0_tok_Wd, L0_tok_bd, L0_tok_WB, L0_tok_bB, L0_tok_WC, L0_tok_bC, L0_tok_Wout, L0_tok_bout)
    h = h + _L0_attn_ref(_layernorm(h, axis=-1), L0_attn_Wq, L0_attn_Wk, L0_attn_Wv, L0_attn_Wf, L0_attn_bf, L0_attn_Wo, L0_attn_gamma, L0_attn_beta)
    h = h + _L0_ffn_ref(_layernorm(h, axis=-1), L0_ffn_gamma_in, L0_ffn_slots1, L0_ffn_gamma2, L0_ffn_w_slot2, L0_ffn_w1, L0_ffn_b1, L0_ffn_w2, L0_ffn_b2)
    return h

_drawn_inputs = setup_inputs


def setup_inputs(seed=0):
    import zlib

    import numpy as np

    out = dict(_drawn_inputs(seed))
    spreads = {'L0_tok_ln_g': (1.0, 0.6),
     'L0_tok_ln_b': (0.0, 0.8),
     'L0_tok_b_in': (0.0, 0.451),
     'L0_tok_convb': (0.0, 0.1),
     'L0_tok_bd': (0.0, 0.8),
     'L0_tok_bB': (0.0, 0.1),
     'L0_tok_bC': (0.0, 0.1),
     'L0_tok_bout': (0.0, 0.1),
     'L0_attn_bf': (0.0, 0.8),
     'L0_attn_gamma': (1.0, 0.2),
     'L0_attn_beta': (0.0, 0.1),
     'L0_ffn_gamma_in': (1.0, 0.2),
     'L0_ffn_gamma2': (1.0, 0.6),
     'L0_ffn_b1': (0.0, 0.763),
     'L0_ffn_b2': (0.0, 0.1)}
    factors = {'L0_tok_Wd': 8.0,
     'L0_tok_WB': 3.347,
     'L0_tok_WC': 3.145,
     'L0_attn_Wq': 8.0,
     'L0_attn_Wk': 8.0,
     'L0_attn_Wf': 8.0,
     'L0_ffn_w_slot2': 7.955,
     'L0_ffn_w1': 2.972}
    for name, (base, spread) in spreads.items():
        noise = np.random.default_rng([zlib.crc32(name.encode()), seed]).standard_normal(out[name].shape)
        drawn = base * np.exp(spread * noise) if base else spread * noise
        out[name] = jnp.asarray(drawn.astype(out[name].dtype))
    for name, factor in factors.items():
        out[name] = (out[name] * factor).astype(out[name].dtype)
    return out
```

```python
import concourse.bass as bass
from concourse import mybir
from contextlib import ExitStack

F32 = mybir.dt.float32
F32R = mybir.dt.float32r
I32 = mybir.dt.int32
ALU = mybir.AluOpType
ACT = mybir.ActivationFunctionType
AX = mybir.AxisListType

P = 128
B, S, D, LAYERS, KC, V = 8, 256, 192, 4, 4, 8000
T = B * S
NT = T // P
H2 = 2
DH = D // H2
CH = 512
BPC = CH // S
TPC = CH // P
NC = T // CH
EPS = 1e-5
EXP_20, EXP_M20 = 485165195.4097903, 2.061153622438558e-09
FMIN = 1e-6
MQ = 64
NG, GT = T // 64, 64
E1N, S1N, E2N, MN = 8, 16, 4, 4
NS = E1N * S1N
KE = E1N * E2N
HID = 512
GQ = 4
EL2 = 1e-6
RD = float(D) ** 0.5
BIG = -1e30
STEPS = LAYERS * NC
G_, B_, BU, W0, CB, BV, BD, W1, W2, W3, BBM, BCM = range(12)
NPC = 12


def build(nc, A, out):
    with ExitStack() as ctx:
        at = [0]

        def sb(name, shape, dt=F32):
            size = 4
            for n in shape[1:]:
                size *= n
            t = nc.alloc_sbuf_tensor_at(name, shape, dt, offset=at[0])
            at[0] += (size + 31) // 32 * 32
            return t

        def sem(name):
            return ctx.enter_context(nc.semaphore(name))

        at[0] = (nc.sbuf_base + 31) // 32 * 32
        X = sb("X", [P, NT, D])
        xn = sb("xn", [P, 2, TPC, D])
        st = sb("st", [P, TPC, 6])
        mv = sb("mv", [P, TPC, 2])
        rs = sb("rs", [P, 2, TPC])
        ve = sb("ve", [P, TPC])
        mhalf = sb("mhalf", [P, TPC])
        nb = sb("nb", [P, 2, TPC])
        ident = sb("ident", [P, P])
        ones = sb("ones", [P, 2])
        hf = sb("hf", [DH, H2, CH])
        hhi = sb("hhi", [DH, 2, H2, CH], F32R)
        hlo = sb("hlo", [DH, 2, H2, CH], F32R)
        slots1 = sb("slots1", [P, D])
        g2 = sb("g2", [P, D])
        gin = sb("gin", [P, D])
        phihi = sb("phihi", [DH, H2, NS], F32R)
        philo = sb("philo", [DH, H2, NS], F32R)
        iavg = sb("iavg", [P, P + NS // MN])
        rz1 = sb("rz1", [P, NT])
        overlay = at[0]
        tok = sb("tok", [P, NT], I32)
        tokn = sb("tokn", [P, NT], I32)
        pos = sb("pos", [P, S // P, D])
        pc = sb("pc", [DH, LAYERS + 1, H2, NPC])
        pw_ln = sb("pw_ln", [DH, H2, 2])
        pw_u = sb("pw_u", [DH, H2, 3])
        pw_v = sb("pw_v", [DH, H2, 2])
        pw_c = sb("pw_c", [DH, H2, 3])
        pw_b = sb("pw_b", [DH, H2, 2])
        bout = sb("bout", [P, D])
        wst = {k: sb("wst_" + k, [DH, H2, n]) for k, n in (("u", D), ("v", D), ("z", 3 * D), ("o", D))}
        whi = {k: sb("whi_" + k, [DH, H2, n], F32R) for k, n in (("u", D), ("v", D), ("z", 3 * D), ("o", D))}
        wlo = {k: sb("wlo_" + k, [DH, H2, n], F32R) for k, n in (("u", D), ("v", D), ("z", 3 * D), ("o", D))}
        u = sb("u", [DH, 2, H2, BPC, KC - 1 + S])
        YN0 = sb("YN0", [P, D])
        uc = sb("uc", [DH, 2, H2, CH])
        uchi = sb("uchi", [DH, 2, H2, CH], F32R)
        uclo = sb("uclo", [DH, 2, H2, CH], F32R)
        sig = sb("sig", [DH, H2, CH])
        sghi = sb("sghi", [DH, 2, H2, CH], F32R)
        sglo = sb("sglo", [DH, 2, H2, CH], F32R)
        dec = sb("dec", [DH, H2, BPC, 1 + S])
        inp = sb("inp", [DH, H2, BPC, 1 + S])
        hs = sb("hs", [DH, H2, BPC, 1 + S])
        hc = sb("hc", [DH, 2, H2, CH])
        y = sb("y", [P, TPC])
        AW = 2 * P + 2 * D
        awst = sb("awst", [DH, H2, AW])
        awhi = sb("awhi", [DH, H2, AW], F32R)
        awlo = sb("awlo", [DH, H2, AW], F32R)
        abf = sb("abf", [P, 1])
        agb = sb("agb", [DH, H2, 2])
        mask = sb("mask", [P, 3, P])
        lim = sb("lim", [P, S])
        one64 = sb("one64", [P, 1])
        eqk = sb("eqk", [P, CH])
        fg = sb("fg", [P, CH])
        cum = sb("cum", [P, CH])
        qk = sb("qk", [P, CH])
        qp = sb("qp", [P, 2, CH])
        kp = sb("kp", [P, 2, CH])
        ast = sb("ast", [P, BPC, 3, P])
        vs = sb("vs", [P, 2, TPC, D + 2])
        den = sb("den", [P, TPC])
        rden = sb("rden", [P, TPC])
        rr = sb("rr", [P, TPC])
        v2 = sb("v2", [P, TPC])
        rs2 = sb("rs2", [P, TPC])
        s2 = sb("s2", [P, TPC])
        nb2 = sb("nb2", [P, TPC])
        st2 = sb("st2", [P, TPC, 6])
        mv2 = sb("mv2", [P, TPC, 2])
        xn2 = sb("xn2", [P, TPC, D])
        h2f = sb("h2f", [DH, H2, CH])
        h2hi = sb("h2hi", [DH, H2, CH], F32R)
        h2lo = sb("h2lo", [DH, H2, CH], F32R)

        at[0] = overlay
        YN = sb("YN", [P, NG, D])
        ynT = sb("ynT", [DH, NG, H2, NS])
        meT = sb("meT", [DH, H2, E1N, NG, MN])
        E1T = sb("E1T", [NS, T])
        sl2T = sb("sl2T", [DH, H2, KE, MN, NG])
        se2T = sb("se2T", [DH, H2, NG, E1N, E2N, MN])
        f_work = at[0]
        xg = sb("xg", [P, 2, TPC, D])
        D1 = sb("D1", [P, CH])
        E1 = sb("E1", [P, TPC, NS])
        DT = sb("DT", [P, TPC, 2, NS])
        sq = sb("sq", [P, D])
        sm1 = sb("sm1", [P, 12, 8])
        ssq = sb("ssq", [P, 8])
        ysc = sb("ysc", [P, 8])
        blk8 = sb("blk8", [P, 8])
        wsl = sb("wsl", [DH, 2, H2, E2N * D])
        at[0] = f_work
        se2n = sb("se2n", [P, 2, E2N, D])
        sq2 = sb("sq2", [P, D])
        sm2 = sb("sm2", [P, 2, 3, E2N])
        at[0] = f_work
        blk = sb("blk", [P, NS])
        L2 = sb("L2", [P, 2, GQ, NS])
        C2 = sb("C2", [P, GQ, NS])
        C2n = sb("C2n", [P, 2, GQ, NS])
        D2T = sb("D2T", [P, GQ, NS])
        D2n = sb("D2n", [P, GQ, NS])
        D2 = sb("D2", [P, 2, GQ, NS])
        sm3 = sb("sm3", [P, 8, GQ])
        at[0] = overlay
        oall = sb("oall", [NS, NG, D])
        NW = 2
        w1b = sb("w1b", [DH, NW, H2, 2 * HID])
        w2b = sb("w2b", [P, NW, HID // P, D])
        b2b = sb("b2b", [P, NW, D])
        b1b = sb("b1b", [P, KE, 2 * HID // P])
        gl = sb("gl", [P, 2, HID // P, P])
        ac2 = sb("ac2", [P, 2, HID // P, P])
        osb = sb("osb", [P, 2, D])

        def ps(name):
            return ctx.enter_context(nc.psum_tensor(name, [P, 512], F32))

        MM = [ps(f"mm{k}") for k in range(4)]
        TP = [ps(f"tp{h}") for h in range(H2)]
        OP = [ps(f"op{h}") for h in range(2)]

        s = {}
        for n in """ld_tok ld_c gat dw_u dw_v dw_z dw_o dw_b st_out init_x bou ident_ok pads pe_u
                 pe_v pe_z pe_b pe_c pe_t pe_o pe_y ac_par_ln ac_par_u ac_par_v ac_u ac_tap ac_sig ac_sghi
                 ac_h ac_hhi ac_uchi ac_dec ac_xn ac_y ac_wu ac_wv ac_wz ac_wo dv_wu dv_wv dv_wz dv_wo
                 dv_par dv_st dv_mv pl_rs dv_nb dv_conv dv_uclo dv_hlo dv_sglo dv_x dv_inp dv_scan dv_hc dv_idx
                 ld_aw ac_aw dv_aw pl_ac pe_f pe_av pe_at pe_num pe_t2 pe_ao ac_f ac_eq ac_vs ac_xn2
                 ac_h2 ac_hhi2 dv_abf dv_qk dv_cum dv_qp dv_kp dv_as dv_v2 dv_s2 dv_nb2 dv_h2lo dv_xa pl_rs2
                 pl_ch ld_f ld_ws0 ld_ws1 ld_w0 ld_w1 ld_b1 dv_ch pl_f pe_ph ac_phi dv_phi f_v f_pow
                 f_nb f_xn f_xg f_tr f_hhi f_hlo f_lt f_l f_mx f_mxt f_e f_d f_etr f_dtr
                 f_e1t f_dt f_sl f_ssq f_v2 f_pow2 f_yn f_yt f_yte f_me f_z g_se g_ssq g_v
                 g_pow g_s g_n g_tr g_ev blk_ok h_l2 h_l2m h_tr h_mxc h_mxd h_c h_d h_cn
                 h_dn h_dtr h_d2 h_sl h_sle h_w h_wt x_g x_gl x_act x_o x_osb x_ld0 x_ld1 y_o
                 y_x""".split():
            s[n] = sem(n)

        block = ctx.enter_context(nc.Block())

        def mmbank(i, k):
            return MM[(10 * i + k) % 4]

        def three(pe, dst, lhi, llo, rhi, rlo):
            n = 0
            for h in range(H2):
                for a, b in ((lhi, rhi), (lhi, rlo), (llo, rhi)):
                    r = pe.matmul(dst, a(h), b(h), start=(n == 0), stop=(n == 5))
                    n += 1
            return r

        def att_done(e):
            e.wait_ge(s["dv_xa"], 2 * NC)
            e.wait_ge(s["pe_ao"], 2 * NC)
            e.wait_ge(s["ac_hhi2"], NC)
            e.wait_ge(s["pl_rs2"], NC)
            e.wait_ge(s["bou"], STEPS)
            e.wait_ge(s["dv_h2lo"], NC)

        @block.sync
        def _(sp):
            sp.dma_start(tok[:], A["tok"]).then_inc(s["ld_tok"], 16)
            sp.dma_start(pos[:], A["pos"]).then_inc(s["ld_f"], 16)
            sp.dma_start(pc[:], A["pc"]).then_inc(s["ld_c"], 16)
            for k in "uvzo":
                sp.dma_start(wst[k][:], A["w" + k][0]).then_inc(s["dw_" + k], 16)
            sp.dma_start(bout[:], A["bout"][0]).then_inc(s["dw_b"], 16)
            sp.dma_start(awst[:], A["aw"]).then_inc(s["ld_aw"], 16)
            sp.dma_start(abf[:], A["abf"]).then_inc(s["ld_f"], 16)
            sp.dma_start(agb[:], A["agb"]).then_inc(s["ld_f"], 16)
            for dst, name in ((slots1, "slots1"), (g2, "g2"), (gin, "gin")):
                sp.dma_start(dst[:], A[name]).then_inc(s["ld_f"], 16)
            for l in range(1, LAYERS):
                for k in "uvzo":
                    sp.wait_ge(s["dv_w" + k], l)
                    sp.dma_start(wst[k][:], A["w" + k][l]).then_inc(s["dw_" + k], 16)
                sp.wait_ge(s["bou"], NC * l)
                sp.dma_start(bout[:], A["bout"][l]).then_inc(s["dw_b"], 16)
            att_done(sp)
            for e in range(E1N):
                if e >= 2:
                    sp.wait_ge(s["g_se"], e - 1)
                sp.dma_start(wsl[:, e % 2], A["wsl"][e]).then_inc(s[f"ld_ws{e % 2}"], 16)
            sp.wait_ge(s["h_sle"], 2 * (NG // GQ))
            sp.wait_ge(s["h_wt"], NG // GQ)
            sp.wait_ge(s["h_sl"], NG // GQ)
            sp.dma_start(b1b[:], A["b1"]).then_inc(s["ld_b1"], 16)
            for k in range(KE):
                n = k % NW
                if k >= NW:
                    sp.wait_ge(s["x_osb"], k - NW + 1)
                sp.dma_start(w1b[:, n], A["w1"][k]).then_inc(s[f"ld_w{n}"], 16)
                sp.dma_start(w2b[:, n], A["w2"][k]).then_inc(s[f"ld_w{n}"], 16)
                sp.dma_start(b2b[:, n], A["b2"][k:k + 1, :].partition_broadcast(P).rearrange("p o d -> p (o d)")).then_inc(s[f"ld_w{n}"], 16)
            for t in range(NT):
                sp.wait_ge(s["y_x"], t + 1)
                sp.dma_start(out[:, t, :], X[:, t, :]).then_inc(s["st_out"], 16)
            sp.wait_ge(s["st_out"], 16 * NT)

        @block.gpsimd
        def _(pl):
            pl.memset(ident[:], 0.0).then_inc(s["ident_ok"], 1)
            pl.wait_ge(s["ident_ok"], 1)
            pl.affine_select(out=ident[:], in_=ident[:], compare_op=ALU.not_equal, fill=1.0, base=0,
                             pattern=[[-1, P]], channel_multiplier=1).then_inc(s["ident_ok"], 1)
            pl.memset(ones[:], 1.0).then_inc(s["pads"], 1)
            pl.memset(mhalf[:], -0.5).then_inc(s["pads"], 1)
            pl.memset(u[:, :, :, :, 0:KC - 1], 0.0).then_inc(s["pads"], 1)
            pl.memset(dec[:, :, :, 0:1], 0.0).then_inc(s["pads"], 1)
            pl.memset(inp[:, :, :, 0:1], 0.0).then_inc(s["pads"], 1)
            pl.memset(mask[:], 1.0).then_inc(s["pl_ch"], 1)
            pl.wait_ge(s["pl_ch"], 1)
            pl.affine_select(out=mask[:, 0:2, :], in_=mask[:, 0:2, :], compare_op=ALU.is_ge, fill=0.0, base=0,
                             pattern=[[0, 2], [1, P]], channel_multiplier=-1).then_inc(s["pl_ac"], 1)
            pl.memset(iavg[:, 0:P], 0.0).then_inc(s["pl_f"], 1)
            pl.wait_ge(s["pl_f"], 1)
            pl.affine_select(out=iavg[:, 0:P], in_=iavg[:, 0:P], compare_op=ALU.not_equal, fill=1.0, base=0,
                             pattern=[[-1, P]], channel_multiplier=1).then_inc(s["pl_f"], 1)
            pl.wait_ge(s["pl_f"], 2)
            avg = iavg[:, P:]
            pl.memset(avg, 1.0 / MN).then_inc(s["pl_f"], 1)
            pl.wait_ge(s["pl_f"], 3)
            pl.affine_select(out=avg, in_=avg, compare_op=ALU.is_ge, fill=0.0, base=0,
                             pattern=[[-MN, NS // MN]], channel_multiplier=1).then_inc(s["pl_f"], 1)
            pl.wait_ge(s["pl_f"], 4)
            pl.affine_select(out=avg, in_=avg, compare_op=ALU.is_ge, fill=0.0, base=MN - 1,
                             pattern=[[MN, NS // MN]], channel_multiplier=-1).then_inc(s["pl_f"], 1)
            pl.wait_ge(s["dv_idx"], 4)
            for t in range(NT):
                pl.indirect_dma_start(out=X[:, t, :], out_offset=None, in_=A["emb"],
                                      in_offset=bass.IndirectOffsetOnAxis(ap=tok[:, t:t + 1], axis=0)
                                      ).then_inc(s["gat"], 16)
            def pool_rs(j):
                pl.wait_ge(s["dv_mv"], TPC * (j + 1))
                if j >= 2:
                    pl.wait_ge(s["ac_xn"], TPC * (j - 1))
                if j >= 1:
                    pl.wait_ge(s["pl_rs"], j)
                pl.tensor_scalar(ve[:], mv[:, :, 1], EPS, None, ALU.add).then_inc(s["pl_ch"], 1)
                pl.wait_ge(s["pl_ch"], j + 2)
                pl.tensor_tensor(rs[:, j % 2, :], ve[:], mhalf[:], ALU.pow).then_inc(s["pl_rs"], 1)

            pl.wait_ge(s["pads"], 5)
            pl.wait_ge(s["dv_phi"], 1)
            pl.tensor_tensor(rz1[:, 1:2], rz1[:, 0:1], mhalf[:, 0:1], ALU.pow).then_inc(s["pl_f"], 1)
            pool_rs(0)
            pool_rs(1)
            for i in range(STEPS):
                c = i % NC
                pl.wait_ge(s["ac_xn"], TPC * (i + 1))
                pl.wait_ge(s["dw_b"], 16 * (i // NC + 1))
                xx = X[:, TPC * c:TPC * (c + 1), :]
                pl.tensor_tensor(xx, xx, bout[:].unsqueeze(1).broadcast_to([P, TPC, D]), ALU.add).then_inc(s["bou"], 1)
                pool_rs(i + 2)
            pool_rs(STEPS + 2)
            pool_rs(STEPS + 3)
            for a in range(NC):
                pl.wait_ge(s["dv_v2"], a + 1)
                if a:
                    pl.wait_ge(s["dv_s2"], a)
                pl.tensor_tensor(rs2[:], v2[:], mhalf[:], ALU.pow).then_inc(s["pl_rs2"], 1)
            att_done(pl)
            pl.memset(blk8[:], -0.5).then_inc(s["f_z"], 1)
            pl.wait_ge(s["f_z"], 1)
            for a in range(NC + 1):
                if a < NC:
                    pl.wait_ge(s["f_v"], a + 1)
                    pl.tensor_tensor(sm1[:, 1, 0:TPC], sm1[:, 0, 0:TPC], blk8[:, 0:TPC], ALU.pow).then_inc(s["f_pow"], 1)
                    for t in range(TPC):
                        cs = slice(2 * t, 2 * t + 2)
                        pl.wait_ge(s["f_v2"], TPC * a + t + 1)
                        pl.tensor_tensor(sm1[:, 9, cs], sm1[:, 8, cs], blk8[:, cs], ALU.pow).then_inc(s["f_pow2"], 1)
            for e in range(E1N):
                pl.wait_ge(s["g_v"], e + 1)
                if e:
                    pl.wait_ge(s["g_pow"], e)
                pl.tensor_tensor(sm2[:, e % 2, 1], sm2[:, e % 2, 0], blk8[:, 0:E2N], ALU.pow).then_inc(s["g_pow"], 1)
            pl.wait_ge(s["g_tr"], 2 * E1N)
            pl.memset(blk[:], 0.0).then_inc(s["blk_ok"], 1)
            bv = blk[:].rearrange("p (e n) -> p e n", e=E1N)
            pl.wait_ge(s["blk_ok"], 1)
            pl.affine_select(out=bv, in_=bv, compare_op=ALU.is_ge, fill=BIG, base=0,
                             pattern=[[-S1N, E1N], [0, S1N]], channel_multiplier=1).then_inc(s["blk_ok"], 1)
            pl.wait_ge(s["blk_ok"], 2)
            pl.affine_select(out=bv, in_=bv, compare_op=ALU.is_ge, fill=BIG, base=S1N - 1,
                             pattern=[[S1N, E1N], [0, S1N]], channel_multiplier=-1).then_inc(s["blk_ok"], 1)

        def par(e, dst, l, a, b, name, copy):
            copy(dst[:], pc[:, l, :, a:b]).then_inc(s[name], 1)

        def act_ln(ac, j):
            c = j % NC
            ac.wait_ge(s["dv_nb"], j + 1)
            if j >= 2:
                ac.wait_ge(s["pe_t"], 2 * (j - 1))
            for t in range(TPC):
                ac.activation(xn[:, j % 2, t, :], X[:, TPC * c + t, :], ACT.Identity,
                              bias=nb[:, j % 2, t:t + 1], scale=rs[:, j % 2, t:t + 1]).then_inc(s["ac_xn"], 1)

        def free_h(e, j):
            if j - 2 < STEPS:
                e.wait_ge(s["pe_v"], 2 * (j - 1))
            else:
                e.wait_ge(s["pe_av"], 2 * (j - 1 - STEPS))

        def act_h(ac, j):
            l = j // NC
            if j % NC == 0:
                ac.copy(pw_ln[:], pc[:, l, :, G_:B_ + 1]).then_inc(s["ac_par_ln"], 1)
            for h in range(H2):
                ac.wait_ge(s["pe_t"], 2 * j + h + 1)
                if h == 0:
                    ac.wait_ge(s["ac_par_ln"], l + 1)
                    if j >= 1:
                        ac.wait_ge(s["dv_hlo"], j)
                ac.activation(hf[:, h, :], TP[h][0:DH, :], ACT.Identity, bias=pw_ln[:, h, 1:2],
                              scale=pw_ln[:, h, 0:1]).then_inc(s["ac_h"], 1)
            ac.wait_ge(s["ac_h"], 2 * (j + 1))
            if j >= 2:
                free_h(ac, j)
            ac.copy(hhi[:, j % 2], hf[:]).then_inc(s["ac_hhi"], 1)

        def act_w(ac, k, l):
            ac.wait_ge(s["dw_" + k], 16 * (l + 1))
            if l:
                last = {"u": ("pe_u", 2 * NC * l), "v": ("pe_v", 2 * NC * l), "z": ("pe_c", 2 * NC * l),
                        "o": ("pe_o", 2 * NC * l)}[k]
                ac.wait_ge(s[last[0]], last[1])
            ac.copy(whi[k][:], wst[k][:]).then_inc(s["ac_w" + k], 1)

        def act_ffn(ac):
            att_done(ac)

            def front(a):
                ac.wait_ge(s["f_nb"], a + 1)
                for t in range(TPC):
                    ac.activation(xn[:, a % 2, t, :], X[:, TPC * a + t, :], ACT.Identity, bias=sm1[:, 2, t:t + 1],
                                  scale=sm1[:, 1, t:t + 1]).then_inc(s["f_xn"], 1)
                for h in range(H2):
                    ac.wait_ge(s["f_tr"], 2 * a + h + 1)
                    if a >= 2 and h == 0:
                        ac.wait_ge(s["f_l"], a - 1)
                    ac.copy(hhi[:, a % 2, h, :], TP[h][0:DH, :]).then_inc(s["f_hhi"], 1)
                ac.wait_ge(s["f_mx"], a + 1)
                if a:
                    ac.wait_ge(s["f_etr"], a)
                for t in range(TPC):
                    ac.activation(E1[:, t, :], MM[1][:, t * NS:(t + 1) * NS], ACT.Exp, bias=sm1[:, 4, t:t + 1],
                                  accum_out=sm1[:, 5, t:t + 1]).then_inc(s["f_e"], 1)
                ac.wait_ge(s["f_mxt"], a + 1)
                if a:
                    ac.wait_ge(s["f_dtr"], a)
                for g in range(8):
                    ac.activation(D1[:, g * GT:(g + 1) * GT], MM[0][:, g * GT:(g + 1) * GT], ACT.Exp,
                                  bias=sm1[:, 7, g:g + 1], accum_out=sm1[:, 10, g:g + 1]).then_inc(s["f_d"], 1)

            def back(a):
                ac.wait_ge(s["f_etr"], a + 1)
                ac.copy(E1T[:, a * CH:(a + 1) * CH], MM[2][:]).then_inc(s["f_e1t"], 1)
                for t in range(TPC):
                    ac.wait_ge(s["f_sl"], TPC * a + t + 1)
                    if t == 0:
                        ac.wait_ge(s["f_z"], a + 2)
                    for g in range(2):
                        n = 2 * t + g
                        if TPC * a + t or g:
                            ac.wait_ge(s["f_ssq"], 8 * a + n)
                        ac.activation(sq[:], OP[t % 2][:, g * D:(g + 1) * D], ACT.Square, scale=sm1[:, 11, n:n + 1],
                                      accum_out=ssq[:, n:n + 1]).then_inc(s["f_ssq"], 1)
                for g in range(8):
                    ac.wait_ge(s["f_yt"], 8 * a + g + 1)
                    ac.copy(ynT[:, 8 * a + g], TP[g % 2][0:DH, 0:2 * (P + 32)].rearrange("p (h n) -> p h n", h=2)[:, :, 0:P]
                            ).then_inc(s["f_yte"], 1)

            for a in range(NC):
                front(a)
                back(a)

            for e in range(E1N + 1):
                if e < E1N:
                    m = 2 * (e % 2)
                    ac.wait_ge(s["g_se"], e + 1)
                    if e >= 2:
                        ac.wait_ge(s["g_v"], e - 1)
                    if e == 0:
                        ac.wait_ge(s["f_me"], NG)
                    for q in range(E2N):
                        if e or q:
                            ac.wait_ge(s["g_ssq"], E2N * e + q)
                        ac.activation(sq2[:], MM[m + q // 2][:, (q % 2) * D:(q % 2 + 1) * D], ACT.Square,
                                      accum_out=sm2[:, e % 2, 2, q:q + 1]).then_inc(s["g_ssq"], 1)
                if e:
                    ac.wait_ge(s["g_tr"], 2 * e - 1)
                    ac.copy(se2T[:, 0, :, e - 1].rearrange("p g q m -> p q g m"),
                            TP[0][0:DH, :].rearrange("p (q g m) -> p q g m", q=E2N, g=NG)).then_inc(s["g_ev"], 1)

            NQ = NG // GQ
            for q in range(NQ + 1):
                if q < NQ:
                    ac.wait_ge(s["h_mxc"], q + 1)
                    if q:
                        ac.wait_ge(s["h_cn"], q)
                    for g in range(GQ):
                        ac.activation(C2[:, g, :], L2[:, q % 2, g, :], ACT.Exp, bias=sm3[:, 1, g:g + 1],
                                      accum_out=sm3[:, 2, g:g + 1]).then_inc(s["h_c"], 1)
                    ac.wait_ge(s["h_mxd"], q + 1)
                    if q:
                        ac.wait_ge(s["h_dn"], q)
                    for g in range(GQ):
                        ac.activation(D2T[:, g, :], MM[1][:, g * NS:(g + 1) * NS], ACT.Exp, bias=sm3[:, 5, g:g + 1],
                                      accum_out=sm3[:, 6, g:g + 1]).then_inc(s["h_d"], 1)
                if q < NQ:
                    ac.wait_ge(s["h_dtr"], q + 1)
                    if q >= 2:
                        ac.wait_ge(s["h_sl"], q - 1)
                    ac.copy(D2[:, q % 2], MM[2][:].rearrange("p (g n) -> p g n", g=GQ)).then_inc(s["h_d2"], 1)
                if q < NQ:
                    ac.wait_ge(s["h_sl"], q + 1)
                    ac.copy(sl2T[:, 0, :, :, GQ * q:GQ * (q + 1)],
                            OP[0][0:DH, :].rearrange("p (g k m) -> p k m g", g=GQ, k=KE)).then_inc(s["h_sle"], 1)
                    ac.wait_ge(s["h_w"], q + 1)
                    ac.copy(E1T[:, q * GQ * GT:(q + 1) * GQ * GT], MM[3][:, 0:GQ * GT]).then_inc(s["h_wt"], 1)

            ac.wait_ge(s["ld_b1"], 16)
            for k in range(KE):
                m = 2 * (k % 2)
                ac.wait_ge(s["x_g"], k + 1)
                if k >= 2:
                    ac.wait_ge(s["x_act"], HID // P * (k - 1))
                for c in range(HID // P):
                    ac.activation(gl[:, k % 2, c, :], MM[m + 1][:, c * P:(c + 1) * P], ACT.Gelu_apprx_tanh,
                                  bias=b1b[:, k, HID // P + c:HID // P + c + 1]).then_inc(s["x_gl"], 1)
                ac.wait_ge(s["x_osb"], k + 1)
                ac.dma_start(oall[MN * k:MN * (k + 1)],
                             osb[:, k % 2, :]).then_inc(s[f"x_ld{k % 2}"], 16)

        def act_att(ac):
            ac.wait_ge(s["dv_abf"], 1)
            ac.wait_ge(s["pl_ac"], 8)
            for a in range(NC + 1):
                if a >= 1:
                    k = a - 1
                    ac.wait_ge(s["dv_nb2"], k + 1)
                    if k:
                        ac.wait_ge(s["pe_t2"], 2 * k)
                    for t in range(TPC):
                        ac.activation(xn2[:, t, :], OP[t // 2][:, (t % 2) * (D + 2):(t % 2) * (D + 2) + D], ACT.Identity,
                                      bias=nb2[:, t:t + 1], scale=s2[:, t:t + 1]).then_inc(s["ac_xn2"], 1)
                    for h in range(H2):
                        ac.wait_ge(s["pe_t2"], 2 * k + h + 1)
                        if k and h == 0:
                            ac.wait_ge(s["dv_h2lo"], k)
                        ac.activation(h2f[:, h, :], TP[h][0:DH, :], ACT.Identity, bias=agb[:, h, 1:2],
                                      scale=agb[:, h, 0:1]).then_inc(s["ac_h2"], 1)
                    ac.wait_ge(s["ac_h2"], 2 * (k + 1))
                    if k:
                        ac.wait_ge(s["pe_ao"], 2 * k)
                    ac.copy(h2hi[:], h2f[:]).then_inc(s["ac_hhi2"], 1)
                if a < NC:
                    m = 2 * (a % 2)
                    ac.wait_ge(s["pe_f"], 2 * a + 1)
                    if a:
                        ac.wait_ge(s["dv_cum"], 4 * a)
                    ac.activation(fg[0:MQ], MM[m + 1][0:MQ, :], ACT.Sigmoid, bias=abf[0:MQ]).then_inc(s["ac_f"], 1)
                    ac.activation(fg[MQ:P], MM[m + 1][MQ:P, :], ACT.Exp, bias=abf[MQ:P], scale=-1.0).then_inc(s["ac_f"], 1)
                    ac.wait_ge(s["pe_f"], 2 * a + 2)
                    if a:
                        ac.wait_ge(s["dv_qk"], a)
                    ac.activation(eqk[:], MM[m][:], ACT.Exp).then_inc(s["ac_eq"], 1)
                    if a >= 2:
                        ac.wait_ge(s["pe_num"], 2 * (a - 1))
                    for t in range(2):
                        ac.wait_ge(s["pe_av"], 2 * a + t + 1)
                        ac.copy(vs[:, a % 2, 2 * t:2 * t + 2, 0:D], OP[t][:, 0:2 * D].rearrange("p (t d) -> p t d", t=2)
                                ).then_inc(s["ac_vs"], 1)
                    if STEPS + 2 + a < STEPS + NC:
                        act_h(ac, STEPS + 2 + a)

        @block.scalar
        def _(ac):
            ac.wait_ge(s["ld_c"], 16)
            for k in "uvzo":
                act_w(ac, k, 0)
            ac.wait_ge(s["ld_aw"], 16)
            ac.copy(awhi[:], awst[:]).then_inc(s["ac_aw"], 1)
            ac.wait_ge(s["pe_ph"], 1)
            for h in range(H2):
                ac.copy(phihi[:, h, :], TP[h][0:DH, 0:NS]).then_inc(s["ac_phi"], 1)
            act_ln(ac, 0)
            act_h(ac, 0)
            act_ln(ac, 1)
            for i in range(STEPS + 2):
                l, c, p = i // NC, i % NC, i % 2
                if i < STEPS:
                    if c == 0:
                        if i >= 1:
                            ac.wait_ge(s["ac_tap"], 2 * i)
                        ac.copy(pw_u[:], pc[:, l, :, BU:CB + 1]).then_inc(s["ac_par_u"], 1)
                    if i >= 2:
                        ac.wait_ge(s["dv_conv"], 6 * (i - 1))
                    else:
                        ac.wait_ge(s["pads"], 5)
                    for h in range(H2):
                        ac.wait_ge(s["pe_u"], 2 * i + h + 1)
                        if h == 0:
                            ac.wait_ge(s["ac_par_u"], l + 1)
                        ac.activation(u[:, p, h, :, KC - 1:], mmbank(i, h)[0:DH, :].rearrange("p (b s) -> p b s", b=BPC),
                                      ACT.Identity, bias=pw_u[:, h, 0:1]).then_inc(s["ac_u"], 1)
                    if i >= 2:
                        ac.wait_ge(s["dv_inp"], 2 * (i - 1))
                        ac.wait_ge(s["dv_uclo"], i - 1)
                    for h in range(H2):
                        ac.wait_ge(s["ac_u"], 2 * i + h + 1)
                        ac.activation(uc[:, p, h, :].rearrange("p (b s) -> p b s", b=BPC), u[:, p, h, :, 0:S],
                                      ACT.Identity, bias=pw_u[:, h, 2:3], scale=pw_u[:, h, 1:2]).then_inc(s["ac_tap"], 1)
                if 1 <= i <= STEPS:
                    k = i - 1
                    if k % NC == 0:
                        ac.copy(pw_v[:], pc[:, k // NC, :, BV:BD + 1]).then_inc(s["ac_par_v"], 1)
                    for h in range(H2):
                        ac.wait_ge(s["pe_v"], 2 * k + h + 1)
                        if h == 0:
                            ac.wait_ge(s["ac_par_v"], k // NC + 1)
                            if k >= 1:
                                ac.wait_ge(s["dv_sglo"], k)
                        ac.activation(sig[:, h, :], mmbank(i, 2 + h)[0:DH, :], ACT.Sigmoid,
                                      bias=pw_v[:, h, 0:1]).then_inc(s["ac_sig"], 1)
                if i <= STEPS:
                    act_h(ac, i + 1)
                if 1 <= i <= STEPS:
                    ac.wait_ge(s["ac_sig"], 2 * (k + 1))
                    if k >= 2:
                        ac.wait_ge(s["pe_o"], 2 * (k - 1))
                    ac.copy(sghi[:, k % 2], sig[:]).then_inc(s["ac_sghi"], 1)
                if i < STEPS:
                    ac.wait_ge(s["dv_conv"], 6 * (i + 1))
                    if i >= 2:
                        ac.wait_ge(s["pe_c"], 2 * (i - 1))
                    ac.copy(uchi[:, p], uc[:, p]).then_inc(s["ac_uchi"], 1)
                if 2 <= i:
                    k = i - 2
                    ac.wait_ge(s["pe_y"], k + 1)
                    if k >= 1:
                        ac.wait_ge(s["dv_x"], TPC * k)
                    ac.copy(y[:], TP[0][:, 0:TPC]).then_inc(s["ac_y"], 1)
                act_ln(ac, i + 2)
                if 1 <= i <= STEPS:
                    k = i - 1
                    for h in range(H2):
                        ac.wait_ge(s["pe_z"], 2 * k + h + 1)
                        if h == 0 and k >= 1:
                            ac.wait_ge(s["dv_scan"], k)
                        ac.activation(dec[:, h, :, 1:], mmbank(i, 4 + h)[0:DH, :].rearrange("p (b s) -> p b s", b=BPC),
                                      ACT.Sigmoid, bias=pw_v[:, h, 1:2], scale=-1.0).then_inc(s["ac_dec"], 1)
                if c == 3 and l + 1 < LAYERS:
                    act_w(ac, "u", l + 1)
                if 0 < l < LAYERS:
                    if c == 0:
                        act_w(ac, "v", l)
                        act_w(ac, "z", l)
                    if c == 1:
                        act_w(ac, "o", l)

            act_att(ac)
            act_ffn(ac)

        def dve_w(dv, k, l):
            dv.wait_ge(s["ac_w" + k], l + 1)
            dv.tensor_tensor(wlo[k][:], wst[k][:], whi[k][:].bitcast(F32), ALU.subtract).then_inc(s["dv_w" + k], 1)

        def dve_ln(dv, j):
            c = j % NC
            for t in range(TPC):
                if j >= NC:
                    dv.wait_ge(s["dv_x"], TPC * (j - NC) + t + 1)
                dv.bn_stats(st[:, t, :], X[:, TPC * c + t, :]).then_inc(s["dv_st"], 1)
            for t in range(TPC):
                dv.wait_ge(s["dv_st"], TPC * j + t + 1)
                if j >= 1:
                    dv.wait_ge(s["pl_rs"], j)
                dv.bn_aggr(mv[:, t, :], st[:, t, :]).then_inc(s["dv_mv"], 1)
            dv.wait_ge(s["dv_mv"], TPC * (j + 1))
            if j >= 2:
                dv.wait_ge(s["ac_xn"], TPC * (j - 1))
            dv.wait_ge(s["pl_rs"], j + 1)
            dv.scalar_tensor_tensor(out=nb[:, j % 2, :], in0=mv[:, :, 0], scalar=-1.0, in1=rs[:, j % 2, :],
                                    op0=ALU.mult, op1=ALU.mult).then_inc(s["dv_nb"], 1)

        def dve_hlo(dv, j):
            dv.wait_ge(s["ac_hhi"], j + 1)
            if j >= 2:
                free_h(dv, j)
            dv.tensor_tensor(hlo[:, j % 2], hf[:], hhi[:, j % 2].bitcast(F32), ALU.subtract).then_inc(s["dv_hlo"], 1)

        count = [0]

        def link(ins):
            ins.then_inc(s["dv_ch"], 1)
            count[0] += 1
            nc.vector.wait_ge(s["dv_ch"], count[0])

        def dve_ffn(dv):
            att_done(dv)
            link(dv.memset(DT[0:GT, :, 1, :], 0.0))
            link(dv.memset(DT[GT:P, :, 0, :], 0.0))
            bc = lambda ap, n: ap.unsqueeze(2).broadcast_to([P, ap.shape[1], n])

            def front(a):
                for t in range(TPC):
                    link(dv.bn_stats(st[:, t, :], X[:, TPC * a + t, :]))
                for t in range(TPC):
                    link(dv.bn_aggr(mv[:, t, :], st[:, t, :]))
                dv.tensor_scalar(sm1[:, 0, 0:TPC], mv[:, :, 1], 1.0 + EL2 / D, EPS * EL2 / D, ALU.mult, ALU.add).then_inc(s["f_v"], 1)
                dv.wait_ge(s["f_pow"], a + 1)
                if a:
                    dv.wait_ge(s["f_xn"], TPC * a)
                dv.scalar_tensor_tensor(out=sm1[:, 2, 0:TPC], in0=mv[:, :, 0], scalar=-1.0, in1=sm1[:, 1, 0:TPC],
                                        op0=ALU.mult, op1=ALU.mult).then_inc(s["f_nb"], 1)
                dv.wait_ge(s["f_xn"], TPC * (a + 1))
                if a >= 2:
                    dv.wait_ge(s["f_sl"], TPC * (a - 1))
                dv.tensor_tensor(xg[:, a % 2], xn[:, a % 2], gin[:].unsqueeze(1).broadcast_to([P, TPC, D]), ALU.mult
                                 ).then_inc(s["f_xg"], 1)
                for h in range(H2):
                    dv.wait_ge(s["f_hhi"], 2 * a + h + 1)
                    if a >= 2 and h == 0:
                        dv.wait_ge(s["f_l"], a - 1)
                    dv.tensor_tensor(hlo[:, a % 2, h, :], TP[h][0:DH, :], hhi[:, a % 2, h, :].bitcast(F32), ALU.subtract
                                     ).then_inc(s["f_hlo"], 1)
                dv.wait_ge(s["f_lt"], a + 1)
                if a:
                    dv.wait_ge(s["f_d"], 8 * a)
                link(dv.tensor_reduce(sm1[:, 6, :], MM[0][:].rearrange("p (g t) -> p g t", g=8), AX.X, ALU.max))
                dv.tensor_scalar(sm1[:, 7, :], sm1[:, 6, :], -1.0, None, ALU.mult).then_inc(s["f_mxt"], 1)
                dv.wait_ge(s["f_l"], a + 1)
                if a:
                    dv.wait_ge(s["f_e"], TPC * a)
                link(dv.tensor_reduce(sm1[:, 3, 0:TPC], MM[1][:].rearrange("p (g t) -> p g t", g=TPC), AX.X, ALU.max))
                dv.tensor_scalar(sm1[:, 4, 0:TPC], sm1[:, 3, 0:TPC], -1.0, None, ALU.mult).then_inc(s["f_mx"], 1)

            def back(a):
                dv.wait_ge(s["f_e"], TPC * (a + 1))
                link(dv.reciprocal(rz1[:, TPC * a:TPC * (a + 1)], sm1[:, 5, 0:TPC]))
                dv.wait_ge(s["f_d"], 8 * (a + 1))
                dv.reciprocal(sm1[:, 11, :], sm1[:, 10, :]).then_inc(s["f_z"], 1)
                dv.wait_ge(s["f_dtr"], a + 1)
                dv.tensor_copy(DT[0:GT, :, 0, :], MM[3][0:GT, :].rearrange("p (t n) -> p t n", t=TPC)).then_inc(s["f_dt"], 1)
                dv.tensor_copy(DT[GT:P, :, 1, :], MM[3][GT:P, :].rearrange("p (t n) -> p t n", t=TPC)).then_inc(s["f_dt"], 1)
                for t in range(TPC):
                    dv.wait_ge(s["f_ssq"], 8 * a + 2 * t + 2)
                    cs = slice(2 * t, 2 * t + 2)
                    if TPC * a + t:
                        dv.wait_ge(s["f_pow2"], TPC * a + t)
                    dv.tensor_scalar(sm1[:, 8, cs], ssq[:, cs], EL2, None, ALU.add).then_inc(s["f_v2"], 1)
                    dv.wait_ge(s["f_pow2"], TPC * a + t + 1)
                    dv.wait_ge(s["f_z"], a + 2)
                    link(dv.scalar_tensor_tensor(out=ysc[:, cs], in0=sm1[:, 9, cs], scalar=RD, in1=sm1[:, 11, cs],
                                                 op0=ALU.mult, op1=ALU.mult))
                    for g in range(2):
                        n = 2 * t + g
                        dv.scalar_tensor_tensor(out=YN[:, 8 * a + n, :], in0=OP[t % 2][:, g * D:(g + 1) * D],
                                                scalar=ysc[:, n:n + 1], in1=g2[:], op0=ALU.mult, op1=ALU.mult).then_inc(s["f_yn"], 1)
                for g in range(8):
                    dv.wait_ge(s["f_yte"], 8 * a + g + 1)
                    dv.tensor_copy(meT[:, :, :, 8 * a + g, :],
                                   TP[g % 2][0:DH, 0:2 * (P + 32)].rearrange("p (h n) -> p h n", h=2)[:, :, P:].rearrange(
                                       "p h (e m) -> p h e m", e=E1N)).then_inc(s["f_me"], 1)

            for a in range(NC):
                front(a)
                back(a)

            for e in range(E1N):
                p, m = e % 2, 2 * (e % 2)
                dv.wait_ge(s["g_ssq"], E2N * (e + 1))
                dv.tensor_scalar(sm2[:, p, 0], sm2[:, p, 2], EL2, None, ALU.add).then_inc(s["g_v"], 1)
                dv.wait_ge(s["g_pow"], e + 1)
                link(dv.tensor_scalar(sm2[:, p, 1], sm2[:, p, 1], RD, None, ALU.mult))
                if e >= 2:
                    dv.wait_ge(s["g_tr"], 2 * (e - 1))
                for q in range(E2N):
                    dv.tensor_scalar(se2n[:, p, q, :], MM[m + q // 2][:, (q % 2) * D:(q % 2 + 1) * D],
                                     sm2[:, p, 1, q:q + 1], None, ALU.mult).then_inc(s["g_n"], 1)
                dv.wait_ge(s["g_tr"], 2 * e + 2)
                dv.tensor_copy(se2T[:, 1, :, e].rearrange("p g q m -> p q g m"),
                               TP[1][0:DH, :].rearrange("p (q g m) -> p q g m", q=E2N, g=NG)).then_inc(s["g_s"], 1)

            dv.wait_ge(s["blk_ok"], 3)
            NQ = NG // GQ
            for q in range(NQ):
                dv.wait_ge(s["h_l2"], q + 1)
                if q >= 2:
                    dv.wait_ge(s["h_c"], GQ * (q - 1))
                    dv.wait_ge(s["h_tr"], q - 1)
                m4 = MM[0][:].rearrange("p (g n) -> p g n", g=GQ)
                dv.tensor_tensor(L2[:, q % 2], m4, blk[:].unsqueeze(1).broadcast_to([P, GQ, NS]), ALU.add).then_inc(s["h_l2m"], 1)
                dv.wait_ge(s["h_l2m"], q + 1)
                if q:
                    dv.wait_ge(s["h_c"], GQ * q)
                link(dv.tensor_reduce(sm3[:, 0, :], L2[:, q % 2], AX.X, ALU.max))
                dv.tensor_scalar(sm3[:, 1, :], sm3[:, 0, :], -1.0, None, ALU.mult).then_inc(s["h_mxc"], 1)
                dv.wait_ge(s["h_tr"], q + 1)
                if q:
                    dv.wait_ge(s["h_d"], GQ * q)
                link(dv.tensor_reduce(sm3[:, 4, :], MM[1][:].rearrange("p (g n) -> p g n", g=GQ), AX.X, ALU.max))
                dv.tensor_scalar(sm3[:, 5, :], sm3[:, 4, :], -1.0, None, ALU.mult).then_inc(s["h_mxd"], 1)
                dv.wait_ge(s["h_c"], GQ * (q + 1))
                link(dv.reciprocal(sm3[:, 3, :], sm3[:, 2, :]))
                if q >= 2:
                    dv.wait_ge(s["h_w"], q - 1)
                dv.tensor_tensor(C2n[:, q % 2], C2[:], bc(sm3[:, 3, :], NS), ALU.mult).then_inc(s["h_cn"], 1)
                dv.wait_ge(s["h_d"], GQ * (q + 1))
                link(dv.reciprocal(sm3[:, 7, :], sm3[:, 6, :]))
                if q:
                    dv.wait_ge(s["h_dtr"], q)
                dv.tensor_tensor(D2n[:], D2T[:], bc(sm3[:, 7, :], NS), ALU.mult).then_inc(s["h_dn"], 1)
                dv.wait_ge(s["h_sl"], q + 1)
                dv.tensor_copy(sl2T[:, 1, :, :, GQ * q:GQ * (q + 1)],
                               OP[1][0:DH, :].rearrange("p (g k m) -> p k m g", g=GQ, k=KE)).then_inc(s["h_sle"], 1)

            dv.wait_ge(s["ld_b1"], 16)
            for k in range(KE):
                m = 2 * (k % 2)
                dv.wait_ge(s["x_g"], k + 1)
                if k >= 2:
                    dv.wait_ge(s["x_o"], k - 1)
                for c in range(HID // P):
                    dv.wait_ge(s["x_gl"], HID // P * k + c + 1)
                    dv.scalar_tensor_tensor(out=ac2[:, k % 2, c, :], in0=MM[m][:, c * P:(c + 1) * P], scalar=b1b[:, k, c:c + 1],
                                            in1=gl[:, k % 2, c, :], op0=ALU.add, op1=ALU.mult).then_inc(s["x_act"], 1)
                dv.wait_ge(s["x_o"], k + 1)
                dv.wait_ge(s[f"ld_w{k % NW}"], 48 * (k // NW + 1))
                if k >= 2:
                    dv.wait_ge(s[f"x_ld{k % 2}"], 16 * (k // 2))
                dv.tensor_tensor(osb[:, k % 2, :], OP[k % 2][:, 0:D], b2b[:, k % NW, :], ALU.add).then_inc(s["x_osb"], 1)

            for t in range(NT):
                dv.wait_ge(s["y_o"], t + 1)
                dv.scalar_tensor_tensor(out=X[:, t, :], in0=OP[t % 2][:, 0:D], scalar=rz1[:, t:t + 1], in1=X[:, t, :],
                                        op0=ALU.mult, op1=ALU.add).then_inc(s["y_x"], 1)

        def dve_att(dv):
            dv.wait_ge(s["pl_ac"], 8)
            for a in range(NC):
                m = 2 * (a % 2)
                dv.wait_ge(s["ac_f"], 2 * (a + 1))
                link(dv.tensor_scalar(fg[:], fg[:], one64[:], FMIN, ALU.add, ALU.max))
                link(dv.tensor_scalar(fg[:], fg[:], 1.0 / FMIN, None, ALU.min))
                dv.wait_ge(s["ac_eq"], a + 1)
                link(dv.tensor_scalar(eqk[:], eqk[:], 1.0, None, ALU.min))
                if a:
                    dv.wait_ge(s["dv_qp"], a)
                    dv.wait_ge(s["dv_kp"], a)
                for b in range(BPC):
                    for r, op in ((0, ALU.max), (MQ, ALU.min)):
                        w = slice(b * S, (b + 1) * S)
                        dv.tensor_tensor_scan(cum[r:r + MQ, w], fg[r:r + MQ, w], lim[r:r + MQ, :], 1.0,
                                              ALU.mult, op).then_inc(s["dv_cum"], 1)
                dv.scalar_tensor_tensor(out=qk[:], in0=MM[m][:], scalar=0.0, in1=eqk[:], op0=ALU.max,
                                        op1=ALU.add).then_inc(s["dv_qk"], 1)
                dv.wait_ge(s["dv_cum"], 4 * (a + 1))
                dv.wait_ge(s["dv_qk"], a + 1)
                if a >= 2:
                    dv.wait_ge(s["pe_at"], 2 * (a - 1))
                dv.scalar_tensor_tensor(out=qp[MQ:P, a % 2, :], in0=qk[0:MQ], scalar=MQ ** -0.5, in1=cum[0:MQ],
                                        op0=ALU.mult, op1=ALU.mult).then_inc(s["dv_qp"], 1)
                dv.tensor_tensor(kp[MQ:P, a % 2, :], qk[MQ:P], cum[MQ:P], ALU.mult).then_inc(s["dv_kp"], 1)
                if STEPS + 2 + a < STEPS + NC:
                    dve_hlo(dv, STEPS + 2 + a)
                if a:
                    dve_att_end(dv, a - 1)
                for b in range(BPC):
                    dv.wait_ge(s["pe_at"], 2 * a + b + 1)
                    if a:
                        dv.wait_ge(s["pe_num"], 2 * a)
                    dv.tensor_tensor(ast[:, b], MM[m + b][:, 0:3 * P].rearrange("p (k l) -> p k l", k=3), mask[:],
                                     ALU.mult).then_inc(s["dv_as"], 1)
                if a:
                    dv.wait_ge(s["dv_nb2"], a)
                for t in range(TPC):
                    o = (t % 2) * (D + 2)
                    dv.wait_ge(s["pe_num"], 2 * a + t // 2 + 1)
                    link(dv.tensor_scalar(den[:, t:t + 1], OP[t // 2][:, o + D:o + D + 1], 1e-6, None, ALU.add))
                    link(dv.bn_stats(st2[:, t, :], OP[t // 2][:, o:o + D]))
                link(dv.reciprocal(rden[:], den[:]))
                for t in range(TPC):
                    link(dv.bn_aggr(mv2[:, t, :], st2[:, t, :]))
                link(dv.tensor_tensor(rr[:], rden[:], rden[:], ALU.mult))
                link(dv.tensor_tensor(rr[:], rr[:], mv2[:, :, 1], ALU.mult))
                if a:
                    dv.wait_ge(s["pl_rs2"], a)
                dv.tensor_scalar(v2[:], rr[:], EPS, None, ALU.add).then_inc(s["dv_v2"], 1)
                dv.wait_ge(s["pl_rs2"], a + 1)
                if a:
                    dv.wait_ge(s["ac_xn2"], TPC * a)
                dv.tensor_tensor(s2[:], rden[:], rs2[:], ALU.mult).then_inc(s["dv_s2"], 1)
                dv.wait_ge(s["dv_s2"], a + 1)
                dv.scalar_tensor_tensor(out=nb2[:], in0=mv2[:, :, 0], scalar=-1.0, in1=s2[:], op0=ALU.mult,
                                        op1=ALU.mult).then_inc(s["dv_nb2"], 1)
                dv.wait_ge(s["ac_hhi2"], a + 1)
                if a:
                    dv.wait_ge(s["pe_ao"], 2 * a)
                dv.tensor_tensor(h2lo[:], h2f[:], h2hi[:].bitcast(F32), ALU.subtract).then_inc(s["dv_h2lo"], 1)
            dve_att_end(dv, NC - 1)

        def dve_att_end(dv, a):
            for t in range(2):
                dv.wait_ge(s["pe_ao"], 2 * a + t + 1)
                xx = X[:, TPC * a + 2 * t:TPC * a + 2 * t + 2, :]
                dv.tensor_tensor(xx, OP[t][:, 0:2 * D].rearrange("p (t d) -> p t d", t=2), xx, ALU.add).then_inc(s["dv_xa"], 1)

        @block.vector
        def _(dv):
            dv.memset(lim[0:64, :], EXP_M20).then_inc(s["pl_ac"], 1)
            dv.memset(lim[64:P, :], EXP_20).then_inc(s["pl_ac"], 1)
            dv.memset(one64[0:64, :], 0.0).then_inc(s["pl_ac"], 1)
            dv.memset(one64[64:P, :], 1.0).then_inc(s["pl_ac"], 1)
            dv.memset(qp[0:64], 0.0).then_inc(s["pl_ac"], 1)
            dv.memset(kp[0:64], 0.0).then_inc(s["pl_ac"], 1)
            dv.memset(vs[:, :, :, D:D + 2], 1.0).then_inc(s["pl_ac"], 1)
            dv.wait_ge(s["ld_tok"], 16)
            dv.tensor_scalar(tokn[:], tok[:], 0.0, float(V), ALU.is_lt, ALU.mult).then_inc(s["dv_idx"], 1)
            dv.wait_ge(s["dv_idx"], 1)
            dv.tensor_tensor(tokn[:], tok[:], tokn[:], ALU.add).then_inc(s["dv_idx"], 1)
            dv.wait_ge(s["dv_idx"], 2)
            dv.tensor_scalar(tok[:], tokn[:], 0.0, float(V - 1), ALU.max, ALU.min).then_inc(s["dv_idx"], 2)
            dv.wait_ge(s["ld_c"], 16)
            for l in range(LAYERS):
                link(dv.tensor_scalar(pc[:, l, :, BD:BD + 1], pc[:, l, :, BD:BD + 1], -1.0, None, ALU.mult))
            for k in "uvzo":
                dve_w(dv, k, 0)
            dv.wait_ge(s["ac_aw"], 1)
            dv.tensor_tensor(awlo[:], awst[:], awhi[:].bitcast(F32), ALU.subtract).then_inc(s["dv_aw"], 1)
            dv.wait_ge(s["ld_f"], 96)
            dv.tensor_scalar(abf[MQ:P], abf[MQ:P], -1.0, None, ALU.mult).then_inc(s["dv_abf"], 1)
            dv.wait_ge(s["ld_f"], 96)
            dv.tensor_tensor_reduce(YN0[:], slots1[:], slots1[:], 1.0, EL2, ALU.mult, ALU.add, rz1[:, 0:1]).then_inc(s["dv_phi"], 1)
            dv.wait_ge(s["pl_f"], 6)
            dv.tensor_scalar(slots1[:], slots1[:], rz1[:, 1:2], RD, ALU.mult, ALU.mult).then_inc(s["dv_phi"], 1)
            for h in range(H2):
                dv.wait_ge(s["ac_phi"], h + 1)
                dv.tensor_tensor(philo[:, h, :], TP[h][0:DH, 0:NS], phihi[:, h, :].bitcast(F32), ALU.subtract).then_inc(s["dv_phi"], 1)
            dv.wait_ge(s["ld_f"], 96)
            for c in range(NC):
                dv.wait_ge(s["gat"], 16 * NT)
                xx = X[:, TPC * c:TPC * (c + 1), :].rearrange("p (b t) d -> p b (t d)", b=BPC)
                dv.tensor_tensor(xx, xx, pos[:].rearrange("p t d -> p (t d)").unsqueeze(1).broadcast_to([P, BPC, S // P * D]),
                                 ALU.add).then_inc(s["init_x"], 1)
            for j in range(2):
                dv.wait_ge(s["init_x"], j + 1)
                dve_ln(dv, j)
            dve_hlo(dv, 0)
            dv.wait_ge(s["init_x"], NC)
            for i in range(STEPS + 2):
                l, c, p = i // NC, i % NC, i % 2
                if i < STEPS:
                    if c == 0:
                        if i:
                            dv.wait_ge(s["dv_conv"], 6 * i)
                        dv.tensor_copy(pw_c[:], pc[:, l, :, W1:W3 + 1]).then_inc(s["dv_par"], 1)
                    for k in range(1, KC):
                        for h in range(H2):
                            if k == 1:
                                dv.wait_ge(s["ac_tap"], 2 * i + h + 1)
                                dv.wait_ge(s["dv_par"], 2 * l + 1)
                            else:
                                dv.wait_ge(s["dv_conv"], 6 * i + 2 * (k - 2) + h + 1)
                            o = uc[:, p, h, :].rearrange("p (b s) -> p b s", b=BPC)
                            dv.scalar_tensor_tensor(out=o, in0=u[:, p, h, :, k:k + S], scalar=pw_c[:, h, k - 1:k],
                                                    in1=o, op0=ALU.mult, op1=ALU.add).then_inc(s["dv_conv"], 1)
                if i <= STEPS:
                    dve_hlo(dv, i + 1)
                if i < STEPS:
                    dv.wait_ge(s["ac_uchi"], i + 1)
                    if i >= 2:
                        dv.wait_ge(s["pe_c"], 2 * (i - 1))
                    dv.tensor_tensor(uclo[:, p], uc[:, p], uchi[:, p].bitcast(F32), ALU.subtract).then_inc(s["dv_uclo"], 1)
                if 1 <= i <= STEPS:
                    k = i - 1
                    dv.wait_ge(s["ac_sghi"], i)
                    if k >= 2:
                        dv.wait_ge(s["pe_o"], 2 * (k - 1))
                    dv.tensor_tensor(sglo[:, k % 2], sig[:], sghi[:, k % 2].bitcast(F32), ALU.subtract).then_inc(s["dv_sglo"], 1)
                if 2 <= i:
                    k = i - 2
                    kc = k % NC
                    dv.wait_ge(s["ac_y"], k + 1)
                    dv.wait_ge(s["bou"], k + 1)
                    for t in range(TPC):
                        dv.wait_ge(s["pe_o"], 2 * k + t // 2 + 1)
                        xx = X[:, TPC * kc + t, :]
                        dv.scalar_tensor_tensor(out=xx, in0=OP[t // 2][:, (t % 2) * D:(t % 2 + 1) * D], scalar=y[:, t:t + 1],
                                                in1=xx, op0=ALU.mult, op1=ALU.add).then_inc(s["dv_x"], 1)
                dve_ln(dv, i + 2)
                if 1 <= i <= STEPS:
                    k = i - 1
                    if k % NC == 0:
                        if k:
                            dv.wait_ge(s["dv_hc"], 2 * k)
                        dv.tensor_copy(pw_b[:], pc[:, k // NC, :, BBM:BCM + 1]).then_inc(s["dv_par"], 1)
                    if k == 0:
                        dv.wait_ge(s["pads"], 5)
                    for h in range(H2):
                        dv.wait_ge(s["pe_b"], 2 * k + h + 1)
                        if h == 0:
                            dv.wait_ge(s["dv_par"], 2 * (k // NC) + 2)
                            if k:
                                dv.wait_ge(s["dv_scan"], k)
                        dv.scalar_tensor_tensor(out=inp[:, h, :, 1:], in0=mmbank(i, 6 + h)[0:DH, :].rearrange("p (b s) -> p b s", b=BPC),
                                                scalar=pw_b[:, h, 0:1], in1=uc[:, k % 2, h, :].rearrange("p (b s) -> p b s", b=BPC),
                                                op0=ALU.add, op1=ALU.mult).then_inc(s["dv_inp"], 1)
                    dv.wait_ge(s["dv_inp"], 2 * (k + 1))
                    dv.wait_ge(s["ac_dec"], 2 * (k + 1))
                    if k:
                        dv.wait_ge(s["dv_hc"], 2 * k)
                    flat = lambda a: a[:].rearrange("p h b s -> p (h b s)")
                    dv.tensor_tensor_scan(flat(hs), flat(dec), flat(inp), 0.0, ALU.mult, ALU.add).then_inc(s["dv_scan"], 1)
                    dv.wait_ge(s["dv_scan"], k + 1)
                    if k >= 2:
                        dv.wait_ge(s["pe_y"], k - 1)
                    for h in range(H2):
                        dv.wait_ge(s["pe_c"], 2 * k + h + 1)
                        dv.scalar_tensor_tensor(out=hc[:, k % 2, h, :].rearrange("p (b s) -> p b s", b=BPC),
                                                in0=mmbank(i, 8 + h)[0:DH, :].rearrange("p (b s) -> p b s", b=BPC),
                                                scalar=pw_b[:, h, 1:2], in1=hs[:, h, :, 1:],
                                                op0=ALU.add, op1=ALU.mult).then_inc(s["dv_hc"], 1)
                if c == 3 and l + 1 < LAYERS:
                    dve_w(dv, "u", l + 1)
                if 0 < l < LAYERS:
                    if c == 0:
                        dve_w(dv, "v", l)
                        dve_w(dv, "z", l)
                    if c == 1:
                        dve_w(dv, "o", l)

            dve_att(dv)
            dve_ffn(dv)

        def pe_tr(pe, j):
            pe.wait_ge(s["ac_xn"], TPC * (j + 1))
            if j >= 1:
                pe.wait_ge(s["ac_h"], 2 * j)
            if j >= 4:
                pe.wait_ge(s["ac_y"], min(j - 3, STEPS))
            if j >= STEPS + 3:
                pe.wait_ge(s["ac_h2"], 2 * (j - STEPS - 2))
            for h in range(H2):
                for t in range(TPC):
                    r = pe.transpose(TP[h][0:DH, t * P:(t + 1) * P], xn[:, j % 2, t, h * DH:(h + 1) * DH], ident[:])
                r.then_inc(s["pe_t"], 1)

        @block.tensor
        def _(pe):
            pe.wait_ge(s["ident_ok"], 2)
            pe.wait_ge(s["pads"], 5)
            pe.wait_ge(s["dv_phi"], 2)
            for h in range(H2):
                r = pe.transpose(TP[h][0:DH, 0:NS], slots1[:, h * DH:(h + 1) * DH], ident[:])
            r.then_inc(s["pe_ph"], 1)
            pe.wait_ge(s["dv_phi"], 4)
            pe_tr(pe, 0)
            for i in range(STEPS + 2):
                l, c, p = i // NC, i % NC, i % 2
                if i < STEPS:
                    pe.wait_ge(s["dv_hlo"], i + 1)
                    pe.wait_ge(s["dv_wu"], l + 1)
                    for m in range(H2):
                        if i >= 2:
                            pe.wait_ge(s["dv_inp"], 2 * (i - 2) + m + 1)
                        three(pe, mmbank(i, m)[0:DH, :],
                              lambda h: whi["u"][:, h, m * DH:(m + 1) * DH], lambda h: wlo["u"][:, h, m * DH:(m + 1) * DH],
                              lambda h: hhi[:, p, h, :], lambda h: hlo[:, p, h, :]).then_inc(s["pe_u"], 1)
                if 1 <= i <= STEPS:
                    k = i - 1
                    pe.wait_ge(s["dv_wv"], k // NC + 1)
                    for m in range(H2):
                        if k >= 1:
                            pe.wait_ge(s["dv_hc"], 2 * (k - 1) + m + 1)
                        three(pe, mmbank(i, 2 + m)[0:DH, :],
                              lambda h: whi["v"][:, h, m * DH:(m + 1) * DH], lambda h: wlo["v"][:, h, m * DH:(m + 1) * DH],
                              lambda h: hhi[:, k % 2, h, :], lambda h: hlo[:, k % 2, h, :]).then_inc(s["pe_v"], 1)
                if i <= STEPS:
                    pe_tr(pe, i + 1)
                if 2 <= i:
                    k = i - 2
                    pe.wait_ge(s["dv_sglo"], k + 1)
                    pe.wait_ge(s["dv_wo"], k // NC + 1)
                    for t in range(TPC):
                        if k >= 1 and t % 2 == 0:
                            pe.wait_ge(s["dv_x"], TPC * (k - 1) + t + 2)
                        r = three(pe, OP[t // 2][:, (t % 2) * D:(t % 2 + 1) * D],
                                  lambda h: sghi[:, k % 2, h, t * P:(t + 1) * P], lambda h: sglo[:, k % 2, h, t * P:(t + 1) * P],
                                  lambda h: whi["o"][:, h, :], lambda h: wlo["o"][:, h, :])
                        if t % 2:
                            r.then_inc(s["pe_o"], 1)
                    pe.wait_ge(s["dv_hc"], 2 * (k + 1))
                    pe.wait_ge(s["ac_h"], 2 * min(i + 2, STEPS + 2))
                    if k >= 1:
                        pe.wait_ge(s["ac_y"], k)
                    for t in range(TPC):
                        for h in range(H2):
                            r = pe.matmul(TP[0][:, t:t + 1], hc[:, k % 2, h, t * P:(t + 1) * P], ones[0:DH, 0:1],
                                          start=(h == 0), stop=(h == 1))
                    r.then_inc(s["pe_y"], 1)
                if 1 <= i <= STEPS:
                    k = i - 1
                    pe.wait_ge(s["dv_uclo"], k + 1)
                    pe.wait_ge(s["dv_wz"], k // NC + 1)
                    for q, name in enumerate(("z", "b", "c")):
                        for m in range(H2):
                            if q == 0 and i < STEPS:
                                pe.wait_ge(s["ac_u"], 2 * i + m + 1)
                            if q == 1:
                                pe.wait_ge(s["ac_sig"], 2 * k + m + 1)
                            if q == 2:
                                pe.wait_ge(s["ac_dec"], 2 * k + m + 1)
                            o = q * D + m * DH
                            three(pe, mmbank(i, 4 + 2 * q + m)[0:DH, :],
                                  lambda h: whi["z"][:, h, o:o + DH], lambda h: wlo["z"][:, h, o:o + DH],
                                  lambda h: uchi[:, k % 2, h, :], lambda h: uclo[:, k % 2, h, :]).then_inc(s["pe_" + name], 1)


            def proj(a):
                j = STEPS + a
                m = 2 * (a % 2)
                hi, lo = (lambda h: hhi[:, j % 2, h, :]), (lambda h: hlo[:, j % 2, h, :])
                w = lambda x, o, n: (lambda h: x[:, h, o:o + n])
                pe.wait_ge(s["dv_hlo"], j + 1)
                if a == 0:
                    pe.wait_ge(s["dv_aw"], 1)
                if a < 2:
                    pe.wait_ge(s["dv_hc"], 2 * STEPS)
                    pe.wait_ge(s["ac_dec"], 2 * STEPS)
                else:
                    pe.wait_ge(s["dv_as"], 2 * (a - 1))
                three(pe, MM[m + 1][:], w(awhi, P, P), w(awlo, P, P), hi, lo).then_inc(s["pe_f"], 1)
                three(pe, MM[m][:], w(awhi, 0, P), w(awlo, 0, P), hi, lo).then_inc(s["pe_f"], 1)
                if a == 0:
                    pe.wait_ge(s["dv_x"], TPC * STEPS)
                else:
                    pe.wait_ge(s["ac_xn2"], TPC * a)
                for t in range(TPC):
                    r = three(pe, OP[t // 2][:, (t % 2) * D:(t % 2 + 1) * D],
                              lambda h: hhi[:, j % 2, h, t * P:(t + 1) * P], lambda h: hlo[:, j % 2, h, t * P:(t + 1) * P],
                              w(awhi, 2 * P, D), w(awlo, 2 * P, D))
                    if t % 2:
                        r.then_inc(s["pe_av"], 1)

            def out_proj(a):
                pe.wait_ge(s["dv_h2lo"], a + 1)
                pe.wait_ge(s["ac_xn2"], TPC * (a + 1))
                if a + 1 < NC:
                    pe.wait_ge(s["ac_vs"], 2 * (a + 2))
                for t in range(TPC):
                    r = three(pe, OP[t // 2][:, (t % 2) * D:(t % 2 + 1) * D],
                              lambda h: h2hi[:, h, t * P:(t + 1) * P], lambda h: h2lo[:, h, t * P:(t + 1) * P],
                              lambda h: awhi[:, h, 2 * P + D:], lambda h: awlo[:, h, 2 * P + D:])
                    if t % 2:
                        r.then_inc(s["pe_ao"], 1)

            proj(0)
            pe_tr(pe, STEPS + 2)
            for a in range(NC):
                m = 2 * (a % 2)
                pe.wait_ge(s["dv_qp"], a + 1)
                pe.wait_ge(s["dv_kp"], a + 1)
                for b in range(BPC):
                    q = lambda l0, l1: qp[:, a % 2, b * S + l0:b * S + l1]
                    k = lambda l0, l1: kp[:, a % 2, b * S + l0:b * S + l1]
                    pe.matmul(MM[m + b][:, 0:P], k(0, P), q(0, P), start=True, stop=True)
                    pe.matmul(MM[m + b][:, 2 * P:3 * P], k(0, P), q(P, S), start=True, stop=True)
                    pe.matmul(MM[m + b][:, P:2 * P], k(P, S), q(P, S), start=True, stop=True).then_inc(s["pe_at"], 1)
                pe.wait_ge(s["ac_vs"], 2 * (a + 1))
                if a:
                    pe.wait_ge(s["dv_xa"], 2 * a)
                for b in range(BPC):
                    pe.wait_ge(s["dv_as"], 2 * a + b + 1)
                    v = lambda t: vs[:, a % 2, 2 * b + t, 0:D + 1]
                    pe.matmul(OP[b][:, 0:D + 1], ast[:, b, 0, :], v(0), start=True, stop=True)
                    pe.matmul(OP[b][:, D + 2:2 * D + 3], ast[:, b, 2, :], v(0), start=True, stop=False)
                    pe.matmul(OP[b][:, D + 2:2 * D + 3], ast[:, b, 1, :], v(1), start=False, stop=True).then_inc(s["pe_num"], 1)
                pe.wait_ge(s["ac_xn2"], TPC * (a + 1))
                pe.wait_ge(s["ac_h"], 2 * min(NC + STEPS, STEPS + 3 + a))
                if a:
                    pe.wait_ge(s["ac_h2"], 2 * a)
                for h in range(H2):
                    for t in range(TPC):
                        r = pe.transpose(TP[h][0:DH, t * P:(t + 1) * P], xn2[:, t, h * DH:(h + 1) * DH], ident[:])
                    r.then_inc(s["pe_t2"], 1)
                if a + 1 < NC:
                    proj(a + 1)
                    if STEPS + 3 + a < STEPS + NC:
                        pe_tr(pe, STEPS + 3 + a)
                out_proj(a)

            att_done(pe)
            pe.wait_ge(s["pl_f"], 5)
            full = lambda x, a: (lambda h: x[:, a % 2, h, :])
            phi_h, phi_l = (lambda h: phihi[:, h, :]), (lambda h: philo[:, h, :])
            for a in range(NC):
                pe.wait_ge(s["f_xg"], a + 1)
                if a:
                    pe.wait_ge(s["f_me"], 8 * a)
                for h in range(H2):
                    for t in range(TPC):
                        r = pe.transpose(TP[h][0:DH, t * P:(t + 1) * P], xg[:, a % 2, t, h * DH:(h + 1) * DH], ident[:])
                    r.then_inc(s["f_tr"], 1)
                pe.wait_ge(s["f_hlo"], 2 * (a + 1))
                three(pe, MM[0][:], phi_h, phi_l, full(hhi, a), full(hlo, a)).then_inc(s["f_lt"], 1)
                for t in range(TPC):
                    r = three(pe, MM[1][:, t * NS:(t + 1) * NS], lambda h: hhi[:, a % 2, h, t * P:(t + 1) * P],
                              lambda h: hlo[:, a % 2, h, t * P:(t + 1) * P], phi_h, phi_l)
                r.then_inc(s["f_l"], 1)
                pe.wait_ge(s["f_e"], TPC * (a + 1))
                for t in range(TPC):
                    r = pe.transpose(MM[2][:, t * P:(t + 1) * P], E1[:, t, :], ident[:])
                r.then_inc(s["f_etr"], 1)
                pe.wait_ge(s["f_d"], 8 * (a + 1))
                for t in range(TPC):
                    r = pe.transpose(MM[3][:, t * P:(t + 1) * P], D1[:, t * P:(t + 1) * P], ident[:])
                r.then_inc(s["f_dtr"], 1)
                pe.wait_ge(s["f_dt"], 2 * (a + 1))
                for t in range(TPC):
                    if a or t >= 2:
                        pe.wait_ge(s["f_yn"], 2 * (TPC * a + t) - 2)
                    for g in range(2):
                        r = pe.matmul(OP[t % 2][:, g * D:(g + 1) * D], DT[:, t, g, :], xg[:, a % 2, t, :], start=True, stop=True)
                    r.then_inc(s["f_sl"], 1)
                for g in range(8):
                    n = 8 * a + g
                    pe.wait_ge(s["f_yn"], n + 1)
                    if g >= 2:
                        pe.wait_ge(s["f_me"], n - 1)
                    for h in range(H2):
                        r = pe.matmul(TP[g % 2][0:DH, h * (P + 32):(h + 1) * (P + 32)], YN[:, n, h * DH:(h + 1) * DH], iavg[:],
                                      start=True, stop=True)
                    r.then_inc(s["f_yt"], 1)

            def queries(e):
                pe.wait_ge(s[f"ld_ws{e % 2}"], 16 * (e // 2 + 1))
                if e == 0:
                    pe.wait_ge(s["f_me"], NG)
                    pe.wait_ge(s["f_e1t"], NC)
                if e >= 2:
                    pe.wait_ge(s["g_n"], E2N * (e - 1))
                for n in range(2):
                    for h in range(H2):
                        r = pe.matmul(MM[2 * (e % 2) + n][:, 0:2 * D], meT[:, h, e].rearrange("p g m -> p (g m)"),
                                      wsl[:, e % 2, h, 2 * n * D:2 * (n + 1) * D], start=(h == 0), stop=(h == 1))
                r.then_inc(s["g_se"], 1)

            queries(0)
            for e in range(E1N):
                if e + 1 < E1N:
                    queries(e + 1)
                pe.wait_ge(s["g_n"], E2N * (e + 1))
                for h in range(H2):
                    if e:
                        pe.wait_ge(s["g_ev"] if h == 0 else s["g_s"], e)
                    for q in range(E2N):
                        r = pe.transpose(TP[h][0:DH, q * P:(q + 1) * P], se2n[:, e % 2, q, h * DH:(h + 1) * DH], ident[:])
                    r.then_inc(s["g_tr"], 1)

            pe.wait_ge(s["g_ev"], E1N)
            pe.wait_ge(s["g_s"], E1N)
            pe.wait_ge(s["f_yte"], NG)
            NQ = NG // GQ
            for q in range(NQ):
                if q:
                    pe.wait_ge(s["h_l2m"], q)
                for g in range(GQ):
                    n = GQ * q + g
                    for h in range(H2):
                        r = pe.matmul(MM[0][:, g * NS:(g + 1) * NS], ynT[:, n, h, :],
                                      se2T[:, h, n].rearrange("p e q m -> p (e q m)"), start=(h == 0), stop=(h == 1))
                r.then_inc(s["h_l2"], 1)
                pe.wait_ge(s["h_l2m"], q + 1)
                if q:
                    pe.wait_ge(s["h_d"], GQ * q)
                for g in range(GQ):
                    r = pe.transpose(MM[1][:, g * NS:(g + 1) * NS], L2[:, q % 2, g, :], ident[:])
                r.then_inc(s["h_tr"], 1)
                pe.wait_ge(s["h_dn"], q + 1)
                if q:
                    pe.wait_ge(s["h_d2"], q)
                for g in range(GQ):
                    r = pe.transpose(MM[2][:, g * NS:(g + 1) * NS], D2n[:, g, :], ident[:])
                r.then_inc(s["h_dtr"], 1)
                pe.wait_ge(s["h_cn"], q + 1)
                if q:
                    pe.wait_ge(s["h_wt"], q)
                for g in range(GQ):
                    n = GQ * q + g
                    r = pe.matmul(MM[3][:, g * GT:(g + 1) * GT], C2n[:, q % 2, g, :], E1T[:, n * GT:(n + 1) * GT],
                                  start=True, stop=True)
                r.then_inc(s["h_w"], 1)
                pe.wait_ge(s["h_d2"], q + 1)
                if q:
                    pe.wait_ge(s["h_sle"], 2 * q)
                for g in range(GQ):
                    for h in range(H2):
                        r = pe.matmul(OP[h][0:DH, g * NS:(g + 1) * NS], YN[:, GQ * q + g, h * DH:(h + 1) * DH], D2[:, q % 2, g, :],
                                      start=True, stop=True)
                r.then_inc(s["h_sl"], 1)

            def up(k):
                if k == 0:
                    pe.wait_ge(s["h_sle"], 2 * NQ)
                    pe.wait_ge(s["h_wt"], NQ)
                pe.wait_ge(s[f"ld_w{k % NW}"], 48 * (k // NW + 1))
                if k >= 2:
                    pe.wait_ge(s["x_act"], HID // P * (k - 1))
                for half in (1, 0):
                    for c in range(HID // P):
                        o = half * HID + c * P
                        for h in range(H2):
                            r = pe.matmul(MM[2 * (k % 2) + half][:, c * P:(c + 1) * P], w1b[:, k % NW, h, o:o + P],
                                          sl2T[:, h, k].rearrange("p m g -> p (m g)"), start=(h == 0), stop=(h == 1))
                r.then_inc(s["x_g"], 1)

            up(0)
            for k in range(KE):
                if k + 1 < KE:
                    up(k + 1)
                pe.wait_ge(s["x_act"], HID // P * (k + 1))
                if k >= 2:
                    pe.wait_ge(s["x_osb"], k - 1)
                for c in range(HID // P):
                    r = pe.matmul(OP[k % 2][:, 0:D], ac2[:, k % 2, c, :], w2b[:, k % NW, c, :], start=(c == 0), stop=(c == 3))
                r.then_inc(s["x_o"], 1)

            pe.wait_ge(s["x_ld0"], 8 * KE)
            pe.wait_ge(s["x_ld1"], 8 * KE)
            pe.wait_ge(s["x_osb"], KE)
            for t in range(NT):
                if t >= 2:
                    pe.wait_ge(s["y_x"], t - 1)
                for g in range(2):
                    r = pe.matmul(OP[t % 2][g * GT:(g + 1) * GT, 0:D], E1T[:, t * P + g * GT:t * P + (g + 1) * GT],
                                  oall[:, 2 * t + g, :], start=True, stop=True)
                r.then_inc(s["y_o"], 1)





def layouts(i):
    import numpy as np
    a = {k: np.asarray(v) for k, v in i.items()}
    g = lambda n: a["L0_tok_" + n]
    L = LAYERS
    halves = lambda w: np.ascontiguousarray(w.reshape(w.shape[0], H2, DH, -1).transpose(0, 2, 1, 3))
    win = g("Win").transpose(0, 2, 1)
    zbc = np.stack([g("Wd"), g("WB"), g("WC")], 1).transpose(0, 3, 1, 2).reshape(L, D, 3 * D)
    one, zero = np.ones((1, D), np.float32), np.zeros((1, D), np.float32)
    cw = g("convw")
    cols = [np.concatenate([g("ln_g"), one]), np.concatenate([g("ln_b"), zero])]
    for v in (g("b_in")[:, :D], cw[..., 0], g("convb"), g("b_in")[:, D:], g("bd"), cw[..., 1], cw[..., 2], cw[..., 3], g("bB"), g("bC")):
        cols.append(np.concatenate([v, zero]))
    pc = np.stack(cols, -1).reshape(L + 1, H2, DH, NPC).transpose(2, 0, 1, 3)
    aw = lambda n: a["L0_attn_" + n]
    attn = np.concatenate([aw("Wq"), aw("Wk"), aw("Wf"), aw("Wf"), aw("Wv"), aw("Wo")], 1)[None]
    ff = lambda n: a["L0_ffn_" + n]
    r = {
        "slots1": ff("slots1").reshape(NS, D),
        "g2": np.repeat(ff("gamma2"), S1N, axis=0),
        "gin": np.broadcast_to(ff("gamma_in"), (P, D)),
        "wsl": halves(ff("w_slot2")),
        "w1": halves(ff("w1").reshape(KE, D, 2 * HID)),
        "w2": ff("w2").reshape(KE, HID // P, P, D).transpose(0, 2, 1, 3),
        "b1": ff("b1").reshape(KE, 2 * HID // P, P).transpose(2, 0, 1),
        "b2": ff("b2").reshape(KE, D),
        "aw": halves(attn)[0],
        "abf": np.concatenate([aw("bf"), aw("bf")])[:, None],
        "agb": np.stack([aw("gamma"), aw("beta")], -1).reshape(H2, DH, 2).transpose(1, 0, 2),
        "tok": a["x"].reshape(NT, P).T,
        "pos": g("pos_enc").reshape(S // P, P, D).transpose(1, 0, 2),
        "emb": g("embedding"),
        "pc": pc,
        "wu": halves(win[:, :, :D]), "wv": halves(win[:, :, D:]), "wz": halves(zbc),
        "wo": halves(g("Wout").transpose(0, 2, 1)),
        "bout": np.broadcast_to(g("bout")[:, None, :], (L, P, D)),
    }
    return {k: np.ascontiguousarray(v) for k, v in r.items()}


def kernel(**inputs):
    import numpy as np
    import concourse.bacc as bacc
    from concourse.bass_utils import run_bass_kernel_spmd

    nc = bacc.Bacc("TRN2", target_bir_lowering=False, num_devices=1)
    arrays = layouts(inputs)
    aps = {n: nc.dram_tensor(n, v.shape, mybir.dt.from_np(v.dtype), kind="ExternalInput").ap() for n, v in arrays.items()}
    out = nc.dram_tensor("out_0", (P, NT, D), F32, kind="ExternalOutput").ap()
    build(nc, aps, out)
    r = run_bass_kernel_spmd(nc, [arrays], core_ids=[0])
    return np.ascontiguousarray(r.results[0]["out_0"].transpose(1, 0, 2)).reshape(B, S, D)
```

```python
import concourse.bass as bass
from concourse import mybir
from contextlib import ExitStack

F32 = mybir.dt.float32
F32R = mybir.dt.float32r
I32 = mybir.dt.int32
ALU = mybir.AluOpType
ACT = mybir.ActivationFunctionType
AX = mybir.AxisListType

P = 128
B, S, D, LAYERS, KC, V = 8, 256, 192, 4, 4, 8000
T = B * S
NT = T // P
H2 = 2
DH = D // H2
CH = 512
BPC = CH // S
TPC = CH // P
NC = T // CH
EPS = 1e-5
EXP_20, EXP_M20 = 485165195.4097903, 2.061153622438558e-09
FMIN = 1e-6
MQ = 64
NG, GT = T // 64, 64
E1N, S1N, E2N, MN = 8, 16, 4, 4
NS = E1N * S1N
KE = E1N * E2N
HID = 512
GQ = 4
EL2 = 1e-6
RD = float(D) ** 0.5
BIG = -1e30
STEPS = LAYERS * NC
G_, B_, BU, W0, CB, BV, BD, W1, W2, W3, BBM, BCM = range(12)
NPC = 12


def blocks(nc, A, keep):
    with ExitStack() as ctx:
        at = [0]

        def sb(name, shape, dt=F32):
            size = 4
            for n in shape[1:]:
                size *= n
            t = nc.alloc_sbuf_tensor_at(name, shape, dt, offset=at[0])
            at[0] += (size + 31) // 32 * 32
            return t

        at[0] = (nc.sbuf_base + 31) // 32 * 32
        X = sb("X", [P, NT, D])
        keep["xn_at"] = at[0]
        xn = sb("xn", [P, 2, TPC, D])
        st = sb("st", [P, TPC, 6])
        mv = sb("mv", [P, TPC, 2])
        rs = sb("rs", [P, 2, TPC])
        ve = sb("ve", [P, TPC])
        mhalf = sb("mhalf", [P, 8])
        nb = sb("nb", [P, 2, TPC])
        ident = sb("ident", [P, P])
        ones = sb("ones", [P, 2])
        keep["hf_at"] = at[0]
        hf = sb("hf", [DH, H2, CH])
        keep["hhi_at"] = at[0]
        hhi = sb("hhi", [DH, 2, H2, CH], F32R)
        keep["hlo_at"] = at[0]
        hlo = sb("hlo", [DH, 2, H2, CH], F32R)
        keep["slots1_at"] = at[0]
        slots1 = sb("slots1", [P, D])
        g2 = sb("g2", [P, D])
        gin = sb("gin", [P, D])
        phihi = sb("phihi", [DH, H2, NS], F32R)
        philo = sb("philo", [DH, H2, NS], F32R)
        iavg = sb("iavg", [P, P + NS // MN])
        rz1 = sb("rz1", [P, NT])
        keep["overlay"] = at[0]
        keep.update(X=X, st=st, ident=ident, g2=g2, gin=gin, iavg=iavg, mhalf=mhalf, rz1=rz1, xn=xn, hf=hf,
                    hhi=hhi, hlo=hlo, phihi=phihi, philo=philo)
        tok = sb("tok", [P, NT], I32)
        tokn = sb("tokn", [P, NT], I32)
        pos = sb("pos", [P, S // P, D])
        pc = sb("pc", [DH, LAYERS + 1, H2, NPC])
        pw_ln = sb("pw_ln", [DH, H2, 2])
        pw_u = sb("pw_u", [DH, H2, 3])
        pw_v = sb("pw_v", [DH, H2, 2])
        pw_c = sb("pw_c", [DH, H2, 3])
        pw_b = sb("pw_b", [DH, H2, 2])
        bout = sb("bout", [P, D])
        wst = {k: sb("wst_" + k, [DH, H2, n]) for k, n in (("u", D), ("v", D), ("z", 3 * D), ("o", D))}
        whi = {k: sb("whi_" + k, [DH, H2, n], F32R) for k, n in (("u", D), ("v", D), ("z", 3 * D), ("o", D))}
        wlo = {k: sb("wlo_" + k, [DH, H2, n], F32R) for k, n in (("u", D), ("v", D), ("z", 3 * D), ("o", D))}
        u = sb("u", [DH, 2, H2, BPC, KC - 1 + S])
        YN0 = sb("YN0", [P, D])
        uc = sb("uc", [DH, 2, H2, CH])
        uchi = sb("uchi", [DH, 2, H2, CH], F32R)
        uclo = sb("uclo", [DH, 2, H2, CH], F32R)
        sig = sb("sig", [DH, H2, CH])
        sghi = sb("sghi", [DH, 2, H2, CH], F32R)
        sglo = sb("sglo", [DH, 2, H2, CH], F32R)
        dec = sb("dec", [DH, H2, BPC, 1 + S])
        inp = sb("inp", [DH, H2, BPC, 1 + S])
        hs = sb("hs", [DH, H2, BPC, 1 + S])
        hc = sb("hc", [DH, 2, H2, CH])
        y = sb("y", [P, TPC])
        AW = 2 * P + 2 * D
        awst = sb("awst", [DH, H2, AW])
        awhi = sb("awhi", [DH, H2, AW], F32R)
        awlo = sb("awlo", [DH, H2, AW], F32R)
        abf = sb("abf", [P, 1])
        agb = sb("agb", [DH, H2, 2])
        mask = sb("mask", [P, 3, P])
        lim = sb("lim", [P, S])
        one64 = sb("one64", [P, 1])
        eqk = sb("eqk", [P, CH])
        fg = sb("fg", [P, CH])
        cum = sb("cum", [P, CH])
        qk = sb("qk", [P, CH])
        qp = sb("qp", [P, 2, CH])
        kp = sb("kp", [P, 2, CH])
        ast = sb("ast", [P, BPC, 3, P])
        vs = sb("vs", [P, 2, TPC, D + 2])
        den = sb("den", [P, TPC])
        rden = sb("rden", [P, TPC])
        rr = sb("rr", [P, TPC])
        v2 = sb("v2", [P, TPC])
        rs2 = sb("rs2", [P, TPC])
        s2 = sb("s2", [P, TPC])
        nb2 = sb("nb2", [P, TPC])
        st2 = sb("st2", [P, TPC, 6])
        mv2 = sb("mv2", [P, TPC, 2])
        xn2 = sb("xn2", [P, TPC, D])
        h2f = sb("h2f", [DH, H2, CH])
        h2hi = sb("h2hi", [DH, H2, CH], F32R)
        h2lo = sb("h2lo", [DH, H2, CH], F32R)
        assert at[0] <= 229368

        MM, TP, OP = keep["MM"], keep["TP"], keep["OP"]
        s = {}
        for n in """ld_tok ld_c gat dw_u dw_v dw_z dw_o dw_b init_x bou ident_ok pads pe_u pe_v
                 pe_z pe_b pe_c pe_t pe_o pe_y ac_par_ln ac_par_u ac_par_v ac_u ac_tap ac_sig ac_sghi ac_h
                 ac_hhi ac_uchi ac_dec ac_xn ac_y ac_wu ac_wv ac_wz ac_wo dv_wu dv_wv dv_wz dv_wo dv_par
                 dv_st dv_mv pl_rs dv_nb dv_conv dv_uclo dv_hlo dv_sglo dv_x dv_inp dv_scan dv_hc dv_idx ld_aw
                 ac_aw dv_aw pl_ac pe_f pe_av pe_at pe_num pe_t2 pe_ao ac_f ac_eq ac_vs ac_xn2 ac_h2
                 ac_hhi2 dv_abf dv_qk dv_cum dv_qp dv_kp dv_as dv_v2 dv_s2 dv_nb2 dv_h2lo dv_xa pl_rs2 pl_ch
                 ld_f dv_ch pl_f pe_ph ac_phi dv_phi""".split():
            s[n] = nc.alloc_semaphore(n)

        block = ctx.enter_context(nc.Block())

        def mmbank(i, k):
            return MM[(10 * i + k) % 4]

        def three(pe, dst, lhi, llo, rhi, rlo):
            n = 0
            for h in range(H2):
                for a, b in ((lhi, rhi), (lhi, rlo), (llo, rhi)):
                    r = pe.matmul(dst, a(h), b(h), start=(n == 0), stop=(n == 5))
                    n += 1
            return r

        @block.sync
        def _(sp):
            sp.dma_start(tok[:], A["tok"]).then_inc(s["ld_tok"], 16)
            sp.dma_start(pos[:], A["pos"]).then_inc(s["ld_f"], 16)
            sp.dma_start(pc[:], A["pc"]).then_inc(s["ld_c"], 16)
            for k in "uvzo":
                sp.dma_start(wst[k][:], A["w" + k][0]).then_inc(s["dw_" + k], 16)
            sp.dma_start(bout[:], A["bout"][0]).then_inc(s["dw_b"], 16)
            sp.dma_start(awst[:], A["aw"]).then_inc(s["ld_aw"], 16)
            sp.dma_start(abf[:], A["abf"]).then_inc(s["ld_f"], 16)
            sp.dma_start(agb[:], A["agb"]).then_inc(s["ld_f"], 16)
            for dst, name in ((slots1, "slots1"), (g2, "g2"), (gin, "gin")):
                sp.dma_start(dst[:], A[name]).then_inc(s["ld_f"], 16)
            for l in range(1, LAYERS):
                for k in "uvzo":
                    sp.wait_ge(s["dv_w" + k], l)
                    sp.dma_start(wst[k][:], A["w" + k][l]).then_inc(s["dw_" + k], 16)
                sp.wait_ge(s["bou"], NC * l)
                sp.dma_start(bout[:], A["bout"][l]).then_inc(s["dw_b"], 16)
        @block.gpsimd
        def _(pl):
            pl.memset(ident[:], 0.0).then_inc(s["ident_ok"], 1)
            pl.wait_ge(s["ident_ok"], 1)
            pl.affine_select(out=ident[:], in_=ident[:], compare_op=ALU.not_equal, fill=1.0, base=0,
                             pattern=[[-1, P]], channel_multiplier=1).then_inc(s["ident_ok"], 1)
            pl.memset(ones[:], 1.0).then_inc(s["pads"], 1)
            pl.memset(mhalf[:], -0.5).then_inc(s["pads"], 1)
            pl.memset(u[:, :, :, :, 0:KC - 1], 0.0).then_inc(s["pads"], 1)
            pl.memset(dec[:, :, :, 0:1], 0.0).then_inc(s["pads"], 1)
            pl.memset(inp[:, :, :, 0:1], 0.0).then_inc(s["pads"], 1)
            pl.memset(mask[:], 1.0).then_inc(s["pl_ch"], 1)
            pl.wait_ge(s["pl_ch"], 1)
            pl.affine_select(out=mask[:, 0:2, :], in_=mask[:, 0:2, :], compare_op=ALU.is_ge, fill=0.0, base=0,
                             pattern=[[0, 2], [1, P]], channel_multiplier=-1).then_inc(s["pl_ac"], 1)
            pl.memset(iavg[:, 0:P], 0.0).then_inc(s["pl_f"], 1)
            pl.wait_ge(s["pl_f"], 1)
            pl.affine_select(out=iavg[:, 0:P], in_=iavg[:, 0:P], compare_op=ALU.not_equal, fill=1.0, base=0,
                             pattern=[[-1, P]], channel_multiplier=1).then_inc(s["pl_f"], 1)
            pl.wait_ge(s["pl_f"], 2)
            avg = iavg[:, P:]
            pl.memset(avg, 1.0 / MN).then_inc(s["pl_f"], 1)
            pl.wait_ge(s["pl_f"], 3)
            pl.affine_select(out=avg, in_=avg, compare_op=ALU.is_ge, fill=0.0, base=0,
                             pattern=[[-MN, NS // MN]], channel_multiplier=1).then_inc(s["pl_f"], 1)
            pl.wait_ge(s["pl_f"], 4)
            pl.affine_select(out=avg, in_=avg, compare_op=ALU.is_ge, fill=0.0, base=MN - 1,
                             pattern=[[MN, NS // MN]], channel_multiplier=-1).then_inc(s["pl_f"], 1)
            pl.wait_ge(s["dv_idx"], 4)
            for t in range(NT):
                pl.indirect_dma_start(out=X[:, t, :], out_offset=None, in_=A["emb"],
                                      in_offset=bass.IndirectOffsetOnAxis(ap=tok[:, t:t + 1], axis=0)
                                      ).then_inc(s["gat"], 16)
            def pool_rs(j):
                pl.wait_ge(s["dv_mv"], TPC * (j + 1))
                if j >= 2:
                    pl.wait_ge(s["ac_xn"], TPC * (j - 1))
                if j >= 1:
                    pl.wait_ge(s["pl_rs"], j)
                pl.tensor_scalar(ve[:], mv[:, :, 1], EPS, None, ALU.add).then_inc(s["pl_ch"], 1)
                pl.wait_ge(s["pl_ch"], j + 2)
                pl.tensor_tensor(rs[:, j % 2, :], ve[:], mhalf[:, 0:TPC], ALU.pow).then_inc(s["pl_rs"], 1)

            pl.wait_ge(s["pads"], 5)
            pl.wait_ge(s["dv_phi"], 1)
            pl.tensor_tensor(rz1[:, 1:2], rz1[:, 0:1], mhalf[:, 0:1], ALU.pow).then_inc(s["pl_f"], 1)
            pool_rs(0)
            pool_rs(1)
            for i in range(STEPS):
                c = i % NC
                pl.wait_ge(s["ac_xn"], TPC * (i + 1))
                pl.wait_ge(s["dw_b"], 16 * (i // NC + 1))
                xx = X[:, TPC * c:TPC * (c + 1), :]
                pl.tensor_tensor(xx, xx, bout[:].unsqueeze(1).broadcast_to([P, TPC, D]), ALU.add).then_inc(s["bou"], 1)
                pool_rs(i + 2)
            pool_rs(STEPS + 2)
            pool_rs(STEPS + 3)
            for a in range(NC):
                pl.wait_ge(s["dv_v2"], a + 1)
                if a:
                    pl.wait_ge(s["dv_s2"], a)
                pl.tensor_tensor(rs2[:], v2[:], mhalf[:, 0:TPC], ALU.pow).then_inc(s["pl_rs2"], 1)
        def par(e, dst, l, a, b, name, copy):
            copy(dst[:], pc[:, l, :, a:b]).then_inc(s[name], 1)

        def act_ln(ac, j):
            c = j % NC
            ac.wait_ge(s["dv_nb"], j + 1)
            if j >= 2:
                ac.wait_ge(s["pe_t"], 2 * (j - 1))
            for t in range(TPC):
                ac.activation(xn[:, j % 2, t, :], X[:, TPC * c + t, :], ACT.Identity,
                              bias=nb[:, j % 2, t:t + 1], scale=rs[:, j % 2, t:t + 1]).then_inc(s["ac_xn"], 1)

        def free_h(e, j):
            if j - 2 < STEPS:
                e.wait_ge(s["pe_v"], 2 * (j - 1))
            else:
                e.wait_ge(s["pe_av"], 2 * (j - 1 - STEPS))

        def act_h(ac, j):
            l = j // NC
            if j % NC == 0:
                ac.copy(pw_ln[:], pc[:, l, :, G_:B_ + 1]).then_inc(s["ac_par_ln"], 1)
            for h in range(H2):
                ac.wait_ge(s["pe_t"], 2 * j + h + 1)
                if h == 0:
                    ac.wait_ge(s["ac_par_ln"], l + 1)
                    if j >= 1:
                        ac.wait_ge(s["dv_hlo"], j)
                ac.activation(hf[:, h, :], TP[h][0:DH, :], ACT.Identity, bias=pw_ln[:, h, 1:2],
                              scale=pw_ln[:, h, 0:1]).then_inc(s["ac_h"], 1)
            ac.wait_ge(s["ac_h"], 2 * (j + 1))
            if j >= 2:
                free_h(ac, j)
            ac.copy(hhi[:, j % 2], hf[:]).then_inc(s["ac_hhi"], 1)

        def act_w(ac, k, l):
            ac.wait_ge(s["dw_" + k], 16 * (l + 1))
            if l:
                last = {"u": ("pe_u", 2 * NC * l), "v": ("pe_v", 2 * NC * l), "z": ("pe_c", 2 * NC * l),
                        "o": ("pe_o", 2 * NC * l)}[k]
                ac.wait_ge(s[last[0]], last[1])
            ac.copy(whi[k][:], wst[k][:]).then_inc(s["ac_w" + k], 1)

        def act_att(ac):
            ac.wait_ge(s["dv_abf"], 1)
            ac.wait_ge(s["pl_ac"], 8)
            for a in range(NC + 1):
                if a >= 1:
                    k = a - 1
                    ac.wait_ge(s["dv_nb2"], k + 1)
                    if k:
                        ac.wait_ge(s["pe_t2"], 2 * k)
                    for t in range(TPC):
                        ac.activation(xn2[:, t, :], OP[t // 2][:, (t % 2) * (D + 2):(t % 2) * (D + 2) + D], ACT.Identity,
                                      bias=nb2[:, t:t + 1], scale=s2[:, t:t + 1]).then_inc(s["ac_xn2"], 1)
                    for h in range(H2):
                        ac.wait_ge(s["pe_t2"], 2 * k + h + 1)
                        if k and h == 0:
                            ac.wait_ge(s["dv_h2lo"], k)
                        ac.activation(h2f[:, h, :], TP[h][0:DH, :], ACT.Identity, bias=agb[:, h, 1:2],
                                      scale=agb[:, h, 0:1]).then_inc(s["ac_h2"], 1)
                    ac.wait_ge(s["ac_h2"], 2 * (k + 1))
                    if k:
                        ac.wait_ge(s["pe_ao"], 2 * k)
                    ac.copy(h2hi[:], h2f[:]).then_inc(s["ac_hhi2"], 1)
                if a < NC:
                    m = 2 * (a % 2)
                    ac.wait_ge(s["pe_f"], 2 * a + 1)
                    if a:
                        ac.wait_ge(s["dv_cum"], 4 * a)
                    ac.activation(fg[0:MQ], MM[m + 1][0:MQ, :], ACT.Sigmoid, bias=abf[0:MQ]).then_inc(s["ac_f"], 1)
                    ac.activation(fg[MQ:P], MM[m + 1][MQ:P, :], ACT.Exp, bias=abf[MQ:P], scale=-1.0).then_inc(s["ac_f"], 1)
                    ac.wait_ge(s["pe_f"], 2 * a + 2)
                    if a:
                        ac.wait_ge(s["dv_qk"], a)
                    ac.activation(eqk[:], MM[m][:], ACT.Exp).then_inc(s["ac_eq"], 1)
                    if a >= 2:
                        ac.wait_ge(s["pe_num"], 2 * (a - 1))
                    for t in range(2):
                        ac.wait_ge(s["pe_av"], 2 * a + t + 1)
                        ac.copy(vs[:, a % 2, 2 * t:2 * t + 2, 0:D], OP[t][:, 0:2 * D].rearrange("p (t d) -> p t d", t=2)
                                ).then_inc(s["ac_vs"], 1)
                    if STEPS + 2 + a < STEPS + NC:
                        act_h(ac, STEPS + 2 + a)

        @block.scalar
        def _(ac):
            ac.wait_ge(s["ld_c"], 16)
            for k in "uvzo":
                act_w(ac, k, 0)
            ac.wait_ge(s["ld_aw"], 16)
            ac.copy(awhi[:], awst[:]).then_inc(s["ac_aw"], 1)
            ac.wait_ge(s["pe_ph"], 1)
            for h in range(H2):
                ac.copy(phihi[:, h, :], TP[h][0:DH, 0:NS]).then_inc(s["ac_phi"], 1)
            act_ln(ac, 0)
            act_h(ac, 0)
            act_ln(ac, 1)
            for i in range(STEPS + 2):
                l, c, p = i // NC, i % NC, i % 2
                if i < STEPS:
                    if c == 0:
                        if i >= 1:
                            ac.wait_ge(s["ac_tap"], 2 * i)
                        ac.copy(pw_u[:], pc[:, l, :, BU:CB + 1]).then_inc(s["ac_par_u"], 1)
                    if i >= 2:
                        ac.wait_ge(s["dv_conv"], 6 * (i - 1))
                    else:
                        ac.wait_ge(s["pads"], 5)
                    for h in range(H2):
                        ac.wait_ge(s["pe_u"], 2 * i + h + 1)
                        if h == 0:
                            ac.wait_ge(s["ac_par_u"], l + 1)
                        ac.activation(u[:, p, h, :, KC - 1:], mmbank(i, h)[0:DH, :].rearrange("p (b s) -> p b s", b=BPC),
                                      ACT.Identity, bias=pw_u[:, h, 0:1]).then_inc(s["ac_u"], 1)
                    if i >= 2:
                        ac.wait_ge(s["dv_inp"], 2 * (i - 1))
                        ac.wait_ge(s["dv_uclo"], i - 1)
                    for h in range(H2):
                        ac.wait_ge(s["ac_u"], 2 * i + h + 1)
                        ac.activation(uc[:, p, h, :].rearrange("p (b s) -> p b s", b=BPC), u[:, p, h, :, 0:S],
                                      ACT.Identity, bias=pw_u[:, h, 2:3], scale=pw_u[:, h, 1:2]).then_inc(s["ac_tap"], 1)
                if 1 <= i <= STEPS:
                    k = i - 1
                    if k % NC == 0:
                        ac.copy(pw_v[:], pc[:, k // NC, :, BV:BD + 1]).then_inc(s["ac_par_v"], 1)
                    for h in range(H2):
                        ac.wait_ge(s["pe_v"], 2 * k + h + 1)
                        if h == 0:
                            ac.wait_ge(s["ac_par_v"], k // NC + 1)
                            if k >= 1:
                                ac.wait_ge(s["dv_sglo"], k)
                        ac.activation(sig[:, h, :], mmbank(i, 2 + h)[0:DH, :], ACT.Sigmoid,
                                      bias=pw_v[:, h, 0:1]).then_inc(s["ac_sig"], 1)
                if i <= STEPS:
                    act_h(ac, i + 1)
                if 1 <= i <= STEPS:
                    ac.wait_ge(s["ac_sig"], 2 * (k + 1))
                    if k >= 2:
                        ac.wait_ge(s["pe_o"], 2 * (k - 1))
                    ac.copy(sghi[:, k % 2], sig[:]).then_inc(s["ac_sghi"], 1)
                if i < STEPS:
                    ac.wait_ge(s["dv_conv"], 6 * (i + 1))
                    if i >= 2:
                        ac.wait_ge(s["pe_c"], 2 * (i - 1))
                    ac.copy(uchi[:, p], uc[:, p]).then_inc(s["ac_uchi"], 1)
                if 2 <= i:
                    k = i - 2
                    ac.wait_ge(s["pe_y"], k + 1)
                    if k >= 1:
                        ac.wait_ge(s["dv_x"], TPC * k)
                    ac.copy(y[:], TP[0][:, 0:TPC]).then_inc(s["ac_y"], 1)
                act_ln(ac, i + 2)
                if 1 <= i <= STEPS:
                    k = i - 1
                    for h in range(H2):
                        ac.wait_ge(s["pe_z"], 2 * k + h + 1)
                        if h == 0 and k >= 1:
                            ac.wait_ge(s["dv_scan"], k)
                        ac.activation(dec[:, h, :, 1:], mmbank(i, 4 + h)[0:DH, :].rearrange("p (b s) -> p b s", b=BPC),
                                      ACT.Sigmoid, bias=pw_v[:, h, 1:2], scale=-1.0).then_inc(s["ac_dec"], 1)
                if c == 3 and l + 1 < LAYERS:
                    act_w(ac, "u", l + 1)
                if 0 < l < LAYERS:
                    if c == 0:
                        act_w(ac, "v", l)
                        act_w(ac, "z", l)
                    if c == 1:
                        act_w(ac, "o", l)

            act_att(ac)

        def dve_w(dv, k, l):
            dv.wait_ge(s["ac_w" + k], l + 1)
            dv.tensor_tensor(wlo[k][:], wst[k][:], whi[k][:].bitcast(F32), ALU.subtract).then_inc(s["dv_w" + k], 1)

        def dve_ln(dv, j):
            c = j % NC
            for t in range(TPC):
                if j >= NC:
                    dv.wait_ge(s["dv_x"], TPC * (j - NC) + t + 1)
                dv.bn_stats(st[:, t, :], X[:, TPC * c + t, :]).then_inc(s["dv_st"], 1)
            for t in range(TPC):
                dv.wait_ge(s["dv_st"], TPC * j + t + 1)
                if j >= 1:
                    dv.wait_ge(s["pl_rs"], j)
                dv.bn_aggr(mv[:, t, :], st[:, t, :]).then_inc(s["dv_mv"], 1)
            dv.wait_ge(s["dv_mv"], TPC * (j + 1))
            if j >= 2:
                dv.wait_ge(s["ac_xn"], TPC * (j - 1))
            dv.wait_ge(s["pl_rs"], j + 1)
            dv.scalar_tensor_tensor(out=nb[:, j % 2, :], in0=mv[:, :, 0], scalar=-1.0, in1=rs[:, j % 2, :],
                                    op0=ALU.mult, op1=ALU.mult).then_inc(s["dv_nb"], 1)

        def dve_hlo(dv, j):
            dv.wait_ge(s["ac_hhi"], j + 1)
            if j >= 2:
                free_h(dv, j)
            dv.tensor_tensor(hlo[:, j % 2], hf[:], hhi[:, j % 2].bitcast(F32), ALU.subtract).then_inc(s["dv_hlo"], 1)

        count = [0]

        def link(ins):
            ins.then_inc(s["dv_ch"], 1)
            count[0] += 1
            nc.vector.wait_ge(s["dv_ch"], count[0])

        def dve_att(dv):
            dv.wait_ge(s["pl_ac"], 8)
            for a in range(NC):
                m = 2 * (a % 2)
                dv.wait_ge(s["ac_f"], 2 * (a + 1))
                link(dv.tensor_scalar(fg[:], fg[:], one64[:], FMIN, ALU.add, ALU.max))
                link(dv.tensor_scalar(fg[:], fg[:], 1.0 / FMIN, None, ALU.min))
                dv.wait_ge(s["ac_eq"], a + 1)
                link(dv.tensor_scalar(eqk[:], eqk[:], 1.0, None, ALU.min))
                if a:
                    dv.wait_ge(s["dv_qp"], a)
                    dv.wait_ge(s["dv_kp"], a)
                for b in range(BPC):
                    for r, op in ((0, ALU.max), (MQ, ALU.min)):
                        w = slice(b * S, (b + 1) * S)
                        dv.tensor_tensor_scan(cum[r:r + MQ, w], fg[r:r + MQ, w], lim[r:r + MQ, :], 1.0,
                                              ALU.mult, op).then_inc(s["dv_cum"], 1)
                dv.scalar_tensor_tensor(out=qk[:], in0=MM[m][:], scalar=0.0, in1=eqk[:], op0=ALU.max,
                                        op1=ALU.add).then_inc(s["dv_qk"], 1)
                dv.wait_ge(s["dv_cum"], 4 * (a + 1))
                dv.wait_ge(s["dv_qk"], a + 1)
                if a >= 2:
                    dv.wait_ge(s["pe_at"], 2 * (a - 1))
                dv.scalar_tensor_tensor(out=qp[MQ:P, a % 2, :], in0=qk[0:MQ], scalar=MQ ** -0.5, in1=cum[0:MQ],
                                        op0=ALU.mult, op1=ALU.mult).then_inc(s["dv_qp"], 1)
                dv.tensor_tensor(kp[MQ:P, a % 2, :], qk[MQ:P], cum[MQ:P], ALU.mult).then_inc(s["dv_kp"], 1)
                if STEPS + 2 + a < STEPS + NC:
                    dve_hlo(dv, STEPS + 2 + a)
                if a:
                    dve_att_end(dv, a - 1)
                for b in range(BPC):
                    dv.wait_ge(s["pe_at"], 2 * a + b + 1)
                    if a:
                        dv.wait_ge(s["pe_num"], 2 * a)
                    dv.tensor_tensor(ast[:, b], MM[m + b][:, 0:3 * P].rearrange("p (k l) -> p k l", k=3), mask[:],
                                     ALU.mult).then_inc(s["dv_as"], 1)
                if a:
                    dv.wait_ge(s["dv_nb2"], a)
                for t in range(TPC):
                    o = (t % 2) * (D + 2)
                    dv.wait_ge(s["pe_num"], 2 * a + t // 2 + 1)
                    link(dv.tensor_scalar(den[:, t:t + 1], OP[t // 2][:, o + D:o + D + 1], 1e-6, None, ALU.add))
                    link(dv.bn_stats(st2[:, t, :], OP[t // 2][:, o:o + D]))
                link(dv.reciprocal(rden[:], den[:]))
                for t in range(TPC):
                    link(dv.bn_aggr(mv2[:, t, :], st2[:, t, :]))
                link(dv.tensor_tensor(rr[:], rden[:], rden[:], ALU.mult))
                link(dv.tensor_tensor(rr[:], rr[:], mv2[:, :, 1], ALU.mult))
                if a:
                    dv.wait_ge(s["pl_rs2"], a)
                dv.tensor_scalar(v2[:], rr[:], EPS, None, ALU.add).then_inc(s["dv_v2"], 1)
                dv.wait_ge(s["pl_rs2"], a + 1)
                if a:
                    dv.wait_ge(s["ac_xn2"], TPC * a)
                dv.tensor_tensor(s2[:], rden[:], rs2[:], ALU.mult).then_inc(s["dv_s2"], 1)
                dv.wait_ge(s["dv_s2"], a + 1)
                dv.scalar_tensor_tensor(out=nb2[:], in0=mv2[:, :, 0], scalar=-1.0, in1=s2[:], op0=ALU.mult,
                                        op1=ALU.mult).then_inc(s["dv_nb2"], 1)
                dv.wait_ge(s["ac_hhi2"], a + 1)
                if a:
                    dv.wait_ge(s["pe_ao"], 2 * a)
                dv.tensor_tensor(h2lo[:], h2f[:], h2hi[:].bitcast(F32), ALU.subtract).then_inc(s["dv_h2lo"], 1)
            dve_att_end(dv, NC - 1)

        def dve_att_end(dv, a):
            for t in range(2):
                dv.wait_ge(s["pe_ao"], 2 * a + t + 1)
                xx = X[:, TPC * a + 2 * t:TPC * a + 2 * t + 2, :]
                dv.tensor_tensor(xx, OP[t][:, 0:2 * D].rearrange("p (t d) -> p t d", t=2), xx, ALU.add).then_inc(s["dv_xa"], 1)

        @block.vector
        def _(dv):
            dv.memset(lim[0:64, :], EXP_M20).then_inc(s["pl_ac"], 1)
            dv.memset(lim[64:P, :], EXP_20).then_inc(s["pl_ac"], 1)
            dv.memset(one64[0:64, :], 0.0).then_inc(s["pl_ac"], 1)
            dv.memset(one64[64:P, :], 1.0).then_inc(s["pl_ac"], 1)
            dv.memset(qp[0:64], 0.0).then_inc(s["pl_ac"], 1)
            dv.memset(kp[0:64], 0.0).then_inc(s["pl_ac"], 1)
            dv.memset(vs[:, :, :, D:D + 2], 1.0).then_inc(s["pl_ac"], 1)
            dv.wait_ge(s["ld_tok"], 16)
            dv.tensor_scalar(tokn[:], tok[:], 0.0, float(V), ALU.is_lt, ALU.mult).then_inc(s["dv_idx"], 1)
            dv.wait_ge(s["dv_idx"], 1)
            dv.tensor_tensor(tokn[:], tok[:], tokn[:], ALU.add).then_inc(s["dv_idx"], 1)
            dv.wait_ge(s["dv_idx"], 2)
            dv.tensor_scalar(tok[:], tokn[:], 0.0, float(V - 1), ALU.max, ALU.min).then_inc(s["dv_idx"], 2)
            dv.wait_ge(s["ld_c"], 16)
            for l in range(LAYERS):
                link(dv.tensor_scalar(pc[:, l, :, BD:BD + 1], pc[:, l, :, BD:BD + 1], -1.0, None, ALU.mult))
            for k in "uvzo":
                dve_w(dv, k, 0)
            dv.wait_ge(s["ac_aw"], 1)
            dv.tensor_tensor(awlo[:], awst[:], awhi[:].bitcast(F32), ALU.subtract).then_inc(s["dv_aw"], 1)
            dv.wait_ge(s["ld_f"], 96)
            dv.tensor_scalar(abf[MQ:P], abf[MQ:P], -1.0, None, ALU.mult).then_inc(s["dv_abf"], 1)
            dv.wait_ge(s["ld_f"], 96)
            dv.tensor_tensor_reduce(YN0[:], slots1[:], slots1[:], 1.0, EL2, ALU.mult, ALU.add, rz1[:, 0:1]).then_inc(s["dv_phi"], 1)
            dv.wait_ge(s["pl_f"], 6)
            dv.tensor_scalar(slots1[:], slots1[:], rz1[:, 1:2], RD, ALU.mult, ALU.mult).then_inc(s["dv_phi"], 1)
            for h in range(H2):
                dv.wait_ge(s["ac_phi"], h + 1)
                dv.tensor_tensor(philo[:, h, :], TP[h][0:DH, 0:NS], phihi[:, h, :].bitcast(F32), ALU.subtract).then_inc(s["dv_phi"], 1)
            dv.wait_ge(s["ld_f"], 96)
            for c in range(NC):
                dv.wait_ge(s["gat"], 16 * NT)
                xx = X[:, TPC * c:TPC * (c + 1), :].rearrange("p (b t) d -> p b (t d)", b=BPC)
                dv.tensor_tensor(xx, xx, pos[:].rearrange("p t d -> p (t d)").unsqueeze(1).broadcast_to([P, BPC, S // P * D]),
                                 ALU.add).then_inc(s["init_x"], 1)
            for j in range(2):
                dv.wait_ge(s["init_x"], j + 1)
                dve_ln(dv, j)
            dve_hlo(dv, 0)
            dv.wait_ge(s["init_x"], NC)
            for i in range(STEPS + 2):
                l, c, p = i // NC, i % NC, i % 2
                if i < STEPS:
                    if c == 0:
                        if i:
                            dv.wait_ge(s["dv_conv"], 6 * i)
                        dv.tensor_copy(pw_c[:], pc[:, l, :, W1:W3 + 1]).then_inc(s["dv_par"], 1)
                    for k in range(1, KC):
                        for h in range(H2):
                            if k == 1:
                                dv.wait_ge(s["ac_tap"], 2 * i + h + 1)
                                dv.wait_ge(s["dv_par"], 2 * l + 1)
                            else:
                                dv.wait_ge(s["dv_conv"], 6 * i + 2 * (k - 2) + h + 1)
                            o = uc[:, p, h, :].rearrange("p (b s) -> p b s", b=BPC)
                            dv.scalar_tensor_tensor(out=o, in0=u[:, p, h, :, k:k + S], scalar=pw_c[:, h, k - 1:k],
                                                    in1=o, op0=ALU.mult, op1=ALU.add).then_inc(s["dv_conv"], 1)
                if i <= STEPS:
                    dve_hlo(dv, i + 1)
                if i < STEPS:
                    dv.wait_ge(s["ac_uchi"], i + 1)
                    if i >= 2:
                        dv.wait_ge(s["pe_c"], 2 * (i - 1))
                    dv.tensor_tensor(uclo[:, p], uc[:, p], uchi[:, p].bitcast(F32), ALU.subtract).then_inc(s["dv_uclo"], 1)
                if 1 <= i <= STEPS:
                    k = i - 1
                    dv.wait_ge(s["ac_sghi"], i)
                    if k >= 2:
                        dv.wait_ge(s["pe_o"], 2 * (k - 1))
                    dv.tensor_tensor(sglo[:, k % 2], sig[:], sghi[:, k % 2].bitcast(F32), ALU.subtract).then_inc(s["dv_sglo"], 1)
                if 2 <= i:
                    k = i - 2
                    kc = k % NC
                    dv.wait_ge(s["ac_y"], k + 1)
                    dv.wait_ge(s["bou"], k + 1)
                    for t in range(TPC):
                        dv.wait_ge(s["pe_o"], 2 * k + t // 2 + 1)
                        xx = X[:, TPC * kc + t, :]
                        dv.scalar_tensor_tensor(out=xx, in0=OP[t // 2][:, (t % 2) * D:(t % 2 + 1) * D], scalar=y[:, t:t + 1],
                                                in1=xx, op0=ALU.mult, op1=ALU.add).then_inc(s["dv_x"], 1)
                dve_ln(dv, i + 2)
                if 1 <= i <= STEPS:
                    k = i - 1
                    if k % NC == 0:
                        if k:
                            dv.wait_ge(s["dv_hc"], 2 * k)
                        dv.tensor_copy(pw_b[:], pc[:, k // NC, :, BBM:BCM + 1]).then_inc(s["dv_par"], 1)
                    if k == 0:
                        dv.wait_ge(s["pads"], 5)
                    for h in range(H2):
                        dv.wait_ge(s["pe_b"], 2 * k + h + 1)
                        if h == 0:
                            dv.wait_ge(s["dv_par"], 2 * (k // NC) + 2)
                            if k:
                                dv.wait_ge(s["dv_scan"], k)
                        dv.scalar_tensor_tensor(out=inp[:, h, :, 1:], in0=mmbank(i, 6 + h)[0:DH, :].rearrange("p (b s) -> p b s", b=BPC),
                                                scalar=pw_b[:, h, 0:1], in1=uc[:, k % 2, h, :].rearrange("p (b s) -> p b s", b=BPC),
                                                op0=ALU.add, op1=ALU.mult).then_inc(s["dv_inp"], 1)
                    dv.wait_ge(s["dv_inp"], 2 * (k + 1))
                    dv.wait_ge(s["ac_dec"], 2 * (k + 1))
                    if k:
                        dv.wait_ge(s["dv_hc"], 2 * k)
                    flat = lambda a: a[:].rearrange("p h b s -> p (h b s)")
                    dv.tensor_tensor_scan(flat(hs), flat(dec), flat(inp), 0.0, ALU.mult, ALU.add).then_inc(s["dv_scan"], 1)
                    dv.wait_ge(s["dv_scan"], k + 1)
                    if k >= 2:
                        dv.wait_ge(s["pe_y"], k - 1)
                    for h in range(H2):
                        dv.wait_ge(s["pe_c"], 2 * k + h + 1)
                        dv.scalar_tensor_tensor(out=hc[:, k % 2, h, :].rearrange("p (b s) -> p b s", b=BPC),
                                                in0=mmbank(i, 8 + h)[0:DH, :].rearrange("p (b s) -> p b s", b=BPC),
                                                scalar=pw_b[:, h, 1:2], in1=hs[:, h, :, 1:],
                                                op0=ALU.add, op1=ALU.mult).then_inc(s["dv_hc"], 1)
                if c == 3 and l + 1 < LAYERS:
                    dve_w(dv, "u", l + 1)
                if 0 < l < LAYERS:
                    if c == 0:
                        dve_w(dv, "v", l)
                        dve_w(dv, "z", l)
                    if c == 1:
                        dve_w(dv, "o", l)

            dve_att(dv)

        def pe_tr(pe, j):
            pe.wait_ge(s["ac_xn"], TPC * (j + 1))
            if j >= 1:
                pe.wait_ge(s["ac_h"], 2 * j)
            if j >= 4:
                pe.wait_ge(s["ac_y"], min(j - 3, STEPS))
            if j >= STEPS + 3:
                pe.wait_ge(s["ac_h2"], 2 * (j - STEPS - 2))
            for h in range(H2):
                for t in range(TPC):
                    r = pe.transpose(TP[h][0:DH, t * P:(t + 1) * P], xn[:, j % 2, t, h * DH:(h + 1) * DH], ident[:])
                r.then_inc(s["pe_t"], 1)

        @block.tensor
        def _(pe):
            pe.wait_ge(s["ident_ok"], 2)
            pe.wait_ge(s["pads"], 5)
            pe.wait_ge(s["dv_phi"], 2)
            for h in range(H2):
                r = pe.transpose(TP[h][0:DH, 0:NS], slots1[:, h * DH:(h + 1) * DH], ident[:])
            r.then_inc(s["pe_ph"], 1)
            pe.wait_ge(s["dv_phi"], 4)
            pe_tr(pe, 0)
            for i in range(STEPS + 2):
                l, c, p = i // NC, i % NC, i % 2
                if i < STEPS:
                    pe.wait_ge(s["dv_hlo"], i + 1)
                    pe.wait_ge(s["dv_wu"], l + 1)
                    for m in range(H2):
                        if i >= 2:
                            pe.wait_ge(s["dv_inp"], 2 * (i - 2) + m + 1)
                        three(pe, mmbank(i, m)[0:DH, :],
                              lambda h: whi["u"][:, h, m * DH:(m + 1) * DH], lambda h: wlo["u"][:, h, m * DH:(m + 1) * DH],
                              lambda h: hhi[:, p, h, :], lambda h: hlo[:, p, h, :]).then_inc(s["pe_u"], 1)
                if 1 <= i <= STEPS:
                    k = i - 1
                    pe.wait_ge(s["dv_wv"], k // NC + 1)
                    for m in range(H2):
                        if k >= 1:
                            pe.wait_ge(s["dv_hc"], 2 * (k - 1) + m + 1)
                        three(pe, mmbank(i, 2 + m)[0:DH, :],
                              lambda h: whi["v"][:, h, m * DH:(m + 1) * DH], lambda h: wlo["v"][:, h, m * DH:(m + 1) * DH],
                              lambda h: hhi[:, k % 2, h, :], lambda h: hlo[:, k % 2, h, :]).then_inc(s["pe_v"], 1)
                if i <= STEPS:
                    pe_tr(pe, i + 1)
                if 2 <= i:
                    k = i - 2
                    pe.wait_ge(s["dv_sglo"], k + 1)
                    pe.wait_ge(s["dv_wo"], k // NC + 1)
                    for t in range(TPC):
                        if k >= 1 and t % 2 == 0:
                            pe.wait_ge(s["dv_x"], TPC * (k - 1) + t + 2)
                        r = three(pe, OP[t // 2][:, (t % 2) * D:(t % 2 + 1) * D],
                                  lambda h: sghi[:, k % 2, h, t * P:(t + 1) * P], lambda h: sglo[:, k % 2, h, t * P:(t + 1) * P],
                                  lambda h: whi["o"][:, h, :], lambda h: wlo["o"][:, h, :])
                        if t % 2:
                            r.then_inc(s["pe_o"], 1)
                    pe.wait_ge(s["dv_hc"], 2 * (k + 1))
                    pe.wait_ge(s["ac_h"], 2 * min(i + 2, STEPS + 2))
                    if k >= 1:
                        pe.wait_ge(s["ac_y"], k)
                    for t in range(TPC):
                        for h in range(H2):
                            r = pe.matmul(TP[0][:, t:t + 1], hc[:, k % 2, h, t * P:(t + 1) * P], ones[0:DH, 0:1],
                                          start=(h == 0), stop=(h == 1))
                    r.then_inc(s["pe_y"], 1)
                if 1 <= i <= STEPS:
                    k = i - 1
                    pe.wait_ge(s["dv_uclo"], k + 1)
                    pe.wait_ge(s["dv_wz"], k // NC + 1)
                    for q, name in enumerate(("z", "b", "c")):
                        for m in range(H2):
                            if q == 0 and i < STEPS:
                                pe.wait_ge(s["ac_u"], 2 * i + m + 1)
                            if q == 1:
                                pe.wait_ge(s["ac_sig"], 2 * k + m + 1)
                            if q == 2:
                                pe.wait_ge(s["ac_dec"], 2 * k + m + 1)
                            o = q * D + m * DH
                            three(pe, mmbank(i, 4 + 2 * q + m)[0:DH, :],
                                  lambda h: whi["z"][:, h, o:o + DH], lambda h: wlo["z"][:, h, o:o + DH],
                                  lambda h: uchi[:, k % 2, h, :], lambda h: uclo[:, k % 2, h, :]).then_inc(s["pe_" + name], 1)


            def proj(a):
                j = STEPS + a
                m = 2 * (a % 2)
                hi, lo = (lambda h: hhi[:, j % 2, h, :]), (lambda h: hlo[:, j % 2, h, :])
                w = lambda x, o, n: (lambda h: x[:, h, o:o + n])
                pe.wait_ge(s["dv_hlo"], j + 1)
                if a == 0:
                    pe.wait_ge(s["dv_aw"], 1)
                if a < 2:
                    pe.wait_ge(s["dv_hc"], 2 * STEPS)
                    pe.wait_ge(s["ac_dec"], 2 * STEPS)
                else:
                    pe.wait_ge(s["dv_as"], 2 * (a - 1))
                three(pe, MM[m + 1][:], w(awhi, P, P), w(awlo, P, P), hi, lo).then_inc(s["pe_f"], 1)
                three(pe, MM[m][:], w(awhi, 0, P), w(awlo, 0, P), hi, lo).then_inc(s["pe_f"], 1)
                if a == 0:
                    pe.wait_ge(s["dv_x"], TPC * STEPS)
                else:
                    pe.wait_ge(s["ac_xn2"], TPC * a)
                for t in range(TPC):
                    r = three(pe, OP[t // 2][:, (t % 2) * D:(t % 2 + 1) * D],
                              lambda h: hhi[:, j % 2, h, t * P:(t + 1) * P], lambda h: hlo[:, j % 2, h, t * P:(t + 1) * P],
                              w(awhi, 2 * P, D), w(awlo, 2 * P, D))
                    if t % 2:
                        r.then_inc(s["pe_av"], 1)

            def out_proj(a):
                pe.wait_ge(s["dv_h2lo"], a + 1)
                pe.wait_ge(s["ac_xn2"], TPC * (a + 1))
                if a + 1 < NC:
                    pe.wait_ge(s["ac_vs"], 2 * (a + 2))
                for t in range(TPC):
                    r = three(pe, OP[t // 2][:, (t % 2) * D:(t % 2 + 1) * D],
                              lambda h: h2hi[:, h, t * P:(t + 1) * P], lambda h: h2lo[:, h, t * P:(t + 1) * P],
                              lambda h: awhi[:, h, 2 * P + D:], lambda h: awlo[:, h, 2 * P + D:])
                    if t % 2:
                        r.then_inc(s["pe_ao"], 1)

            proj(0)
            pe_tr(pe, STEPS + 2)
            for a in range(NC):
                m = 2 * (a % 2)
                pe.wait_ge(s["dv_qp"], a + 1)
                pe.wait_ge(s["dv_kp"], a + 1)
                for b in range(BPC):
                    q = lambda l0, l1: qp[:, a % 2, b * S + l0:b * S + l1]
                    k = lambda l0, l1: kp[:, a % 2, b * S + l0:b * S + l1]
                    pe.matmul(MM[m + b][:, 0:P], k(0, P), q(0, P), start=True, stop=True)
                    pe.matmul(MM[m + b][:, 2 * P:3 * P], k(0, P), q(P, S), start=True, stop=True)
                    pe.matmul(MM[m + b][:, P:2 * P], k(P, S), q(P, S), start=True, stop=True).then_inc(s["pe_at"], 1)
                pe.wait_ge(s["ac_vs"], 2 * (a + 1))
                if a:
                    pe.wait_ge(s["dv_xa"], 2 * a)
                for b in range(BPC):
                    pe.wait_ge(s["dv_as"], 2 * a + b + 1)
                    v = lambda t: vs[:, a % 2, 2 * b + t, 0:D + 1]
                    pe.matmul(OP[b][:, 0:D + 1], ast[:, b, 0, :], v(0), start=True, stop=True)
                    pe.matmul(OP[b][:, D + 2:2 * D + 3], ast[:, b, 2, :], v(0), start=True, stop=False)
                    pe.matmul(OP[b][:, D + 2:2 * D + 3], ast[:, b, 1, :], v(1), start=False, stop=True).then_inc(s["pe_num"], 1)
                pe.wait_ge(s["ac_xn2"], TPC * (a + 1))
                pe.wait_ge(s["ac_h"], 2 * min(NC + STEPS, STEPS + 3 + a))
                if a:
                    pe.wait_ge(s["ac_h2"], 2 * a)
                for h in range(H2):
                    for t in range(TPC):
                        r = pe.transpose(TP[h][0:DH, t * P:(t + 1) * P], xn2[:, t, h * DH:(h + 1) * DH], ident[:])
                    r.then_inc(s["pe_t2"], 1)
                if a + 1 < NC:
                    proj(a + 1)
                    if STEPS + 3 + a < STEPS + NC:
                        pe_tr(pe, STEPS + 3 + a)
                out_proj(a)

    return list(s.values())


def mixture(nc, A, out, keep):
    X, st, ident, g2, gin, iavg, mhalf, rz1 = (keep[k] for k in ("X", "st", "ident", "g2", "gin", "iavg", "mhalf", "rz1"))
    xn, hf, hhi, hlo, phihi, philo = (keep[k] for k in ("xn", "hf", "hhi", "hlo", "phihi", "philo"))
    MM, TP, OP = keep["MM"], keep["TP"], keep["OP"]
    with ExitStack() as ctx:
        at = [keep["overlay"]]
        s = {"st_out": keep["st_out"]}
        for n in """ld_ws0 ld_ws1 ld_b1 ld_u0 ld_u1 ld_u2 ld_u3 ld_d0 ld_d1 ld_d2 ld_d3 st_o0 st_o1
                 f_st f_v f_pow f_nb f_xn f_xg f_tr f_hhi f_hlo f_lt f_l f_mx f_mxt f_e f_d f_etr f_dtr f_e1t f_dt f_z
                 f_sl f_ssq f_v2 f_pow2 f_yn f_yt f_yte f_me g_se g_ssq g_v g_pow g_s g_n g_tr g_ev blk_ok
                 h_l2 h_l2m h_tr h_mxc h_mxd h_c h_d h_cn h_dn h_dtr h_d2 h_sl h_sle h_w h_wt
                 x_up x_gl x_act x_down x_o y_o y_x f_ch""".split():
            s[n] = ctx.enter_context(nc.semaphore(n))

        def sb(name, shape, dt=F32):
            size = 4
            for n in shape[1:]:
                size *= n
            t = nc.alloc_sbuf_tensor_at(name, shape, dt, offset=at[0])
            at[0] += (size + 31) // 32 * 32
            return t

        YN = sb("YN", [P, NG, D])
        ynT = sb("ynT", [DH, NG, H2, NS])
        meT_at = at[0]
        meT = sb("meT", [DH, H2, E1N, NG, MN])
        E1T = sb("E1T", [NS, T])
        sl2T = sb("sl2T", [DH, H2, KE, MN, NG])
        se2T_at = at[0]
        se2T = sb("se2T", [DH, H2, NG, E1N, E2N, MN])
        work = at[0]
        xg = sb("xg", [P, 2, TPC, D])
        D1 = sb("D1", [P, CH])
        E1 = sb("E1", [P, TPC, NS])
        DT = sb("DT", [P, TPC, 2, NS])
        sq = sb("sq", [P, D])
        mvx = sb("mvx", [P, NT, 2])
        lnx = sb("lnx", [P, 3, NT])
        sm1 = sb("sm1", [P, 2, 10, 8])
        wsl = sb("wsl", [DH, 2, H2, E2N * D])
        assert at[0] <= 229368
        at[0] = work
        se2n = sb("se2n", [P, 2, E2N, D])
        sq2 = sb("sq2", [P, D])
        sm2 = sb("sm2", [P, 2, 3, E2N])
        at[0] = work
        blk = sb("blk", [P, NS])
        L2 = sb("L2", [P, 2, GQ, NS])
        C2 = sb("C2", [P, GQ, NS])
        C2n = sb("C2n", [P, GQ, NS])
        D2T = sb("D2T", [P, GQ, NS])
        D2n = sb("D2n", [P, GQ, NS])
        D2 = sb("D2", [P, 2, GQ, NS])
        sm3 = sb("sm3", [P, 8, GQ])
        w1_at3 = at[0]
        NW = 4
        w1b, w2b = [], []
        for n, o in enumerate((keep["hhi_at"], keep["hlo_at"], meT_at, w1_at3)):
            at[0] = o
            w1b.append(sb(f"w1b{n}", [DH, H2, 2 * HID]))
        assert at[0] <= 229368
        for n, o in enumerate((keep["xn_at"], keep["xn_at"] + HID // P * D * 4, keep["hf_at"], keep["slots1_at"])):
            at[0] = o
            w2b.append(sb(f"w2b{n}", [P, HID // P, D]))
        at[0] = keep["overlay"]
        oall = sb("oall", [NS, NG, D])
        assert at[0] <= meT_at
        at[0] = se2T_at
        b2b = [sb(f"b2b{n}", [P, D]) for n in range(NW)]
        b1b = sb("b1b", [P, KE, 2 * HID // P])
        gl = sb("gl", [P, 2, HID // P, P])
        ac2 = sb("ac2", [P, 2, HID // P, P])
        osb = sb("osb", [P, 2, D])

        block = ctx.enter_context(nc.Block())
        NQ = NG // GQ
        Z, MXD, NMXD, V2, P2, RZ, ZD, YS, SS, MXE = range(10)

        def three(pe, dst, lhi, llo, rhi, rlo):
            n = 0
            for h in range(H2):
                for a, b in ((lhi, rhi), (lhi, rlo), (llo, rhi)):
                    r = pe.matmul(dst, a(h), b(h), start=(n == 0), stop=(n == 5))
                    n += 1
            return r

        def f3_done(e):
            e.wait_ge(s["h_sle"], 2 * NQ)
            e.wait_ge(s["h_wt"], NQ)
            e.wait_ge(s["h_sl"], NQ)

        def store(ac, k):
            ac.wait_ge(s["x_o"], k + 1)
            ac.dma_start(oall[MN * k:MN * (k + 1)], osb[:, k % 2, :]).then_inc(s[f"st_o{k % 2}"], 16)

        @block.sync
        def _(sp):
            for e in range(E1N):
                if e >= 2:
                    sp.wait_ge(s["g_se"], e - 1)
                sp.dma_start(wsl[:, e % 2], A["wsl"][e]).then_inc(s[f"ld_ws{e % 2}"], 16)
            sp.wait_ge(s["f_me"], NG)
            sp.wait_ge(s["g_se"], E1N)
            sp.wait_ge(s["g_tr"], 2 * E1N)
            for k in range(KE + 1):
                if k < KE:
                    n = k % NW
                    if k >= NW:
                        sp.wait_ge(s["x_up"], k - NW + 1)
                    sp.dma_start(w1b[n][:], A["w1"][k]).then_inc(s[f"ld_u{n}"], 16)
                    if k < NW:
                        sp.dma_start(w2b[n][:], A["w2"][k]).then_inc(s[f"ld_d{n}"], 16)
                    if k == NW - 1:
                        f3_done(sp)
                        sp.dma_start(b1b[:], A["b1"]).then_inc(s["ld_b1"], 16)
                        for n in range(NW):
                            sp.dma_start(b2b[n][:], A["b2"][n:n + 1, :].partition_broadcast(P).rearrange("p o d -> p (o d)")
                                         ).then_inc(s[f"ld_d{n}"], 16)
                if k > NW:
                    n = (k - 1) % NW
                    sp.wait_ge(s["x_o"], k - NW)
                    sp.dma_start(w2b[n][:], A["w2"][k - 1]).then_inc(s[f"ld_d{n}"], 16)
                    sp.dma_start(b2b[n][:], A["b2"][k - 1:k, :].partition_broadcast(P).rearrange("p o d -> p (o d)")
                                 ).then_inc(s[f"ld_d{n}"], 16)
            for t in range(0, NT, 2):
                sp.wait_ge(s["y_x"], t + 2)
                sp.dma_start(out[:, t:t + 2, :], X[:, t:t + 2, :]).then_inc(s["st_out"], 16)
            sp.wait_ge(s["st_out"], 8 * NT)

        @block.gpsimd
        def _(pl):
            pl.wait_ge(s["f_v"], 1)
            for c in range(NT // 8):
                pl.tensor_tensor(lnx[:, 1, 8 * c:8 * c + 8], lnx[:, 0, 8 * c:8 * c + 8], mhalf[:], ALU.pow).then_inc(s["f_pow"], 1)

            def gain(a):
                for t in range(TPC):
                    pl.wait_ge(s["f_xn"], TPC * a + t + 1)
                    if a >= 2 and t == 0:
                        pl.wait_ge(s["f_sl"], TPC * (a - 1))
                    pl.tensor_tensor(xg[:, a % 2, t, :], xn[:, a % 2, t, :], gin[:], ALU.mult).then_inc(s["f_xg"], 1)

            gain(0)
            for a in range(NC):
                if a + 1 < NC:
                    gain(a + 1)
                for t in range(TPC):
                    cs = slice(2 * t, 2 * t + 2)
                    pl.wait_ge(s["f_v2"], TPC * a + t + 1)
                    pl.tensor_tensor(sm1[:, a % 2, P2, cs], sm1[:, a % 2, V2, cs], mhalf[:, 0:2], ALU.pow).then_inc(s["f_pow2"], 1)
            for e in range(E1N):
                pl.wait_ge(s["g_v"], e + 1)
                if e >= 2:
                    pl.wait_ge(s["g_n"], E2N * (e - 1))
                pl.tensor_tensor(sm2[:, e % 2, 1], sm2[:, e % 2, 0], mhalf[:, 0:E2N], ALU.pow).then_inc(s["g_pow"], 1)
            pl.wait_ge(s["g_tr"], 2 * E1N)
            pl.memset(blk[:], 0.0).then_inc(s["blk_ok"], 1)
            bv = blk[:].rearrange("p (e n) -> p e n", e=E1N)
            pl.wait_ge(s["blk_ok"], 1)
            pl.affine_select(out=bv, in_=bv, compare_op=ALU.is_ge, fill=BIG, base=0,
                             pattern=[[-S1N, E1N], [0, S1N]], channel_multiplier=1).then_inc(s["blk_ok"], 1)
            pl.wait_ge(s["blk_ok"], 2)
            pl.affine_select(out=bv, in_=bv, compare_op=ALU.is_ge, fill=BIG, base=S1N - 1,
                             pattern=[[S1N, E1N], [0, S1N]], channel_multiplier=-1).then_inc(s["blk_ok"], 1)

        @block.scalar
        def _(ac):
            def rows(a):
                if a == 0:
                    ac.wait_ge(s["f_nb"], 1)
                if a >= 2:
                    ac.wait_ge(s["f_xg"], TPC * (a - 1))
                for t in range(TPC):
                    n = TPC * a + t
                    ac.activation(xn[:, a % 2, t, :], X[:, n, :], ACT.Identity, bias=lnx[:, 2, n:n + 1],
                                  scale=lnx[:, 1, n:n + 1]).then_inc(s["f_xn"], 1)

            def high(a):
                for h in range(H2):
                    ac.wait_ge(s["f_tr"], 2 * a + h + 1)
                    if a >= 2 and h == 0:
                        ac.wait_ge(s["f_l"], a - 1)
                    ac.copy(hhi[:, a % 2, h, :], TP[h][0:DH, :]).then_inc(s["f_hhi"], 1)

            def disp(a):
                ac.wait_ge(s["f_mxt"], a + 1)
                if a:
                    ac.wait_ge(s["f_dtr"], a)
                for g in range(8):
                    ac.activation(D1[:, g * GT:(g + 1) * GT], MM[0][:, g * GT:(g + 1) * GT], ACT.Exp,
                                  bias=sm1[:, a % 2, NMXD, g:g + 1], accum_out=sm1[:, a % 2, ZD, g:g + 1]).then_inc(s["f_d"], 1)

            def comb(a):
                ac.wait_ge(s["f_mx"], a + 1)
                if a:
                    ac.wait_ge(s["f_etr"], a)
                for t in range(TPC):
                    ac.activation(E1[:, t, :], MM[1][:, t * NS:(t + 1) * NS], ACT.Exp, bias=sm1[:, a % 2, MXE, 4 + t:5 + t],
                                  accum_out=sm1[:, a % 2, Z, t:t + 1]).then_inc(s["f_e"], 1)

            rows(0)
            high(0)
            disp(0)
            comb(0)
            for a in range(NC):
                if a + 1 < NC:
                    rows(a + 1)
                ac.wait_ge(s["f_etr"], a + 1)
                ac.copy(E1T[:, a * CH:(a + 1) * CH], MM[2][:]).then_inc(s["f_e1t"], 1)
                if a + 1 < NC:
                    high(a + 1)
                for t in range(TPC):
                    ac.wait_ge(s["f_sl"], TPC * a + t + 1)
                    if t == 0:
                        ac.wait_ge(s["f_z"], a + 1)
                    for g in range(2):
                        n = 2 * t + g
                        if TPC * a + t or g:
                            ac.wait_ge(s["f_ssq"], 8 * a + n)
                        ac.activation(sq[:], OP[t % 2][:, g * D:(g + 1) * D], ACT.Square, scale=sm1[:, a % 2, RZ, n:n + 1],
                                      accum_out=sm1[:, a % 2, SS, n:n + 1]).then_inc(s["f_ssq"], 1)
                if a + 1 < NC:
                    disp(a + 1)
                for g in range(8):
                    ac.wait_ge(s["f_yt"], 8 * a + g + 1)
                    ac.copy(ynT[:, 8 * a + g], TP[g % 2][0:DH, 0:2 * (P + 32)].rearrange("p (h n) -> p h n", h=2)[:, :, 0:P]
                            ).then_inc(s["f_yte"], 1)
                    if g == 3 and a + 1 < NC:
                        comb(a + 1)

            for e in range(E1N + 1):
                if e < E1N:
                    m = 2 * (e % 2)
                    ac.wait_ge(s["g_se"], e + 1)
                    if e >= 2:
                        ac.wait_ge(s["g_v"], e - 1)
                    if e == 0:
                        ac.wait_ge(s["f_me"], NG)
                    for q in range(E2N):
                        if e or q:
                            ac.wait_ge(s["g_ssq"], E2N * e + q)
                        ac.activation(sq2[:], MM[m + q // 2][:, (q % 2) * D:(q % 2 + 1) * D], ACT.Square,
                                      accum_out=sm2[:, e % 2, 2, q:q + 1]).then_inc(s["g_ssq"], 1)
                if e:
                    ac.wait_ge(s["g_tr"], 2 * e - 1)
                    ac.copy(se2T[:, 0, :, e - 1].rearrange("p g q m -> p q g m"),
                            TP[0][0:DH, :].rearrange("p (q g m) -> p q g m", q=E2N, g=NG)).then_inc(s["g_ev"], 1)

            def exps(q, which):
                if which == 0:
                    ac.wait_ge(s["h_mxc"], q + 1)
                    if q:
                        ac.wait_ge(s["h_cn"], q)
                    for g in range(GQ):
                        ac.activation(C2[:, g, :], L2[:, q % 2, g, :], ACT.Exp, bias=sm3[:, 1, g:g + 1],
                                      accum_out=sm3[:, 2, g:g + 1]).then_inc(s["h_c"], 1)
                else:
                    ac.wait_ge(s["h_mxd"], q + 1)
                    if q:
                        ac.wait_ge(s["h_dn"], q)
                    for g in range(GQ):
                        ac.activation(D2T[:, g, :], MM[1][:, g * NS:(g + 1) * NS], ACT.Exp, bias=sm3[:, 5, g:g + 1],
                                      accum_out=sm3[:, 6, g:g + 1]).then_inc(s["h_d"], 1)

            exps(0, 0)
            exps(0, 1)
            for q in range(NQ):
                ac.wait_ge(s["h_dtr"], q + 1)
                if q >= 2:
                    ac.wait_ge(s["h_sl"], q - 1)
                ac.copy(D2[:, q % 2], MM[2][:].rearrange("p (g n) -> p g n", g=GQ)).then_inc(s["h_d2"], 1)
                if q + 1 < NQ:
                    exps(q + 1, 0)
                ac.wait_ge(s["h_w"], q + 1)
                ac.copy(E1T[:, q * GQ * GT:(q + 1) * GQ * GT], MM[3][:, 0:GQ * GT]).then_inc(s["h_wt"], 1)
                if q + 1 < NQ:
                    exps(q + 1, 1)
                ac.wait_ge(s["h_sl"], q + 1)
                ac.copy(sl2T[:, 0, :, :, GQ * q:GQ * (q + 1)],
                        OP[0][0:DH, :].rearrange("p (g k m) -> p k m g", g=GQ, k=KE)).then_inc(s["h_sle"], 1)

            ac.wait_ge(s["ld_b1"], 16)
            for k in range(KE):
                m = 2 * (k % 2)
                ac.wait_ge(s["x_up"], k + 1)
                if k >= 2:
                    ac.wait_ge(s["x_act"], HID // P * (k - 1))
                for c in range(HID // P):
                    ac.activation(gl[:, k % 2, c, :], MM[m + 1][:, c * P:(c + 1) * P], ACT.Gelu_apprx_tanh,
                                  bias=b1b[:, k, HID // P + c:HID // P + c + 1]).then_inc(s["x_gl"], 1)
                if k:
                    store(ac, k - 1)
            store(ac, KE - 1)

        @block.vector
        def _(dv):
            count = [0]

            def link(ins):
                ins.then_inc(s["f_ch"], 1)
                count[0] += 1
                dv.wait_ge(s["f_ch"], count[0])

            for c in range(NC):
                for t in range(TPC):
                    if c:
                        dv.wait_ge(s["f_st"], 2 * TPC * c - TPC + t + 1)
                    dv.bn_stats(st[:, t, :], X[:, TPC * c + t, :]).then_inc(s["f_st"], 1)
                for t in range(TPC):
                    dv.wait_ge(s["f_st"], 2 * TPC * c + t + 1)
                    dv.bn_aggr(mvx[:, TPC * c + t, :], st[:, t, :]).then_inc(s["f_st"], 1)
            dv.wait_ge(s["f_st"], 2 * NT)
            dv.tensor_scalar(lnx[:, 0, :], mvx[:, :, 1], 1.0 + EL2 / D, EPS * EL2 / D, ALU.mult, ALU.add).then_inc(s["f_v"], 1)
            dv.memset(DT[0:GT, :, 1, :], 0.0).then_inc(s["f_dt"], 1)
            dv.memset(DT[GT:P, :, 0, :], 0.0).then_inc(s["f_dt"], 1)
            dv.wait_ge(s["f_pow"], 2)
            dv.scalar_tensor_tensor(out=lnx[:, 2, :], in0=mvx[:, :, 0], scalar=-1.0, in1=lnx[:, 1, :],
                                    op0=ALU.mult, op1=ALU.mult).then_inc(s["f_nb"], 1)
            bc = lambda ap, n: ap.unsqueeze(2).broadcast_to([P, ap.shape[1], n])

            def low(a):
                for h in range(H2):
                    dv.wait_ge(s["f_hhi"], 2 * a + h + 1)
                    if a >= 2 and h == 0:
                        dv.wait_ge(s["f_l"], a - 1)
                    dv.tensor_tensor(hlo[:, a % 2, h, :], TP[h][0:DH, :], hhi[:, a % 2, h, :].bitcast(F32), ALU.subtract
                                     ).then_inc(s["f_hlo"], 1)

            def max_disp(a):
                p = a % 2
                dv.wait_ge(s["f_lt"], a + 1)
                if a >= 2:
                    dv.wait_ge(s["f_d"], 8 * (a - 1))
                link(dv.tensor_reduce(sm1[:, p, MXD, :], MM[0][:].rearrange("p (g t) -> p g t", g=8), AX.X, ALU.max))
                dv.tensor_scalar(sm1[:, p, NMXD, :], sm1[:, p, MXD, :], -1.0, None, ALU.mult).then_inc(s["f_mxt"], 1)

            def max_comb(a):
                p = a % 2
                dv.wait_ge(s["f_l"], a + 1)
                if a >= 2:
                    dv.wait_ge(s["f_e"], TPC * (a - 1))
                link(dv.tensor_reduce(sm1[:, p, MXE, 0:TPC], MM[1][:].rearrange("p (g t) -> p g t", g=TPC), AX.X, ALU.max))
                dv.tensor_scalar(sm1[:, p, MXE, 4:4 + TPC], sm1[:, p, MXE, 0:TPC], -1.0, None, ALU.mult).then_inc(s["f_mx"], 1)

            low(0)
            max_disp(0)
            max_comb(0)
            for a in range(NC):
                p = a % 2
                dv.wait_ge(s["f_e"], TPC * (a + 1))
                link(dv.reciprocal(rz1[:, TPC * a:TPC * (a + 1)], sm1[:, p, Z, 0:TPC]))
                dv.wait_ge(s["f_d"], 8 * (a + 1))
                if a >= 2:
                    dv.wait_ge(s["f_ssq"], 8 * (a - 1))
                dv.reciprocal(sm1[:, p, RZ, :], sm1[:, p, ZD, :]).then_inc(s["f_z"], 1)
                dv.wait_ge(s["f_dtr"], a + 1)
                if a:
                    dv.wait_ge(s["f_sl"], TPC * a)
                dv.tensor_copy(DT[0:GT, :, 0, :], MM[3][0:GT, :].rearrange("p (t n) -> p t n", t=TPC)).then_inc(s["f_dt"], 1)
                dv.tensor_copy(DT[GT:P, :, 1, :], MM[3][GT:P, :].rearrange("p (t n) -> p t n", t=TPC)).then_inc(s["f_dt"], 1)
                if a + 1 < NC:
                    low(a + 1)
                    max_disp(a + 1)

                def gains(t):
                    cs = slice(2 * t, 2 * t + 2)
                    dv.wait_ge(s["f_pow2"], TPC * a + t + 1)
                    if t == 0:
                        dv.wait_ge(s["f_z"], a + 1)
                    link(dv.scalar_tensor_tensor(out=sm1[:, p, YS, cs], in0=sm1[:, p, P2, cs], scalar=RD,
                                                 in1=sm1[:, p, RZ, cs], op0=ALU.mult, op1=ALU.mult))
                    for g in range(2):
                        n = 2 * t + g
                        dv.scalar_tensor_tensor(out=YN[:, 8 * a + n, :], in0=OP[t % 2][:, g * D:(g + 1) * D],
                                                scalar=sm1[:, p, YS, n:n + 1], in1=g2[:], op0=ALU.mult, op1=ALU.mult
                                                ).then_inc(s["f_yn"], 1)

                for t in range(TPC):
                    dv.wait_ge(s["f_ssq"], 8 * a + 2 * t + 2)
                    cs = slice(2 * t, 2 * t + 2)
                    dv.tensor_scalar(sm1[:, p, V2, cs], sm1[:, p, SS, cs], EL2, None, ALU.add).then_inc(s["f_v2"], 1)
                    if t % 2:
                        gains(t - 1)
                        gains(t)
                if a + 1 < NC:
                    max_comb(a + 1)
                for g in range(8):
                    dv.wait_ge(s["f_yte"], 8 * a + g + 1)
                    dv.tensor_copy(meT[:, :, :, 8 * a + g, :],
                                   TP[g % 2][0:DH, 0:2 * (P + 32)].rearrange("p (h n) -> p h n", h=2)[:, :, P:].rearrange(
                                       "p h (e m) -> p h e m", e=E1N)).then_inc(s["f_me"], 1)

            def copy_query(e):
                dv.wait_ge(s["g_tr"], 2 * e + 2)
                dv.tensor_copy(se2T[:, 1, :, e].rearrange("p g q m -> p q g m"),
                               TP[1][0:DH, :].rearrange("p (q g m) -> p q g m", q=E2N, g=NG)).then_inc(s["g_s"], 1)

            for e in range(E1N):
                p, m = e % 2, 2 * (e % 2)
                dv.wait_ge(s["g_ssq"], E2N * (e + 1))
                dv.tensor_scalar(sm2[:, p, 0], sm2[:, p, 2], EL2, None, ALU.add).then_inc(s["g_v"], 1)
                if e:
                    copy_query(e - 1)
                dv.wait_ge(s["g_pow"], e + 1)
                for q in range(E2N):
                    dv.tensor_scalar(se2n[:, p, q, :], MM[m + q // 2][:, (q % 2) * D:(q % 2 + 1) * D],
                                     sm2[:, p, 1, q:q + 1], RD, ALU.mult, ALU.mult).then_inc(s["g_n"], 1)
            copy_query(E1N - 1)

            dv.wait_ge(s["blk_ok"], 3)

            def logits2(q):
                dv.wait_ge(s["h_l2"], q + 1)
                if q >= 2:
                    dv.wait_ge(s["h_c"], GQ * (q - 1))
                    dv.wait_ge(s["h_tr"], q - 1)
                m4 = MM[0][:].rearrange("p (g n) -> p g n", g=GQ)
                dv.tensor_tensor(L2[:, q % 2], m4, blk[:].unsqueeze(1).broadcast_to([P, GQ, NS]), ALU.add).then_inc(s["h_l2m"], 1)
                dv.wait_ge(s["h_l2m"], q + 1)
                if q:
                    dv.wait_ge(s["h_c"], GQ * q)
                link(dv.tensor_reduce(sm3[:, 0, :], L2[:, q % 2], AX.X, ALU.max))
                dv.tensor_scalar(sm3[:, 1, :], sm3[:, 0, :], -1.0, None, ALU.mult).then_inc(s["h_mxc"], 1)
                dv.wait_ge(s["h_tr"], q + 1)
                if q:
                    dv.wait_ge(s["h_d"], GQ * q)
                link(dv.tensor_reduce(sm3[:, 4, :], MM[1][:].rearrange("p (g n) -> p g n", g=GQ), AX.X, ALU.max))
                dv.tensor_scalar(sm3[:, 5, :], sm3[:, 4, :], -1.0, None, ALU.mult).then_inc(s["h_mxd"], 1)

            logits2(0)
            for q in range(NQ):
                dv.wait_ge(s["h_c"], GQ * (q + 1))
                link(dv.reciprocal(sm3[:, 3, :], sm3[:, 2, :]))
                if q:
                    dv.wait_ge(s["h_w"], q)
                dv.tensor_tensor(C2n[:], C2[:], bc(sm3[:, 3, :], NS), ALU.mult).then_inc(s["h_cn"], 1)
                dv.wait_ge(s["h_d"], GQ * (q + 1))
                link(dv.reciprocal(sm3[:, 7, :], sm3[:, 6, :]))
                if q:
                    dv.wait_ge(s["h_dtr"], q)
                dv.tensor_tensor(D2n[:], D2T[:], bc(sm3[:, 7, :], NS), ALU.mult).then_inc(s["h_dn"], 1)
                if q + 1 < NQ:
                    logits2(q + 1)
                dv.wait_ge(s["h_sl"], q + 1)
                dv.tensor_copy(sl2T[:, 1, :, :, GQ * q:GQ * (q + 1)],
                               OP[1][0:DH, :].rearrange("p (g k m) -> p k m g", g=GQ, k=KE)).then_inc(s["h_sle"], 1)

            dv.wait_ge(s["ld_b1"], 16)

            def bias2(k):
                dv.wait_ge(s["x_down"], k + 1)
                dv.wait_ge(s[f"ld_d{k % NW}"], 32 * (k // NW + 1))
                if k >= 2:
                    dv.wait_ge(s[f"st_o{k % 2}"], 16 * (k // 2))
                dv.tensor_tensor(osb[:, k % 2, :], OP[k % 2][:, 0:D], b2b[k % NW][:], ALU.add).then_inc(s["x_o"], 1)

            for k in range(KE):
                m = 2 * (k % 2)
                dv.wait_ge(s["x_up"], k + 1)
                if k >= 2:
                    dv.wait_ge(s["x_down"], k - 1)
                for c in range(HID // P):
                    dv.wait_ge(s["x_gl"], HID // P * k + c + 1)
                    dv.scalar_tensor_tensor(out=ac2[:, k % 2, c, :], in0=MM[m][:, c * P:(c + 1) * P], scalar=b1b[:, k, c:c + 1],
                                            in1=gl[:, k % 2, c, :], op0=ALU.add, op1=ALU.mult).then_inc(s["x_act"], 1)
                if k:
                    bias2(k - 1)
            bias2(KE - 1)

            for t in range(NT):
                dv.wait_ge(s["y_o"], t + 1)
                dv.scalar_tensor_tensor(out=X[:, t, :], in0=OP[t % 2][:, 0:D], scalar=rz1[:, t:t + 1], in1=X[:, t, :],
                                        op0=ALU.mult, op1=ALU.add).then_inc(s["y_x"], 1)

        @block.tensor
        def _(pe):
            full = lambda x, a: (lambda h: x[:, a % 2, h, :])
            phi_h, phi_l = (lambda h: phihi[:, h, :]), (lambda h: philo[:, h, :])

            def turn(a):
                for t in range(TPC):
                    pe.wait_ge(s["f_xg"], TPC * a + t + 1)
                    if a >= 2 and t == 0:
                        pe.wait_ge(s["f_me"], 8 * (a - 1))
                    for h in range(H2):
                        r = pe.transpose(TP[h][0:DH, t * P:(t + 1) * P], xg[:, a % 2, t, h * DH:(h + 1) * DH], ident[:])
                        if t == TPC - 1:
                            r.then_inc(s["f_tr"], 1)

            def by_slot(a):
                pe.wait_ge(s["f_hlo"], 2 * (a + 1))
                if a:
                    pe.wait_ge(s["f_d"], 8 * a)
                three(pe, MM[0][:], phi_h, phi_l, full(hhi, a), full(hlo, a)).then_inc(s["f_lt"], 1)

            def by_token(a):
                if a:
                    pe.wait_ge(s["f_e"], TPC * a)
                for t in range(TPC):
                    r = three(pe, MM[1][:, t * NS:(t + 1) * NS], lambda h: hhi[:, a % 2, h, t * P:(t + 1) * P],
                              lambda h: hlo[:, a % 2, h, t * P:(t + 1) * P], phi_h, phi_l)
                r.then_inc(s["f_l"], 1)

            turn(0)
            by_slot(0)
            by_token(0)
            for a in range(NC):
                if a + 1 < NC:
                    turn(a + 1)
                pe.wait_ge(s["f_d"], 8 * (a + 1))
                if a:
                    pe.wait_ge(s["f_dt"], 2 * a + 2)
                for t in range(TPC):
                    r = pe.transpose(MM[3][:, t * P:(t + 1) * P], D1[:, t * P:(t + 1) * P], ident[:])
                r.then_inc(s["f_dtr"], 1)
                pe.wait_ge(s["f_e"], TPC * (a + 1))
                if a:
                    pe.wait_ge(s["f_e1t"], a)
                for t in range(TPC):
                    r = pe.transpose(MM[2][:, t * P:(t + 1) * P], E1[:, t, :], ident[:])
                r.then_inc(s["f_etr"], 1)
                if a + 1 < NC:
                    by_slot(a + 1)
                pe.wait_ge(s["f_dt"], 2 * (a + 2))
                for t in range(TPC):
                    if a or t >= 2:
                        pe.wait_ge(s["f_yn"], 2 * (TPC * a + t) - 2)
                    for g in range(2):
                        r = pe.matmul(OP[t % 2][:, g * D:(g + 1) * D], DT[:, t, g, :], xg[:, a % 2, t, :], start=True, stop=True)
                    r.then_inc(s["f_sl"], 1)
                    if t == 1 and a + 1 < NC:
                        by_token(a + 1)
                for g in range(8):
                    n = 8 * a + g
                    pe.wait_ge(s["f_yn"], n + 1)
                    if g >= 2:
                        pe.wait_ge(s["f_me"], n - 1)
                    for h in range(H2):
                        r = pe.matmul(TP[g % 2][0:DH, h * (P + 32):(h + 1) * (P + 32)], YN[:, n, h * DH:(h + 1) * DH], iavg[:],
                                      start=True, stop=True)
                    r.then_inc(s["f_yt"], 1)

            def queries(e):
                pe.wait_ge(s[f"ld_ws{e % 2}"], 16 * (e // 2 + 1))
                if e == 0:
                    pe.wait_ge(s["f_me"], NG)
                    pe.wait_ge(s["f_e1t"], NC)
                if e >= 2:
                    pe.wait_ge(s["g_n"], E2N * (e - 1))
                for n in range(2):
                    for h in range(H2):
                        r = pe.matmul(MM[2 * (e % 2) + n][:, 0:2 * D], meT[:, h, e].rearrange("p g m -> p (g m)"),
                                      wsl[:, e % 2, h, 2 * n * D:2 * (n + 1) * D], start=(h == 0), stop=(h == 1))
                r.then_inc(s["g_se"], 1)

            queries(0)
            for e in range(E1N):
                if e + 1 < E1N:
                    queries(e + 1)
                pe.wait_ge(s["g_n"], E2N * (e + 1))
                for h in range(H2):
                    if e:
                        pe.wait_ge(s["g_ev"] if h == 0 else s["g_s"], e)
                    for q in range(E2N):
                        r = pe.transpose(TP[h][0:DH, q * P:(q + 1) * P], se2n[:, e % 2, q, h * DH:(h + 1) * DH], ident[:])
                    r.then_inc(s["g_tr"], 1)

            pe.wait_ge(s["g_ev"], E1N)
            pe.wait_ge(s["g_s"], E1N)

            def match(q):
                if q:
                    pe.wait_ge(s["h_l2m"], q)
                for g in range(GQ):
                    n = GQ * q + g
                    for h in range(H2):
                        r = pe.matmul(MM[0][:, g * NS:(g + 1) * NS], ynT[:, n, h, :],
                                      se2T[:, h, n].rearrange("p e q m -> p (e q m)"), start=(h == 0), stop=(h == 1))
                r.then_inc(s["h_l2"], 1)

            def match_turn(q):
                pe.wait_ge(s["h_l2m"], q + 1)
                if q:
                    pe.wait_ge(s["h_d"], GQ * q)
                for g in range(GQ):
                    r = pe.transpose(MM[1][:, g * NS:(g + 1) * NS], L2[:, q % 2, g, :], ident[:])
                r.then_inc(s["h_tr"], 1)

            match(0)
            match_turn(0)
            for q in range(NQ):
                if q + 1 < NQ:
                    match(q + 1)
                pe.wait_ge(s["h_dn"], q + 1)
                if q:
                    pe.wait_ge(s["h_d2"], q)
                for g in range(GQ):
                    r = pe.transpose(MM[2][:, g * NS:(g + 1) * NS], D2n[:, g, :], ident[:])
                r.then_inc(s["h_dtr"], 1)
                pe.wait_ge(s["h_cn"], q + 1)
                if q:
                    pe.wait_ge(s["h_wt"], q)
                for g in range(GQ):
                    n = GQ * q + g
                    r = pe.matmul(MM[3][:, g * GT:(g + 1) * GT], C2n[:, g, :], E1T[:, n * GT:(n + 1) * GT],
                                  start=True, stop=True)
                r.then_inc(s["h_w"], 1)
                if q + 1 < NQ:
                    match_turn(q + 1)
                pe.wait_ge(s["h_d2"], q + 1)
                if q:
                    pe.wait_ge(s["h_sle"], 2 * q)
                for g in range(GQ):
                    for h in range(H2):
                        r = pe.matmul(OP[h][0:DH, g * NS:(g + 1) * NS], YN[:, GQ * q + g, h * DH:(h + 1) * DH], D2[:, q % 2, g, :],
                                      start=True, stop=True)
                r.then_inc(s["h_sl"], 1)

            def up(k):
                if k == 0:
                    pe.wait_ge(s["h_sle"], 2 * NQ)
                    pe.wait_ge(s["h_wt"], NQ)
                pe.wait_ge(s[f"ld_u{k % NW}"], 16 * (k // NW + 1))
                if k >= 2:
                    pe.wait_ge(s["x_act"], HID // P * (k - 1))
                for half in (1, 0):
                    for c in range(HID // P):
                        o = half * HID + c * P
                        for h in range(H2):
                            r = pe.matmul(MM[2 * (k % 2) + half][:, c * P:(c + 1) * P], w1b[k % NW][:, h, o:o + P],
                                          sl2T[:, h, k].rearrange("p m g -> p (m g)"), start=(h == 0), stop=(h == 1))
                r.then_inc(s["x_up"], 1)

            up(0)
            for k in range(KE):
                if k + 1 < KE:
                    up(k + 1)
                pe.wait_ge(s["x_act"], HID // P * (k + 1))
                pe.wait_ge(s[f"ld_d{k % NW}"], 32 * (k // NW + 1))
                if k >= 2:
                    pe.wait_ge(s["x_o"], k - 1)
                for c in range(HID // P):
                    r = pe.matmul(OP[k % 2][:, 0:D], ac2[:, k % 2, c, :], w2b[k % NW][:, c, :], start=(c == 0), stop=(c == 3))
                r.then_inc(s["x_down"], 1)

            pe.wait_ge(s["st_o0"], 8 * KE)
            pe.wait_ge(s["st_o1"], 8 * KE)
            pe.wait_ge(s["x_o"], KE)
            for t in range(NT):
                if t >= 2:
                    pe.wait_ge(s["y_x"], t - 1)
                for g in range(2):
                    r = pe.matmul(OP[t % 2][g * GT:(g + 1) * GT, 0:D], E1T[:, t * P + g * GT:t * P + (g + 1) * GT],
                                  oall[:, 2 * t + g, :], start=True, stop=True)
                r.then_inc(s["y_o"], 1)


def build(nc, A, out):
    with ExitStack() as ctx:
        def ps(name):
            return ctx.enter_context(nc.psum_tensor(name, [P, 512], F32))

        keep = {
            "st_out": ctx.enter_context(nc.semaphore("st_out")),
            "MM": [ps(f"mm{k}") for k in range(4)],
            "TP": [ps(f"tp{h}") for h in range(2)],
            "OP": [ps(f"op{h}") for h in range(2)],
        }
        used = blocks(nc, A, keep)
        nc.all_engine_barrier()
        nc.clear_and_free_semaphores(used)
        nc.all_engine_barrier()
        mixture(nc, A, out, keep)


def layouts(i):
    import numpy as np
    a = {k: np.asarray(v) for k, v in i.items()}
    g = lambda n: a["L0_tok_" + n]
    L = LAYERS
    halves = lambda w: np.ascontiguousarray(w.reshape(w.shape[0], H2, DH, -1).transpose(0, 2, 1, 3))
    win = g("Win").transpose(0, 2, 1)
    zbc = np.stack([g("Wd"), g("WB"), g("WC")], 1).transpose(0, 3, 1, 2).reshape(L, D, 3 * D)
    one, zero = np.ones((1, D), np.float32), np.zeros((1, D), np.float32)
    cw = g("convw")
    cols = [np.concatenate([g("ln_g"), one]), np.concatenate([g("ln_b"), zero])]
    for v in (g("b_in")[:, :D], cw[..., 0], g("convb"), g("b_in")[:, D:], g("bd"), cw[..., 1], cw[..., 2], cw[..., 3], g("bB"), g("bC")):
        cols.append(np.concatenate([v, zero]))
    pc = np.stack(cols, -1).reshape(L + 1, H2, DH, NPC).transpose(2, 0, 1, 3)
    aw = lambda n: a["L0_attn_" + n]
    attn = np.concatenate([aw("Wq"), aw("Wk"), aw("Wf"), aw("Wf"), aw("Wv"), aw("Wo")], 1)[None]
    ff = lambda n: a["L0_ffn_" + n]
    r = {
        "slots1": ff("slots1").reshape(NS, D),
        "g2": np.repeat(ff("gamma2"), S1N, axis=0),
        "gin": np.broadcast_to(ff("gamma_in"), (P, D)),
        "wsl": halves(ff("w_slot2")),
        "w1": halves(ff("w1").reshape(KE, D, 2 * HID)),
        "w2": ff("w2").reshape(KE, HID // P, P, D).transpose(0, 2, 1, 3),
        "b1": ff("b1").reshape(KE, 2 * HID // P, P).transpose(2, 0, 1),
        "b2": ff("b2").reshape(KE, D),
        "aw": halves(attn)[0],
        "abf": np.concatenate([aw("bf"), aw("bf")])[:, None],
        "agb": np.stack([aw("gamma"), aw("beta")], -1).reshape(H2, DH, 2).transpose(1, 0, 2),
        "tok": a["x"].reshape(NT, P).T,
        "pos": g("pos_enc").reshape(S // P, P, D).transpose(1, 0, 2),
        "emb": g("embedding"),
        "pc": pc,
        "wu": halves(win[:, :, :D]), "wv": halves(win[:, :, D:]), "wz": halves(zbc),
        "wo": halves(g("Wout").transpose(0, 2, 1)),
        "bout": np.broadcast_to(g("bout")[:, None, :], (L, P, D)),
    }
    return {k: np.ascontiguousarray(v) for k, v in r.items()}
def kernel(**inputs):
    import numpy as np
    import concourse.bacc as bacc
    from concourse.bass_utils import run_bass_kernel_spmd

    nc = bacc.Bacc("TRN2", target_bir_lowering=False, num_devices=1)
    arrays = layouts(inputs)
    aps = {n: nc.dram_tensor(n, v.shape, mybir.dt.from_np(v.dtype), kind="ExternalInput").ap() for n, v in arrays.items()}
    out = nc.dram_tensor("out_0", (P, NT, D), F32, kind="ExternalOutput").ap()
    build(nc, aps, out)
    r = run_bass_kernel_spmd(nc, [arrays], core_ids=[0])
    return np.ascontiguousarray(r.results[0]["out_0"].transpose(1, 0, 2)).reshape(B, S, D)
```

```python
import concourse.bass as bass
from concourse import mybir
from contextlib import ExitStack

F32 = mybir.dt.float32
F32R = mybir.dt.float32r
I32 = mybir.dt.int32
ALU = mybir.AluOpType
ACT = mybir.ActivationFunctionType
AX = mybir.AxisListType

P = 128
B, S, D, LAYERS, KC, V = 8, 256, 192, 4, 4, 8000
T = B * S
NT = T // P
H2 = 2
DH = D // H2
DB = D - P
PH = (P, DB)
CH = 512
BPC = CH // S
TPC = CH // P
NC = T // CH
EPS = 1e-5
EXP_20, EXP_M20 = 485165195.4097903, 2.061153622438558e-09
FMIN = 1e-6
MQ = 64
NG, GT = T // 64, 64
E1N, S1N, E2N, MN = 8, 16, 4, 4
NS = E1N * S1N
KE = E1N * E2N
HID = 512
GQ = 4
EL2 = 1e-6
RD = float(D) ** 0.5
BIG = -1e30
STEPS = LAYERS * NC
G_, B_, BU, W0, CVB, BV, BD, W1, W2, W3, BBM, BCM = range(12)
NPC = 12


def blocks(nc, A, keep):
    with ExitStack() as ctx:
        at = [0]

        def sb(name, shape, dt=F32):
            size = 4
            for n in shape[1:]:
                size *= n
            t = nc.alloc_sbuf_tensor_at(name, shape, dt, offset=at[0])
            at[0] += (size + 31) // 32 * 32
            return t

        at[0] = (nc.sbuf_base + 31) // 32 * 32
        X = sb("X", [P, NT, D])
        keep["xn_at"] = at[0]
        xn = sb("xn", [P, 2, TPC, D])
        st = sb("st", [P, TPC, 6])
        mv = sb("mv", [P, TPC, 2])
        rs = sb("rs", [P, 2, TPC])
        ve = sb("ve", [P, TPC])
        mhalf = sb("mhalf", [P, 8])
        nb = sb("nb", [P, 2, TPC])
        ident = sb("ident", [P, P])
        ones = sb("ones", [P, 2])
        keep["hhi_at"] = at[0]
        hhi = sb("hhi", [P, 2, H2, CH], F32R)
        keep["hf_at"] = at[0]
        hf = sb("hf", [P, H2, CH])
        hlo = sb("hlo", [P, 2, CH], F32R)
        keep["slots1_at"] = at[0]
        slots1 = sb("slots1", [P, 2 * P])
        g2 = sb("g2", [P, D])
        gin = sb("gin", [P, D])
        phihi = sb("phihi", [P, H2, NS], F32R)
        philo = sb("philo", [P, H2, NS], F32R)
        iavg = sb("iavg", [P, P + NS // MN])
        rz1 = sb("rz1", [P, NT])
        mvx = sb("mvx", [P, NT, 2])
        lnx = sb("lnx", [P, 3, NT])
        keep["overlay"] = at[0]
        keep.update(X=X, st=st, ident=ident, g2=g2, gin=gin, iavg=iavg, mhalf=mhalf, rz1=rz1, xn=xn,
                    hhi=hhi, hlo=hlo, phihi=phihi, philo=philo, mvx=mvx, lnx=lnx)
        tok = sb("tok", [P, NT], I32)
        tokn = sb("tokn", [P, NT], I32)
        pos = sb("pos", [P, S // P, D])
        pc = sb("pc", [P, LAYERS + 1, H2, NPC])
        bout = sb("bout", [P, D])
        widths = (("u", 2 * D), ("z", 3 * D), ("o", D))
        wst = {k: sb("wst_" + k, [P, H2, n]) for k, n in widths}
        whi = {k: sb("whi_" + k, [P, H2, n], F32R) for k, n in widths}
        wlo = {k: sb("wlo_" + k, [P, H2, n], F32R) for k, n in widths}
        u = sb("u", [P, 2, H2, BPC, KC - 1 + S])
        squares = sb("squares", [P, D])
        uc = sb("uc", [P, 2, H2, CH])
        uchi = sb("uchi", [P, 2, H2, CH], F32R)
        uclo = sb("uclo", [P, 2, CH], F32R)
        sig = sb("sig", [P, H2, CH])
        sghi = sb("sghi", [P, 3, H2, CH], F32R)
        sglo = sb("sglo", [P, 3, CH], F32R)
        dec = sb("dec", [P, H2, BPC, 1 + S])
        inp = sb("inp", [P, H2, BPC, 1 + S])
        hs = sb("hs", [P, H2, BPC, 1 + S])
        hc = sb("hc", [P, 2, H2, CH])
        y = sb("y", [P, TPC])
        AW = 2 * P + 2 * D
        awst = sb("awst", [P, H2, AW])
        awhi = sb("awhi", [P, H2, AW], F32R)
        awlo = sb("awlo", [P, H2, AW], F32R)
        abf = sb("abf", [P, 1])
        agb = sb("agb", [P, H2, 2])
        mask = sb("mask", [P, 3, P])
        lim = sb("lim", [P, S])
        eqk = sb("eqk", [P, CH])
        fg = sb("fg", [P, CH])
        cum = sb("cum", [P, CH])
        qk = sb("qk", [P, CH])
        qp = sb("qp", [P, 2, CH])
        kp = sb("kp", [P, 2, CH])
        ast = sb("ast", [P, BPC, 3, P])
        vs = sb("vs", [P, 2, TPC, D + 2])
        den = sb("den", [P, TPC])
        rden = sb("rden", [P, TPC])
        rr = sb("rr", [P, TPC])
        v2 = sb("v2", [P, TPC])
        rs2 = sb("rs2", [P, TPC])
        s2 = sb("s2", [P, TPC])
        nb2 = sb("nb2", [P, TPC])
        st2 = sb("st2", [P, TPC, 6])
        mv2 = sb("mv2", [P, TPC, 2])
        xn2 = sb("xn2", [P, TPC, D])
        h2f = sb("h2f", [P, H2, CH])
        h2hi = sb("h2hi", [P, H2, CH], F32R)
        h2lo = sb("h2lo", [P, CH], F32R)
        assert at[0] <= 229368

        MM, TP, OP = keep["MM"], keep["TP"], keep["OP"]
        s = {}
        for n in """ld_tok ld_c gat0 gat1 gat2 gat3 dw_u dw_z dw_o dw_b init_x bou ident_ok pads pe_u pe_v pe_z
                 pe_bz pe_b pe_c pe_t pe_o pe_y ac_u ac_tap ac_sig ac_sghi ac_h ac_hhi ac_uchi ac_dec ac_xn ac_y
                 ac_wu ac_wz ac_wo lo_wu lo_wz lo_wo dv_st dv_mv pl_rs dv_nb dv_conv pl_uclo dv_hlo pl_sglo dv_x
                 dv_inp dv_scan dv_hc dv_idx ld_aw ac_aw dv_aw pl_ac pe_f pe_av pe_at pe_num pe_t2 pe_ao ac_f
                 ac_eq ac_vs ac_xn2 ac_h2 ac_hhi2 dv_abf dv_qk dv_cum dv_qp dv_kp dv_as dv_v2 dv_s2 dv_nb2
                 dv_h2lo dv_lx dv_xa pl_rs2 pl_ch ld_f dv_zero dv_ch pl_f pe_ph ac_phi dv_phi""".split():
            s[n] = nc.alloc_semaphore(n)

        block = ctx.enter_context(nc.Block())

        UA, UV, VA = slice(0, P), slice(P, 2 * P), slice(2 * P, 3 * P)
        ZA, BA, CA, BZ = (slice(P * k, P * (k + 1)) for k in range(4))
        CB = slice(4 * P, 4 * P + DB)

        def five(pe, dst, whi, wlo, c, xhi, xlo, t, rows=False):
            parts = ((whi[:, 0, c], xhi[:, 0, t]), (whi[:, 0, c], xlo[:, t]), (wlo[:, 0, c], xhi[:, 0, t]),
                     (whi[:, 1, c], xhi[:, 1, t]), (wlo[:, 1, c], xhi[:, 1, t]))
            for n, (w, x) in enumerate(parts):
                r = pe.matmul(dst, x if rows else w, w if rows else x, start=(n == 0), stop=(n == 4))
            return r

        ALL = slice(0, CH)

        def split(dv, name, hi, lo, x):
            dv.tensor_tensor(lo, x[:, 0, :], hi[:, 0, :].bitcast(F32), ALU.subtract).then_inc(s[name], 1)
            dv.tensor_tensor(hi[DB:P, 1, :], x[0:DB, 1, :], hi[0:DB, 1, :].bitcast(F32), ALU.subtract).then_inc(s[name], 1)

        @block.sync
        def _(sp):
            sp.dma_start(tok[:], A["tok"]).then_inc(s["ld_tok"], 16)
            sp.dma_start(pos[:], A["pos"]).then_inc(s["ld_f"], 16)
            sp.dma_start(pc[:], A["pc"]).then_inc(s["ld_c"], 16)
            for k in "uzo":
                sp.dma_start(wst[k][:], A["w" + k][0]).then_inc(s["dw_" + k], 16)
            sp.dma_start(bout[:], A["bout"][0]).then_inc(s["dw_b"], 16)
            sp.dma_start(awst[:], A["aw"]).then_inc(s["ld_aw"], 16)
            sp.dma_start(abf[:], A["abf"]).then_inc(s["ld_f"], 16)
            sp.dma_start(agb[:], A["agb"]).then_inc(s["ld_f"], 16)
            for dst, name in ((slots1, "slots1"), (g2, "g2"), (gin, "gin")):
                sp.dma_start(dst[:], A[name]).then_inc(s["ld_f"], 16)
            for l in range(1, LAYERS):
                for k in "uzo":
                    sp.wait_ge(s["lo_w" + k], l)
                    sp.dma_start(wst[k][:], A["w" + k][l]).then_inc(s["dw_" + k], 16)
                sp.wait_ge(s["bou"], NC * l)
                sp.dma_start(bout[:], A["bout"][l]).then_inc(s["dw_b"], 16)

        def low_w(e, k, l):
            e.wait_ge(s["ac_w" + k], l + 1)
            e.tensor_tensor(wlo[k][:], wst[k][:], whi[k][:].bitcast(F32), ALU.subtract).then_inc(s["lo_w" + k], 1)

        @block.gpsimd
        def _(pl):
            pl.memset(ident[:], 0.0).then_inc(s["ident_ok"], 1)
            pl.wait_ge(s["ident_ok"], 1)
            pl.affine_select(out=ident[:], in_=ident[:], compare_op=ALU.not_equal, fill=1.0, base=0,
                             pattern=[[-1, P]], channel_multiplier=1).then_inc(s["ident_ok"], 1)
            pl.memset(ones[:], 1.0).then_inc(s["pads"], 1)
            pl.memset(mhalf[:], -0.5).then_inc(s["pads"], 1)
            pl.memset(u[:, :, :, :, 0:KC - 1], 0.0).then_inc(s["pads"], 1)
            pl.memset(mask[:], 1.0).then_inc(s["pl_ch"], 1)
            pl.wait_ge(s["pl_ch"], 1)
            pl.affine_select(out=mask[:, 0:2, :], in_=mask[:, 0:2, :], compare_op=ALU.is_ge, fill=0.0, base=0,
                             pattern=[[0, 2], [1, P]], channel_multiplier=-1).then_inc(s["pl_ac"], 1)
            pl.wait_ge(s["dv_idx"], 4)

            def gather(c):
                for t in range(TPC * c, TPC * (c + 1)):
                    pl.indirect_dma_start(out=X[:, t, :], out_offset=None, in_=A["emb"],
                                          in_offset=bass.IndirectOffsetOnAxis(ap=tok[:, t:t + 1], axis=0)
                                          ).then_inc(s[f"gat{c}"], 16)

            def pool_rs(j):
                pl.wait_ge(s["dv_mv"], TPC * (j + 1))
                if j >= 2:
                    pl.wait_ge(s["ac_xn"], TPC * (j - 1))
                if j >= 1:
                    pl.wait_ge(s["pl_rs"], j)
                pl.tensor_scalar(ve[:], mv[:, :, 1], EPS, None, ALU.add).then_inc(s["pl_ch"], 1)
                pl.wait_ge(s["pl_ch"], j + 2)
                pl.tensor_tensor(rs[:, j % 2, :], ve[:], mhalf[:, 0:TPC], ALU.pow).then_inc(s["pl_rs"], 1)

            gather(0)
            gather(1)
            pl.wait_ge(s["pads"], 3)
            pool_rs(0)
            gather(2)
            pool_rs(1)
            gather(3)
            pl.memset(iavg[:, 0:P], 0.0).then_inc(s["pl_f"], 1)
            pl.wait_ge(s["pl_f"], 1)
            pl.affine_select(out=iavg[:, 0:P], in_=iavg[:, 0:P], compare_op=ALU.not_equal, fill=1.0, base=0,
                             pattern=[[-1, P]], channel_multiplier=1).then_inc(s["pl_f"], 1)
            pl.wait_ge(s["pl_f"], 2)
            avg = iavg[:, P:]
            pl.memset(avg, 1.0 / MN).then_inc(s["pl_f"], 1)
            pl.wait_ge(s["pl_f"], 3)
            pl.affine_select(out=avg, in_=avg, compare_op=ALU.is_ge, fill=0.0, base=0,
                             pattern=[[-MN, NS // MN]], channel_multiplier=1).then_inc(s["pl_f"], 1)
            pl.wait_ge(s["pl_f"], 4)
            pl.affine_select(out=avg, in_=avg, compare_op=ALU.is_ge, fill=0.0, base=MN - 1,
                             pattern=[[MN, NS // MN]], channel_multiplier=-1).then_inc(s["pl_f"], 1)
            pl.wait_ge(s["dv_phi"], 1)
            pl.tensor_tensor(rz1[:, 1:2], rz1[:, 0:1], mhalf[:, 0:1], ALU.pow).then_inc(s["pl_f"], 1)
            def pool_lnx(a):
                c = slice(TPC * a, TPC * (a + 1))
                pl.wait_ge(s["dv_lx"], a + 1)
                pl.tensor_tensor(lnx[:, 1, c], lnx[:, 0, c], mhalf[:, 0:TPC], ALU.pow).then_inc(s["pl_ch"], 1)

            for i in range(STEPS):
                c, l, p = i % NC, i // NC, i % 2
                pl.wait_ge(s["ac_xn"], TPC * (i + 1))
                pl.wait_ge(s["dw_b"], 16 * (i // NC + 1))
                xx = X[:, TPC * c:TPC * (c + 1), :]
                pl.tensor_tensor(xx, xx, bout[:].unsqueeze(1).broadcast_to([P, TPC, D]), ALU.add).then_inc(s["bou"], 1)
                pl.wait_ge(s["ac_sghi"], i + 1)
                if i >= 3:
                    pl.wait_ge(s["pe_o"], 2 * (i - 2))
                hi, lo = sghi[:, i % 3], sglo[:, i % 3]
                pl.tensor_tensor(lo, sig[:, 0, :], hi[:, 0, :].bitcast(F32), ALU.subtract).then_inc(s["pl_sglo"], 1)
                pl.wait_ge(s["pl_sglo"], 2 * i + 1)
                pl.tensor_tensor(hi[DB:P, 1, :], sig[0:DB, 1, :], hi[0:DB, 1, :].bitcast(F32), ALU.subtract).then_inc(s["pl_sglo"], 1)
                pl.wait_ge(s["pl_sglo"], 2 * i + 2)
                pool_rs(i + 2)
                pl.wait_ge(s["ac_uchi"], i + 1)
                if i >= 2:
                    pl.wait_ge(s["pe_c"], 2 * (i - 1))
                hi, lo = uchi[:, p], uclo[:, p]
                pl.tensor_tensor(lo, uc[:, p, 0, :], hi[:, 0, :].bitcast(F32), ALU.subtract).then_inc(s["pl_uclo"], 1)
                pl.wait_ge(s["pl_uclo"], 2 * i + 1)
                pl.tensor_tensor(hi[DB:P, 1, :], uc[0:DB, p, 1, :], hi[0:DB, 1, :].bitcast(F32), ALU.subtract).then_inc(s["pl_uclo"], 1)
                pl.wait_ge(s["pl_uclo"], 2 * i + 2)
                if l >= 1 and c < 2:
                    low_w(pl, "zo"[c], l)
            pool_rs(STEPS + 2)
            pool_rs(STEPS + 3)
            for a in range(NC):
                pl.wait_ge(s["dv_v2"], a + 1)
                if a:
                    pl.wait_ge(s["dv_s2"], a)
                pl.tensor_tensor(rs2[:], v2[:], mhalf[:, 0:TPC], ALU.pow).then_inc(s["pl_rs2"], 1)
                if a >= 1:
                    pool_lnx(a - 1)
            pool_lnx(NC - 1)

        def act_ln(ac, j):
            c = j % NC
            ac.wait_ge(s["dv_nb"], j + 1)
            if j >= 2:
                ac.wait_ge(s["pe_t"], 2 * (j - 1))
            for t in range(TPC):
                ac.activation(xn[:, j % 2, t, :], X[:, TPC * c + t, :], ACT.Identity,
                              bias=nb[:, j % 2, t:t + 1], scale=rs[:, j % 2, t:t + 1]).then_inc(s["ac_xn"], 1)

        def free_h(e, j):
            if j - 2 < STEPS:
                e.wait_ge(s["pe_v"], j - 1)
            else:
                e.wait_ge(s["pe_av"], 2 * (j - 1 - STEPS))

        def act_h(ac, j):
            l = j // NC
            for h in range(H2):
                ac.wait_ge(s["pe_t"], 2 * j + h + 1)
                if h == 0:
                    if j >= 1:
                        ac.wait_ge(s["dv_hlo"], 2 * j)
                r = slice(0, PH[h])
                ac.activation(hf[r, h, :], TP[h][r, :], ACT.Identity, bias=pc[r, l, h, B_:B_ + 1],
                              scale=pc[r, l, h, G_:G_ + 1]).then_inc(s["ac_h"], 1)
            ac.wait_ge(s["ac_h"], 2 * (j + 1))
            if j >= 2:
                free_h(ac, j)
            ac.copy(hhi[:, j % 2], hf[:]).then_inc(s["ac_hhi"], 1)

        def act_w(ac, k, l):
            ac.wait_ge(s["dw_" + k], 16 * (l + 1))
            if l:
                last = {"u": ("pe_v", NC * l), "z": ("pe_c", 2 * NC * l),
                        "o": ("pe_o", 2 * NC * l)}[k]
                ac.wait_ge(s[last[0]], last[1])
            ac.copy(whi[k][:], wst[k][:]).then_inc(s["ac_w" + k], 1)

        def act_att(ac):
            ac.wait_ge(s["dv_abf"], 1)
            ac.wait_ge(s["pl_ac"], 6)

            def exps(a):
                m = 2 * (a % 2)
                ac.wait_ge(s["pe_f"], 2 * a + 1)
                if a:
                    ac.wait_ge(s["dv_cum"], 4 * a)
                ac.activation(fg[0:MQ], MM[m + 1][0:MQ, :], ACT.Sigmoid, bias=abf[0:MQ]).then_inc(s["ac_f"], 1)
                ac.activation(fg[MQ:P], MM[m + 1][MQ:P, :], ACT.Exp, bias=abf[MQ:P], scale=-1.0).then_inc(s["ac_f"], 1)
                ac.wait_ge(s["pe_f"], 2 * a + 2)
                if a:
                    ac.wait_ge(s["dv_qk"], a)
                ac.activation(eqk[:], MM[m][:], ACT.Exp).then_inc(s["ac_eq"], 1)

            def values(a):
                if a >= 2:
                    ac.wait_ge(s["pe_num"], 2 * (a - 1))
                for t in range(2):
                    ac.wait_ge(s["pe_av"], 2 * a + t + 1)
                    ac.copy(vs[:, a % 2, 2 * t:2 * t + 2, 0:D], OP[t][:, 0:2 * D].rearrange("p (t d) -> p t d", t=2)
                            ).then_inc(s["ac_vs"], 1)

            exps(0)
            values(0)
            for a in range(NC + 1):
                if a + 1 < NC:
                    exps(a + 1)
                if a >= 1:
                    k = a - 1
                    ac.wait_ge(s["dv_nb2"], k + 1)
                    if k:
                        ac.wait_ge(s["pe_t2"], 2 * k)
                    for t in range(TPC):
                        ac.activation(xn2[:, t, :], OP[t // 2][:, (t % 2) * (D + 2):(t % 2) * (D + 2) + D], ACT.Identity,
                                      bias=nb2[:, t:t + 1], scale=s2[:, t:t + 1]).then_inc(s["ac_xn2"], 1)
                if a + 1 < NC:
                    values(a + 1)
                if a >= 1:
                    for h in range(H2):
                        ac.wait_ge(s["pe_t2"], 2 * k + h + 1)
                        if k and h == 0:
                            ac.wait_ge(s["dv_h2lo"], 2 * k)
                        r = slice(0, PH[h])
                        ac.activation(h2f[r, h, :], TP[h][r, :], ACT.Identity, bias=agb[r, h, 1:2],
                                      scale=agb[r, h, 0:1]).then_inc(s["ac_h2"], 1)
                    ac.wait_ge(s["ac_h2"], 2 * (k + 1))
                    if k:
                        ac.wait_ge(s["pe_ao"], 2 * k)
                    ac.copy(h2hi[:], h2f[:]).then_inc(s["ac_hhi2"], 1)
                if a + 2 < NC:
                    act_h(ac, STEPS + 2 + a)

        @block.scalar
        def _(ac):
            ac.wait_ge(s["ld_c"], 16)
            for k in "uzo":
                act_w(ac, k, 0)
            ac.wait_ge(s["ld_aw"], 16)
            ac.copy(awhi[:], awst[:]).then_inc(s["ac_aw"], 1)
            act_ln(ac, 0)
            ac.wait_ge(s["dv_zero"], 11)
            ac.wait_ge(s["pads"], 3)
            act_h(ac, 0)
            act_ln(ac, 1)
            for i in range(STEPS + 2):
                l, c, p = i // NC, i % NC, i % 2
                if i < STEPS:
                    if i >= 2:
                        ac.wait_ge(s["dv_conv"], 6 * (i - 1))
                    for h in range(H2):
                        r = slice(0, PH[h])
                        ac.wait_ge(s["pe_u"], 2 * i + h + 1)
                        ac.activation(u[r, p, h, :, KC - 1:], MM[h][r, :].rearrange("p (b s) -> p b s", b=BPC),
                                      ACT.Identity, bias=pc[r, l, h, BU:BU + 1]).then_inc(s["ac_u"], 1)
                    if i >= 2:
                        ac.wait_ge(s["dv_inp"], 2 * (i - 1))
                        ac.wait_ge(s["pl_uclo"], 2 * (i - 1))
                    for h in range(H2):
                        r = slice(0, PH[h])
                        ac.wait_ge(s["ac_u"], 2 * i + h + 1)
                        ac.activation(uc[r, p, h, :].rearrange("p (b s) -> p b s", b=BPC), u[r, p, h, :, 0:S],
                                      ACT.Identity, bias=pc[r, l, h, CVB:CVB + 1], scale=pc[r, l, h, W0:W0 + 1]
                                      ).then_inc(s["ac_tap"], 1)
                    if i >= 1:
                        ac.wait_ge(s["pl_sglo"], 2 * i)
                    ac.activation(sig[0:DB, 1, :], MM[1][P - DB:P, :], ACT.Sigmoid, bias=pc[P - DB:P, l, 1, BV:BV + 1]
                                  ).then_inc(s["ac_sig"], 1)
                    ac.wait_ge(s["pe_v"], i + 1)
                    ac.activation(sig[:, 0, :], MM[2][:], ACT.Sigmoid, bias=pc[:, l, 0, BV:BV + 1]).then_inc(s["ac_sig"], 1)
                if i <= STEPS:
                    act_h(ac, i + 1)
                if i < STEPS:
                    ac.wait_ge(s["ac_sig"], 2 * (i + 1))
                    if i >= 3:
                        ac.wait_ge(s["pe_o"], 2 * (i - 2))
                    ac.copy(sghi[:, i % 3], sig[:]).then_inc(s["ac_sghi"], 1)
                if i < STEPS:
                    ac.wait_ge(s["dv_conv"], 6 * (i + 1))
                    if i >= 2:
                        ac.wait_ge(s["pe_c"], 2 * (i - 1))
                    ac.copy(uchi[:, p], uc[:, p]).then_inc(s["ac_uchi"], 1)
                if c == 3 and l + 1 < LAYERS:
                    act_w(ac, "u", l + 1)
                if 2 <= i:
                    k = i - 2
                    ac.wait_ge(s["pe_y"], k + 1)
                    if k >= 1:
                        ac.wait_ge(s["dv_x"], TPC * k)
                    ac.copy(y[:], TP[0][:, 0:TPC]).then_inc(s["ac_y"], 1)
                if 1 <= i <= STEPS:
                    k = i - 1
                    for h in range(H2):
                        ac.wait_ge(s["pe_bz"] if h else s["pe_z"], k + 1)
                        if h == 0 and k >= 1:
                            ac.wait_ge(s["dv_scan"], k)
                        r = slice(P - PH[h], P)
                        ac.activation(dec[0:PH[h], h, :, 1:], MM[0 if h else 3][r, :].rearrange("p (b s) -> p b s", b=BPC),
                                      ACT.Sigmoid, bias=pc[r, k // NC, h, BD:BD + 1], scale=-1.0).then_inc(s["ac_dec"], 1)
                act_ln(ac, i + 2)
                if i == 0:
                    ac.wait_ge(s["pe_ph"], 1)
                    for h in range(H2):
                        ac.copy(phihi[:, h, :], MM[3][:, h * NS:(h + 1) * NS]).then_inc(s["ac_phi"], 1)
                if 0 < l < LAYERS:
                    if c == 0:
                        act_w(ac, "z", l)
                    if c == 1:
                        act_w(ac, "o", l)

            act_att(ac)

        def dve_ln(dv, j):
            c = j % NC
            for t in range(TPC):
                if j >= NC:
                    dv.wait_ge(s["dv_x"], TPC * (j - NC) + t + 1)
                dv.bn_stats(st[:, t, :], X[:, TPC * c + t, :]).then_inc(s["dv_st"], 1)
            for t in range(TPC):
                dv.wait_ge(s["dv_st"], TPC * j + t + 1)
                if j >= 1:
                    dv.wait_ge(s["pl_rs"], j)
                dv.bn_aggr(mv[:, t, :], st[:, t, :]).then_inc(s["dv_mv"], 1)

        def dve_nb(dv, j):
            dv.wait_ge(s["dv_mv"], TPC * (j + 1))
            if j >= 2:
                dv.wait_ge(s["ac_xn"], TPC * (j - 1))
            dv.wait_ge(s["pl_rs"], j + 1)
            dv.scalar_tensor_tensor(out=nb[:, j % 2, :], in0=mv[:, :, 0], scalar=-1.0, in1=rs[:, j % 2, :],
                                    op0=ALU.mult, op1=ALU.mult).then_inc(s["dv_nb"], 1)

        def dve_hlo(dv, j):
            dv.wait_ge(s["ac_hhi"], j + 1)
            if j >= 2:
                free_h(dv, j)
            split(dv, "dv_hlo", hhi[:, j % 2], hlo[:, j % 2], hf)

        count = [0]

        def link(ins):
            ins.then_inc(s["dv_ch"], 1)
            count[0] += 1
            nc.vector.wait_ge(s["dv_ch"], count[0])

        def start(ins):
            ins.then_inc(s["dv_ch"], 1)
            count[0] += 1

        def wait_all(dv):
            dv.wait_ge(s["dv_ch"], count[0])

        def dve_att(dv):
            dv.wait_ge(s["pl_ac"], 6)

            def keys(a):
                m = 2 * (a % 2)
                dv.wait_ge(s["ac_f"], 2 * (a + 1))
                start(dv.tensor_scalar(fg[0:MQ], fg[0:MQ], FMIN, None, ALU.max))
                start(dv.tensor_scalar(fg[MQ:P], fg[MQ:P], 1.0, 1.0 / FMIN, ALU.add, ALU.min))
                dv.wait_ge(s["ac_eq"], a + 1)
                link(dv.tensor_scalar(eqk[:], eqk[:], 1.0, None, ALU.min))
                if a:
                    dv.wait_ge(s["dv_qp"], a)
                    dv.wait_ge(s["dv_kp"], a)
                dv.scalar_tensor_tensor(out=qk[:], in0=MM[m][:], scalar=0.0, in1=eqk[:], op0=ALU.max,
                                        op1=ALU.add).then_inc(s["dv_qk"], 1)
                for r, op in ((MQ, ALU.min), (0, ALU.max)):
                    for b in range(BPC):
                        w = slice(b * S, (b + 1) * S)
                        dv.tensor_tensor_scan(cum[r:r + MQ, w], fg[r:r + MQ, w], lim[r:r + MQ, :], 1.0,
                                              ALU.mult, op).then_inc(s["dv_cum"], 1)
                dv.wait_ge(s["dv_cum"], 4 * (a + 1))
                dv.wait_ge(s["dv_qk"], a + 1)
                if a >= 2:
                    dv.wait_ge(s["pe_at"], 2 * (a - 1))
                dv.scalar_tensor_tensor(out=qp[MQ:P, a % 2, :], in0=qk[0:MQ], scalar=MQ ** -0.5, in1=cum[0:MQ],
                                        op0=ALU.mult, op1=ALU.mult).then_inc(s["dv_qp"], 1)
                dv.tensor_tensor(kp[MQ:P, a % 2, :], qk[MQ:P], cum[MQ:P], ALU.mult).then_inc(s["dv_kp"], 1)

            def norm(a):
                if a:
                    dv.wait_ge(s["dv_nb2"], a)
                for b in range(2):
                    dv.wait_ge(s["pe_num"], 2 * a + b + 1)
                    ds = OP[b][:, 0:2 * (D + 2)].rearrange("p (t w) -> p t w", t=2)[:, :, D]
                    start(dv.tensor_scalar(den[:, 2 * b:2 * b + 2], ds, 1e-6, None, ALU.add))
                    for t in range(2):
                        start(dv.bn_stats(st2[:, 2 * b + t, :], OP[b][:, t * (D + 2):t * (D + 2) + D]))
                wait_all(dv)
                start(dv.reciprocal(rden[:], den[:]))
                for t in range(TPC):
                    start(dv.bn_aggr(mv2[:, t, :], st2[:, t, :]))
                wait_all(dv)
                link(dv.tensor_tensor(rr[:], rden[:], rden[:], ALU.mult))
                link(dv.tensor_tensor(rr[:], rr[:], mv2[:, :, 1], ALU.mult))
                if a:
                    dv.wait_ge(s["pl_rs2"], a)
                dv.tensor_scalar(v2[:], rr[:], EPS, None, ALU.add).then_inc(s["dv_v2"], 1)
                dv.wait_ge(s["pl_rs2"], a + 1)
                if a:
                    dv.wait_ge(s["ac_xn2"], TPC * a)
                dv.tensor_tensor(s2[:], rden[:], rs2[:], ALU.mult).then_inc(s["dv_s2"], 1)
                dv.wait_ge(s["dv_s2"], a + 1)
                dv.scalar_tensor_tensor(out=nb2[:], in0=mv2[:, :, 0], scalar=-1.0, in1=s2[:], op0=ALU.mult,
                                        op1=ALU.mult).then_inc(s["dv_nb2"], 1)

            def rows_next(a):
                for t in range(TPC):
                    dv.wait_ge(s["dv_xa"], 2 * a + t // 2 + 1)
                    start(dv.bn_stats(st[:, t, :], X[:, TPC * a + t, :]))
                wait_all(dv)
                for t in range(TPC):
                    start(dv.bn_aggr(mvx[:, TPC * a + t, :], st[:, t, :]))
                wait_all(dv)
                dv.tensor_scalar(lnx[:, 0, TPC * a:TPC * (a + 1)], mvx[:, TPC * a:TPC * (a + 1), 1], 1.0 + EL2 / D,
                                 EPS * EL2 / D, ALU.mult, ALU.add).then_inc(s["dv_lx"], 1)

            keys(0)
            for a in range(NC + 1):
                if a < NC:
                    for b in range(BPC):
                        dv.wait_ge(s["pe_at"], 2 * a + b + 1)
                        if a:
                            dv.wait_ge(s["pe_num"], 2 * a)
                        dv.tensor_tensor(ast[:, b], MM[2 * (a % 2) + b][:, 0:3 * P].rearrange("p (k l) -> p k l", k=3), mask[:],
                                         ALU.mult).then_inc(s["dv_as"], 1)
                if a + 1 < NC:
                    keys(a + 1)
                if a >= 1:
                    dv.wait_ge(s["ac_hhi2"], a)
                    if a >= 2:
                        dv.wait_ge(s["pe_ao"], 2 * (a - 1))
                    split(dv, "dv_h2lo", h2hi, h2lo[:], h2f)
                if a + 2 < NC:
                    dve_hlo(dv, STEPS + 2 + a)
                if a < NC:
                    norm(a)
                if a >= 1:
                    dve_att_end(dv, a - 1)
                    rows_next(a - 1)

        def dve_att_end(dv, a):
            for t in range(2):
                dv.wait_ge(s["pe_ao"], 2 * a + t + 1)
                xx = X[:, TPC * a + 2 * t:TPC * a + 2 * t + 2, :]
                dv.tensor_tensor(xx, MM[2 * (a % 2) + t][:, 0:2 * D].rearrange("p (t d) -> p t d", t=2), xx, ALU.add).then_inc(s["dv_xa"], 1)

        @block.vector
        def _(dv):
            dv.wait_ge(s["ld_tok"], 16)
            dv.tensor_scalar(tokn[:], tok[:], 0.0, float(V), ALU.is_lt, ALU.mult).then_inc(s["dv_idx"], 1)
            dv.wait_ge(s["dv_idx"], 1)
            dv.tensor_tensor(tokn[:], tok[:], tokn[:], ALU.add).then_inc(s["dv_idx"], 1)
            dv.wait_ge(s["dv_idx"], 2)
            dv.tensor_scalar(tok[:], tokn[:], 0.0, float(V - 1), ALU.max, ALU.min).then_inc(s["dv_idx"], 2)
            for z in (hf[DB:P, 1, :], uc[DB:P, 0, 1, :], uc[DB:P, 1, 1, :], sig[DB:P, 1, :], dec[DB:P, 1, :, 1:],
                      inp[DB:P, 1, :, 1:], h2f[DB:P, 1, :], dec[:, 0, :, 0:1], dec[:, 1, :, 0:1], inp[:, 0, :, 0:1],
                      inp[:, 1, :, 0:1]):
                dv.memset(z, 0.0).then_inc(s["dv_zero"], 1)
            dv.wait_ge(s["ld_c"], 16)
            for l in range(LAYERS):
                link(dv.tensor_scalar(pc[:, l, :, BD:BD + 1], pc[:, l, :, BD:BD + 1], -1.0, None, ALU.mult))
            for k in "uzo":
                low_w(dv, k, 0)
            dv.wait_ge(s["ac_aw"], 1)
            dv.tensor_tensor(awlo[:], awst[:], awhi[:].bitcast(F32), ALU.subtract).then_inc(s["dv_aw"], 1)
            dv.wait_ge(s["ld_f"], 96)
            dv.tensor_scalar(abf[MQ:P], abf[MQ:P], -1.0, None, ALU.mult).then_inc(s["dv_abf"], 1)

            def place(c):
                dv.wait_ge(s[f"gat{c}"], 16 * TPC)
                xx = X[:, TPC * c:TPC * (c + 1), :].rearrange("p (b t) d -> p b (t d)", b=BPC)
                dv.tensor_tensor(xx, xx, pos[:].rearrange("p t d -> p (t d)").unsqueeze(1).broadcast_to([P, BPC, S // P * D]),
                                 ALU.add).then_inc(s["init_x"], 1)

            for c in range(2):
                place(c)
                dv.wait_ge(s["init_x"], c + 1)
                dve_ln(dv, c)
                dve_nb(dv, c)
            dv.tensor_tensor_reduce(squares[:], slots1[:, 0:D], slots1[:, 0:D], 1.0, EL2, ALU.mult, ALU.add, rz1[:, 0:1]).then_inc(s["dv_phi"], 1)
            dve_hlo(dv, 0)
            for c in range(2, NC):
                place(c)
            dv.memset(lim[0:64, :], EXP_M20).then_inc(s["pl_ac"], 1)
            dv.memset(lim[64:P, :], EXP_20).then_inc(s["pl_ac"], 1)
            dv.memset(qp[0:64], 0.0).then_inc(s["pl_ac"], 1)
            dv.memset(kp[0:64], 0.0).then_inc(s["pl_ac"], 1)
            dv.memset(vs[:, :, :, D:D + 2], 1.0).then_inc(s["pl_ac"], 1)
            dv.wait_ge(s["init_x"], NC)
            dv.wait_ge(s["pl_f"], 6)
            dv.tensor_scalar(slots1[:], slots1[:], rz1[:, 1:2], RD, ALU.mult, ALU.mult).then_inc(s["dv_phi"], 1)
            for i in range(STEPS + 2):
                l, c, p = i // NC, i % NC, i % 2
                if i < STEPS:
                    for k in range(1, KC):
                        for h in range(H2):
                            if k == 1:
                                dv.wait_ge(s["ac_tap"], 2 * i + h + 1)
                            else:
                                dv.wait_ge(s["dv_conv"], 6 * i + 2 * (k - 2) + h + 1)
                            r = slice(0, PH[h])
                            o = uc[r, p, h, :].rearrange("p (b s) -> p b s", b=BPC)
                            dv.scalar_tensor_tensor(out=o, in0=u[r, p, h, :, k:k + S], scalar=pc[r, l, h, W1 + k - 1:W1 + k],
                                                    in1=o, op0=ALU.mult, op1=ALU.add).then_inc(s["dv_conv"], 1)
                if i <= STEPS:
                    dve_hlo(dv, i + 1)
                if 2 <= i:
                    k = i - 2
                    kc = k % NC
                    dv.wait_ge(s["ac_y"], k + 1)
                    dv.wait_ge(s["bou"], k + 1)
                    for t in range(TPC):
                        dv.wait_ge(s["pe_o"], 2 * k + t // 2 + 1)
                        xx = X[:, TPC * kc + t, :]
                        dv.scalar_tensor_tensor(out=xx, in0=OP[t // 2][:, (t % 2) * D:(t % 2 + 1) * D], scalar=y[:, t:t + 1],
                                                in1=xx, op0=ALU.mult, op1=ALU.add).then_inc(s["dv_x"], 1)
                dve_ln(dv, i + 2)
                if c == 3 and l + 1 < LAYERS:
                    low_w(dv, "u", l + 1)
                if 1 <= i <= STEPS:
                    k = i - 1
                    if k == 0:
                        dv.wait_ge(s["dv_zero"], 11)
                    for h in (1, 0):
                        dv.wait_ge(s["pe_bz"] if h else s["pe_b"], k + 1)
                        if h and k:
                            dv.wait_ge(s["dv_scan"], k)
                        r = slice(0, PH[h])
                        dv.scalar_tensor_tensor(out=inp[r, h, :, 1:], in0=MM[0 if h else 1][r, :].rearrange("p (b s) -> p b s", b=BPC),
                                                scalar=pc[r, k // NC, h, BBM:BBM + 1],
                                                in1=uc[r, k % 2, h, :].rearrange("p (b s) -> p b s", b=BPC),
                                                op0=ALU.add, op1=ALU.mult).then_inc(s["dv_inp"], 1)
                    dve_nb(dv, i + 2)
                    dv.wait_ge(s["dv_inp"], 2 * (k + 1))
                    dv.wait_ge(s["ac_dec"], 2 * (k + 1))
                    if k:
                        dv.wait_ge(s["dv_hc"], 2 * k)
                    flat = lambda a: a[:].rearrange("p h b s -> p (h b s)")
                    dv.tensor_tensor_scan(flat(hs), flat(dec), flat(inp), 0.0, ALU.mult, ALU.add).then_inc(s["dv_scan"], 1)
                    dv.wait_ge(s["dv_scan"], k + 1)
                    if k >= 2:
                        dv.wait_ge(s["pe_y"], k - 1)
                    for h in range(H2):
                        dv.wait_ge(s["pe_c"], 2 * k + h + 1)
                        r = slice(0, PH[h])
                        dv.scalar_tensor_tensor(out=hc[r, k % 2, h, :].rearrange("p (b s) -> p b s", b=BPC),
                                                in0=MM[2 + h][r, :].rearrange("p (b s) -> p b s", b=BPC),
                                                scalar=pc[r, k // NC, h, BCM:BCM + 1], in1=hs[r, h, :, 1:],
                                                op0=ALU.add, op1=ALU.mult).then_inc(s["dv_hc"], 1)
                if i == 0 or i == STEPS + 1:
                    dve_nb(dv, i + 2)
                if i == 0:
                    dv.wait_ge(s["ac_phi"], 2)
                    for h in range(H2):
                        dv.tensor_tensor(philo[:, h, :], MM[3][:, h * NS:(h + 1) * NS], phihi[:, h, :].bitcast(F32), ALU.subtract
                                         ).then_inc(s["dv_phi"], 1)

            dve_att(dv)

        def pe_tr(pe, j):
            pe.wait_ge(s["ac_xn"], TPC * (j + 1))
            if j >= 1:
                pe.wait_ge(s["ac_h"], 2 * j)
            if j >= 4:
                pe.wait_ge(s["ac_y"], min(j - 3, STEPS))
            if j >= STEPS + 3:
                pe.wait_ge(s["ac_h2"], 2 * (j - STEPS - 2))
            for h in range(H2):
                for t in range(TPC):
                    r = pe.transpose(TP[h][0:PH[h], t * P:(t + 1) * P], xn[:, j % 2, t, h * P:h * P + PH[h]], ident[:])
                r.then_inc(s["pe_t"], 1)

        @block.tensor
        def _(pe):
            pe.wait_ge(s["ident_ok"], 2)
            pe.wait_ge(s["pads"], 3)
            pe_tr(pe, 0)
            for i in range(STEPS + 2):
                l, c, p = i // NC, i % NC, i % 2
                if i < STEPS:
                    pe.wait_ge(s["dv_hlo"], 2 * (i + 1))
                    pe.wait_ge(s["lo_wu"], l + 1)
                    x = (hhi[:, p], hlo[:, p], ALL)
                    if i >= 2:
                        pe.wait_ge(s["ac_dec"], 2 * (i - 1))
                        pe.wait_ge(s["dv_inp"], 2 * (i - 1))
                    five(pe, MM[0][:], whi["u"], wlo["u"], UA, *x).then_inc(s["pe_u"], 1)
                    five(pe, MM[1][:], whi["u"], wlo["u"], UV, *x).then_inc(s["pe_u"], 1)
                    if i >= 2:
                        pe.wait_ge(s["dv_hc"], 2 * (i - 2) + 1)
                    five(pe, MM[2][:], whi["u"], wlo["u"], VA, *x).then_inc(s["pe_v"], 1)
                if i <= STEPS:
                    pe_tr(pe, i + 1)
                if i == 0:
                    pe.wait_ge(s["dv_phi"], 2)
                    for h in range(H2):
                        r = pe.transpose(MM[3][:, h * NS:(h + 1) * NS], slots1[:, h * P:(h + 1) * P], ident[:])
                    r.then_inc(s["pe_ph"], 1)
                if 2 <= i:
                    k = i - 2
                    pe.wait_ge(s["pl_sglo"], 2 * (k + 1))
                    pe.wait_ge(s["lo_wo"], k // NC + 1)
                    for t in range(TPC):
                        if k >= 1 and t % 2 == 0:
                            pe.wait_ge(s["dv_x"], TPC * (k - 1) + t + 2)
                        r = five(pe, OP[t // 2][:, (t % 2) * D:(t % 2 + 1) * D], whi["o"], wlo["o"], slice(0, D),
                                 sghi[:, k % 3], sglo[:, k % 3], slice(t * P, (t + 1) * P), rows=True)
                        if t % 2:
                            r.then_inc(s["pe_o"], 1)
                    pe.wait_ge(s["dv_hc"], 2 * (k + 1))
                    pe.wait_ge(s["ac_h"], 2 * min(i + 2, STEPS + 2))
                    if k >= 1:
                        pe.wait_ge(s["ac_y"], k)
                    for t in range(TPC):
                        for h in range(H2):
                            r = pe.matmul(TP[0][:, t:t + 1], hc[0:PH[h], k % 2, h, t * P:(t + 1) * P], ones[0:PH[h], 0:1],
                                          start=(h == 0), stop=(h == 1))
                    r.then_inc(s["pe_y"], 1)
                if 1 <= i <= STEPS:
                    k = i - 1
                    pe.wait_ge(s["pl_uclo"], 2 * (k + 1))
                    pe.wait_ge(s["lo_wz"], k // NC + 1)
                    x = (uchi[:, k % 2], uclo[:, k % 2], ALL)
                    z = whi["z"], wlo["z"]
                    if i == 1:
                        pe.wait_ge(s["dv_phi"], 4)
                    if k >= 1:
                        pe.wait_ge(s["dv_hc"], 2 * k)
                    five(pe, MM[3][:], *z, ZA, *x).then_inc(s["pe_z"], 1)
                    if i < STEPS:
                        pe.wait_ge(s["ac_u"], 2 * i + 1)
                    five(pe, MM[0][:], *z, BZ, *x).then_inc(s["pe_bz"], 1)
                    if i < STEPS:
                        pe.wait_ge(s["ac_sig"], 2 * i + 1)
                    five(pe, MM[1][:], *z, BA, *x).then_inc(s["pe_b"], 1)
                    if i < STEPS:
                        pe.wait_ge(s["ac_sig"], 2 * i + 2)
                    five(pe, MM[2][:], *z, CA, *x).then_inc(s["pe_c"], 1)
                    pe.wait_ge(s["ac_dec"], 2 * k + 1)
                    five(pe, MM[3][0:DB, :], *z, CB, *x).then_inc(s["pe_c"], 1)

            def keys(a):
                j = STEPS + a
                m = 2 * (a % 2)
                x = (hhi[:, j % 2], hlo[:, j % 2], ALL)
                pe.wait_ge(s["dv_hlo"], 2 * (j + 1))
                if a == 0:
                    pe.wait_ge(s["dv_aw"], 1)
                if a < 2:
                    pe.wait_ge(s["dv_hc"], 2 * STEPS)
                    pe.wait_ge(s["ac_dec"], 2 * STEPS)
                else:
                    pe.wait_ge(s["dv_as"], 2 * (a - 1))
                five(pe, MM[m + 1][:], awhi, awlo, slice(P, 2 * P), *x).then_inc(s["pe_f"], 1)
                five(pe, MM[m][:], awhi, awlo, slice(0, P), *x).then_inc(s["pe_f"], 1)

            def values(a):
                j = STEPS + a
                if a == 0:
                    pe.wait_ge(s["dv_x"], TPC * STEPS)
                elif a == 1:
                    pe.wait_ge(s["ac_vs"], 2)
                else:
                    pe.wait_ge(s["ac_xn2"], TPC * (a - 1))
                for t in range(TPC):
                    r = five(pe, OP[t // 2][:, (t % 2) * D:(t % 2 + 1) * D], awhi, awlo, slice(2 * P, 2 * P + D),
                             hhi[:, j % 2], hlo[:, j % 2], slice(t * P, (t + 1) * P), rows=True)
                    if t % 2:
                        r.then_inc(s["pe_av"], 1)

            def out_proj(a):
                pe.wait_ge(s["dv_h2lo"], 2 * (a + 1))
                pe.wait_ge(s["dv_qk"], min(a + 3, NC))
                pe.wait_ge(s["dv_as"], 2 * (a + 1))
                for t in range(TPC):
                    r = five(pe, MM[2 * (a % 2) + t // 2][:, (t % 2) * D:(t % 2 + 1) * D], awhi, awlo,
                             slice(2 * P + D, 2 * P + 2 * D), h2hi, h2lo, slice(t * P, (t + 1) * P), rows=True)
                    if t % 2:
                        r.then_inc(s["pe_ao"], 1)

            keys(0)
            values(0)
            for a in range(NC + 1):
                m = 2 * (a % 2)
                if a + 1 < NC:
                    keys(a + 1)
                if a < NC:
                    if a >= 2:
                        pe.wait_ge(s["dv_xa"], 2 * (a - 1))
                    pe.wait_ge(s["dv_qp"], a + 1)
                    pe.wait_ge(s["dv_kp"], a + 1)
                    for b in range(BPC):
                        q = lambda l0, l1: qp[:, a % 2, b * S + l0:b * S + l1]
                        k = lambda l0, l1: kp[:, a % 2, b * S + l0:b * S + l1]
                        pe.matmul(MM[m + b][:, 0:P], k(0, P), q(0, P), start=True, stop=True)
                        pe.matmul(MM[m + b][:, 2 * P:3 * P], k(0, P), q(P, S), start=True, stop=True)
                        pe.matmul(MM[m + b][:, P:2 * P], k(P, S), q(P, S), start=True, stop=True).then_inc(s["pe_at"], 1)
                if a + 1 < NC:
                    values(a + 1)
                if a >= 1:
                    pe.wait_ge(s["ac_xn2"], TPC * a)
                    pe.wait_ge(s["ac_h"], 2 * min(NC + STEPS, STEPS + 2 + a))
                    if a >= 2:
                        pe.wait_ge(s["ac_h2"], 2 * (a - 1))
                    for h in range(H2):
                        for t in range(TPC):
                            r = pe.transpose(TP[h][0:PH[h], t * P:(t + 1) * P], xn2[:, t, h * P:h * P + PH[h]], ident[:])
                        r.then_inc(s["pe_t2"], 1)
                if a + 2 < NC:
                    pe_tr(pe, STEPS + 2 + a)
                if a < NC:
                    pe.wait_ge(s["ac_vs"], 2 * min(a + 2, NC))
                    if a:
                        pe.wait_ge(s["ac_xn2"], TPC * a)
                    for b in range(BPC):
                        pe.wait_ge(s["dv_as"], 2 * a + b + 1)
                        v = lambda t: vs[:, a % 2, 2 * b + t, 0:D + 1]
                        pe.matmul(OP[b][:, 0:D + 1], ast[:, b, 0, :], v(0), start=True, stop=True)
                        pe.matmul(OP[b][:, D + 2:2 * D + 3], ast[:, b, 2, :], v(0), start=True, stop=False)
                        pe.matmul(OP[b][:, D + 2:2 * D + 3], ast[:, b, 1, :], v(1), start=False, stop=True).then_inc(s["pe_num"], 1)
                if a >= 1:
                    out_proj(a - 1)

    return list(s.values())


def mixture(nc, A, out, keep):
    X, ident, g2, gin, iavg, mhalf, rz1 = (keep[k] for k in ("X", "ident", "g2", "gin", "iavg", "mhalf", "rz1"))
    xn, hhi, hlo, phihi, philo = (keep[k] for k in ("xn", "hhi", "hlo", "phihi", "philo"))
    mvx, lnx = keep["mvx"], keep["lnx"]
    MM, TP, OP = keep["MM"], keep["TP"], keep["OP"]
    with ExitStack() as ctx:
        at = [keep["overlay"]]
        s = {"st_out": keep["st_out"]}
        for n in """ld_ws0 ld_ws1 ld_b1 ld_u0 ld_u1 ld_u2 ld_u3 ld_d0 ld_d1 ld_d2 ld_d3 st_o0 st_o1
                 f_nb f_xn f_xg f_tr f_hhi f_hlo f_lt f_l f_mx f_mxt f_e f_d f_etr f_dtr f_e1t f_dt f_z
                 f_sl f_ssq f_v2 f_pow2 f_yn f_yt f_yte f_me g_se g_ssq g_v g_pow g_s g_n g_tr g_ev blk_ok
                 h_l2 h_l2m h_tr h_mxc h_mxd h_c h_d h_cn h_dn h_dtr h_d2 h_sl h_sle h_w h_wt
                 x_up x_gl x_act x_down x_o y_o y_x f_ch""".split():
            s[n] = ctx.enter_context(nc.semaphore(n))

        def sb(name, shape, dt=F32):
            size = 4
            for n in shape[1:]:
                size *= n
            t = nc.alloc_sbuf_tensor_at(name, shape, dt, offset=at[0])
            at[0] += (size + 31) // 32 * 32
            return t

        YN = sb("YN", [P, NG, D])
        ynT = sb("ynT", [DH, NG, H2, NS])
        meT_at = at[0]
        meT = sb("meT", [DH, H2, E1N, NG, MN])
        E1T = sb("E1T", [NS, T])
        sl2T = sb("sl2T", [DH, H2, KE, MN, NG])
        se2T_at = at[0]
        se2T = sb("se2T", [DH, H2, NG, E1N, E2N, MN])
        work = at[0]
        xg = sb("xg", [P, 2, TPC, D])
        D1 = sb("D1", [P, CH])
        E1 = sb("E1", [P, TPC, NS])
        DT = sb("DT", [P, TPC, 2, NS])
        sq = sb("sq", [P, D])
        sm1 = sb("sm1", [P, 2, 10, 8])
        wsl = sb("wsl", [DH, 2, H2, E2N * D])
        assert at[0] <= 229368
        at[0] = work
        se2n = sb("se2n", [P, 2, E2N, D])
        sq2 = sb("sq2", [P, D])
        sm2 = sb("sm2", [P, 2, 3, E2N])
        at[0] = work
        blk = sb("blk", [P, NS])
        L2 = sb("L2", [P, 2, GQ, NS])
        C2 = sb("C2", [P, 2, GQ, NS])
        D2T = sb("D2T", [P, GQ, NS])
        D2n = sb("D2n", [P, GQ, NS])
        D2 = sb("D2", [P, 2, GQ, NS])
        sm3 = sb("sm3", [P, 8, GQ])
        w1_at3 = at[0]
        NW = 4
        w1b, w2b = [], []
        for n, o in enumerate((keep["hhi_at"], keep["hf_at"], meT_at, w1_at3)):
            at[0] = o
            w1b.append(sb(f"w1b{n}", [DH, H2, 2 * HID]))
        assert at[0] <= 229368
        for n, o in enumerate((keep["xn_at"], keep["xn_at"] + HID // P * D * 4, keep["slots1_at"])):
            at[0] = o
            w2b.append(sb(f"w2b{n}", [P, HID // P, D]))
        at[0] = keep["overlay"]
        oall = sb("oall", [NS, NG, D])
        assert at[0] <= meT_at
        at[0] = se2T_at
        w2b.append(sb("w2b3", [P, HID // P, D]))
        b2b = [sb(f"b2b{n}", [P, D]) for n in range(NW)]
        b1b = sb("b1b", [P, KE, 2 * HID // P])
        gl = sb("gl", [P, 2, HID // P, P])
        ac2 = sb("ac2", [P, 2, HID // P, P])
        osb = sb("osb", [P, 2, D])

        block = ctx.enter_context(nc.Block())
        NQ = NG // GQ
        SL = (OP[0], OP[1], MM[3], MM[2])
        YT = (TP[0], TP[1], OP[0], OP[1])
        Z, MXD, NMXD, V2, P2, RZ, ZD, YS, SS, MXE = range(10)

        def five(pe, dst, whi, wlo, c, xhi, xlo, t, rows=False):
            parts = ((whi[:, 0, c], xhi[:, 0, t]), (whi[:, 0, c], xlo[:, t]), (wlo[:, 0, c], xhi[:, 0, t]),
                     (whi[:, 1, c], xhi[:, 1, t]), (wlo[:, 1, c], xhi[:, 1, t]))
            for n, (w, x) in enumerate(parts):
                r = pe.matmul(dst, x if rows else w, w if rows else x, start=(n == 0), stop=(n == 4))
            return r

        def f3_done(e):
            e.wait_ge(s["h_sle"], 2 * NQ)
            e.wait_ge(s["h_wt"], NQ)
            e.wait_ge(s["h_sl"], NQ)

        def experts(e, body):
            for n in range(NW):
                body(n, n, -1)
            with e.Fori(1, KE // NW - 1) as i:
                for n in range(NW):
                    body(i * NW + n, n, 0)
            for n in range(NW):
                body(KE - NW + n, n, 1)

        @block.sync
        def _(sp):
            for e in range(E1N):
                if e >= 2:
                    sp.wait_ge(s["g_se"], e - 1)
                sp.dma_start(wsl[:, e % 2], A["wsl"][e]).then_inc(s[f"ld_ws{e % 2}"], 16)
            sp.wait_ge(s["f_me"], NG)
            sp.wait_ge(s["g_se"], E1N)
            sp.wait_ge(s["g_tr"], 2 * E1N)
            for n in range(NW):
                sp.dma_start(w1b[n][:], A["w1"][n]).then_inc(s[f"ld_u{n}"], 16)
                if n < NW - 1:
                    sp.dma_start(w2b[n][:], A["w2"][n]).then_inc(s[f"ld_d{n}"], 16)
            f3_done(sp)
            sp.dma_start(w2b[NW - 1][:], A["w2"][NW - 1]).then_inc(s[f"ld_d{NW - 1}"], 16)
            sp.dma_start(b1b[:], A["b1"]).then_inc(s["ld_b1"], 16)
            for n in range(NW):
                sp.dma_start(b2b[n][:], A["b2"][n:n + 1, :].partition_broadcast(P).rearrange("p o d -> p (o d)")
                             ).then_inc(s[f"ld_d{n}"], 16)
            with sp.Fori(1, KE // NW) as i:
                for n in range(NW):
                    k = i * NW + n
                    sp.wait_ge(s["x_up"], k + (1 - NW))
                    sp.dma_start(w1b[n][:], A["w1"][bass.ds(k, 1)].rearrange("k p h f -> (k p) h f")
                                 ).then_inc(s[f"ld_u{n}"], 16)
                    sp.wait_ge(s["x_o"], k + (1 - NW))
                    sp.dma_start(w2b[n][:], A["w2"][bass.ds(k, 1)].rearrange("k p c d -> (k p) c d")
                                 ).then_inc(s[f"ld_d{n}"], 16)
                    sp.dma_start(b2b[n][:], A["b2"][bass.ds(k, 1), :].partition_broadcast(P).rearrange("p o d -> p (o d)")
                                 ).then_inc(s[f"ld_d{n}"], 16)
            for t in range(0, NT, 2):
                sp.wait_ge(s["y_x"], t + 2)
                sp.dma_start(out[:, t:t + 2, :], X[:, t:t + 2, :]).then_inc(s["st_out"], 16)
            sp.wait_ge(s["st_out"], 8 * NT)

        @block.gpsimd
        def _(pl):

            def gain(a):
                for t in range(TPC):
                    pl.wait_ge(s["f_xn"], TPC * a + t + 1)
                    if a >= 2 and t == 0:
                        pl.wait_ge(s["f_sl"], TPC * (a - 1))
                    pl.tensor_tensor(xg[:, a % 2, t, :], xn[:, a % 2, t, :], gin[:], ALU.mult).then_inc(s["f_xg"], 1)

            gain(0)
            gain(1)
            for a in range(NC):
                for c in range(2):
                    cs = slice(4 * c, 4 * c + 4)
                    pl.wait_ge(s["f_v2"], 2 * a + c + 1)
                    pl.tensor_tensor(sm1[:, a % 2, P2, cs], sm1[:, a % 2, V2, cs], mhalf[:, 0:4], ALU.pow).then_inc(s["f_pow2"], 1)
                if a + 2 < NC:
                    gain(a + 2)
            for e in range(E1N):
                pl.wait_ge(s["g_v"], e + 1)
                if e >= 2:
                    pl.wait_ge(s["g_n"], E2N * (e - 1))
                pl.tensor_tensor(sm2[:, e % 2, 1], sm2[:, e % 2, 0], mhalf[:, 0:E2N], ALU.pow).then_inc(s["g_pow"], 1)
            pl.wait_ge(s["g_tr"], 2 * E1N)
            pl.memset(blk[:], 0.0).then_inc(s["blk_ok"], 1)
            bv = blk[:].rearrange("p (e n) -> p e n", e=E1N)
            pl.wait_ge(s["blk_ok"], 1)
            pl.affine_select(out=bv, in_=bv, compare_op=ALU.is_ge, fill=BIG, base=0,
                             pattern=[[-S1N, E1N], [0, S1N]], channel_multiplier=1).then_inc(s["blk_ok"], 1)
            pl.wait_ge(s["blk_ok"], 2)
            pl.affine_select(out=bv, in_=bv, compare_op=ALU.is_ge, fill=BIG, base=S1N - 1,
                             pattern=[[S1N, E1N], [0, S1N]], channel_multiplier=-1).then_inc(s["blk_ok"], 1)
            f3_done(pl)
            for k in range(KE):
                pl.wait_ge(s["x_o"], k + 1)
                pl.dma_start(oall[MN * k:MN * (k + 1)], osb[:, k % 2, :]).then_inc(s[f"st_o{k % 2}"], 16)

        @block.scalar
        def _(ac):
            def rows(a):
                if a == 0:
                    ac.wait_ge(s["f_nb"], 1)
                if a >= 2:
                    ac.wait_ge(s["f_xg"], TPC * (a - 1))
                for t in range(TPC):
                    n = TPC * a + t
                    ac.activation(xn[:, a % 2, t, :], X[:, n, :], ACT.Identity, bias=lnx[:, 2, n:n + 1],
                                  scale=lnx[:, 1, n:n + 1]).then_inc(s["f_xn"], 1)

            def high(a):
                for h in range(H2):
                    ac.wait_ge(s["f_tr"], 2 * a + h + 1)
                    if a >= 2 and h == 0:
                        ac.wait_ge(s["f_l"], a - 1)
                    ac.copy(hhi[0:PH[h], a % 2, h, :], TP[h][0:PH[h], :]).then_inc(s["f_hhi"], 1)

            def disp(a):
                ac.wait_ge(s["f_mxt"], a + 1)
                if a:
                    ac.wait_ge(s["f_dtr"], a)
                for g in range(8):
                    ac.activation(D1[:, g * GT:(g + 1) * GT], MM[0][:, g * GT:(g + 1) * GT], ACT.Exp,
                                  bias=sm1[:, a % 2, NMXD, g:g + 1], accum_out=sm1[:, a % 2, ZD, g:g + 1]).then_inc(s["f_d"], 1)

            def comb(a):
                ac.wait_ge(s["f_mx"], a + 1)
                if a:
                    ac.wait_ge(s["f_etr"], a)
                for t in range(TPC):
                    ac.activation(E1[:, t, :], MM[1][:, t * NS:(t + 1) * NS], ACT.Exp, bias=sm1[:, a % 2, MXE, 4 + t:5 + t],
                                  accum_out=sm1[:, a % 2, Z, t:t + 1]).then_inc(s["f_e"], 1)

            rows(0)
            high(0)
            rows(1)
            disp(0)
            comb(0)
            for a in range(NC):
                if a + 1 < NC:
                    high(a + 1)
                ac.wait_ge(s["f_etr"], a + 1)
                ac.copy(E1T[:, a * CH:(a + 1) * CH], MM[2][:]).then_inc(s["f_e1t"], 1)
                if a + 2 < NC:
                    rows(a + 2)
                for t in range(TPC):
                    ac.wait_ge(s["f_sl"], TPC * a + t + 1)
                    if t == 0:
                        ac.wait_ge(s["f_z"], a + 1)
                    for g in range(2):
                        n = 2 * t + g
                        if TPC * a + t or g:
                            ac.wait_ge(s["f_ssq"], 8 * a + n)
                        ac.activation(sq[:], SL[t][:, g * D:(g + 1) * D], ACT.Square, scale=sm1[:, a % 2, RZ, n:n + 1],
                                      accum_out=sm1[:, a % 2, SS, n:n + 1]).then_inc(s["f_ssq"], 1)
                if a + 1 < NC:
                    disp(a + 1)
                for g in range(8):
                    ac.wait_ge(s["f_yt"], 8 * a + g + 1)
                    ac.copy(ynT[:, 8 * a + g], YT[g % 4][0:DH, 0:2 * (P + 32)].rearrange("p (h n) -> p h n", h=2)[:, :, 0:P]
                            ).then_inc(s["f_yte"], 1)
                    if g == 3 and a + 1 < NC:
                        comb(a + 1)

            for e in range(E1N + 1):
                if e < E1N:
                    m = 2 * (e % 2)
                    ac.wait_ge(s["g_se"], e + 1)
                    if e >= 2:
                        ac.wait_ge(s["g_v"], e - 1)
                    if e == 0:
                        ac.wait_ge(s["f_me"], NG)
                    for q in range(E2N):
                        if e or q:
                            ac.wait_ge(s["g_ssq"], E2N * e + q)
                        ac.activation(sq2[:], MM[m + q // 2][:, (q % 2) * D:(q % 2 + 1) * D], ACT.Square,
                                      accum_out=sm2[:, e % 2, 2, q:q + 1]).then_inc(s["g_ssq"], 1)
                if e:
                    ac.wait_ge(s["g_tr"], 2 * e - 1)
                    ac.copy(se2T[:, 0, :, e - 1].rearrange("p g q m -> p q g m"),
                            TP[0][0:DH, :].rearrange("p (q g m) -> p q g m", q=E2N, g=NG)).then_inc(s["g_ev"], 1)

            def exps(q, which):
                if which == 0:
                    ac.wait_ge(s["h_mxc"], q + 1)
                    if q:
                        ac.wait_ge(s["h_cn"], q)
                    if q >= 2:
                        ac.wait_ge(s["h_w"], q - 1)
                    for g in range(GQ):
                        ac.activation(C2[:, q % 2, g, :], L2[:, q % 2, g, :], ACT.Exp, bias=sm3[:, 1, g:g + 1],
                                      accum_out=sm3[:, 2, g:g + 1]).then_inc(s["h_c"], 1)
                else:
                    ac.wait_ge(s["h_mxd"], q + 1)
                    if q:
                        ac.wait_ge(s["h_dn"], q)
                    for g in range(GQ):
                        ac.activation(D2T[:, g, :], MM[1][:, g * NS:(g + 1) * NS], ACT.Exp, bias=sm3[:, 5, g:g + 1],
                                      accum_out=sm3[:, 6, g:g + 1]).then_inc(s["h_d"], 1)

            exps(0, 0)
            exps(0, 1)
            for q in range(NQ):
                ac.wait_ge(s["h_dtr"], q + 1)
                if q >= 2:
                    ac.wait_ge(s["h_sl"], q - 1)
                ac.copy(D2[:, q % 2], MM[2][:].rearrange("p (g n) -> p g n", g=GQ)).then_inc(s["h_d2"], 1)
                if q + 1 < NQ:
                    exps(q + 1, 0)
                ac.wait_ge(s["h_w"], q + 1)
                ac.copy(E1T[:, q * GQ * GT:(q + 1) * GQ * GT], MM[3][:, 0:GQ * GT]).then_inc(s["h_wt"], 1)
                if q + 1 < NQ:
                    exps(q + 1, 1)
                ac.wait_ge(s["h_sl"], q + 1)
                ac.copy(sl2T[:, 0, :, :, GQ * q:GQ * (q + 1)],
                        OP[0][0:DH, :].rearrange("p (g k m) -> p k m g", g=GQ, k=KE)).then_inc(s["h_sle"], 1)

            ac.wait_ge(s["ld_b1"], 16)

            def gate(k, n, edge):
                ac.wait_ge(s["x_up"], k + 1)
                if edge >= 0 or n >= 2:
                    ac.wait_ge(s["x_act"], (k - 1) * (HID // P))
                for c in range(HID // P):
                    ac.activation(gl[:, n % 2, c, :], MM[2 * (n % 2) + 1][:, c * P:(c + 1) * P], ACT.Gelu_apprx_tanh,
                                  bias=b1b[:, bass.ds(k, 1), HID // P + c]).then_inc(s["x_gl"], 1)

            experts(ac, gate)
        @block.vector
        def _(dv):
            count = [0]

            def link(ins):
                ins.then_inc(s["f_ch"], 1)
                count[0] += 1
                dv.wait_ge(s["f_ch"], count[0])

            dv.scalar_tensor_tensor(out=lnx[:, 2, :], in0=mvx[:, :, 0], scalar=-1.0, in1=lnx[:, 1, :],
                                    op0=ALU.mult, op1=ALU.mult).then_inc(s["f_nb"], 1)
            dv.memset(DT[0:GT, :, 1, :], 0.0).then_inc(s["f_dt"], 1)
            dv.memset(DT[GT:P, :, 0, :], 0.0).then_inc(s["f_dt"], 1)
            bc = lambda ap, n: ap.unsqueeze(2).broadcast_to([P, ap.shape[1], n])

            def low(a):
                for h in range(H2):
                    dv.wait_ge(s["f_hhi"], 2 * a + h + 1)
                    if a >= 2 and h == 0:
                        dv.wait_ge(s["f_l"], a - 1)
                    dv.tensor_tensor(hhi[P - DB:P, a % 2, 1, :] if h else hlo[:, a % 2, :], TP[h][0:PH[h], :],
                                     hhi[0:PH[h], a % 2, h, :].bitcast(F32), ALU.subtract).then_inc(s["f_hlo"], 1)

            def max_disp(a):
                p = a % 2
                dv.wait_ge(s["f_lt"], a + 1)
                if a >= 2:
                    dv.wait_ge(s["f_d"], 8 * (a - 1))
                link(dv.tensor_reduce(sm1[:, p, MXD, :], MM[0][:].rearrange("p (g t) -> p g t", g=8), AX.X, ALU.max))
                dv.tensor_scalar(sm1[:, p, NMXD, :], sm1[:, p, MXD, :], -1.0, None, ALU.mult).then_inc(s["f_mxt"], 1)

            def max_comb(a):
                p = a % 2
                dv.wait_ge(s["f_l"], a + 1)
                if a >= 2:
                    dv.wait_ge(s["f_e"], TPC * (a - 1))
                link(dv.tensor_reduce(sm1[:, p, MXE, 0:TPC], MM[1][:].rearrange("p (g t) -> p g t", g=TPC), AX.X, ALU.max))
                dv.tensor_scalar(sm1[:, p, MXE, 4:4 + TPC], sm1[:, p, MXE, 0:TPC], -1.0, None, ALU.mult).then_inc(s["f_mx"], 1)

            low(0)
            max_disp(0)
            max_comb(0)
            for a in range(NC):
                p = a % 2
                dv.wait_ge(s["f_e"], TPC * (a + 1))
                link(dv.reciprocal(rz1[:, TPC * a:TPC * (a + 1)], sm1[:, p, Z, 0:TPC]))
                dv.wait_ge(s["f_d"], 8 * (a + 1))
                if a >= 2:
                    dv.wait_ge(s["f_ssq"], 8 * (a - 1))
                dv.reciprocal(sm1[:, p, RZ, :], sm1[:, p, ZD, :]).then_inc(s["f_z"], 1)
                dv.wait_ge(s["f_dtr"], a + 1)
                if a:
                    dv.wait_ge(s["f_sl"], TPC * a)
                dv.tensor_copy(DT[0:GT, :, 0, :], MM[3][0:GT, :].rearrange("p (t n) -> p t n", t=TPC)).then_inc(s["f_dt"], 1)
                dv.tensor_copy(DT[GT:P, :, 1, :], MM[3][GT:P, :].rearrange("p (t n) -> p t n", t=TPC)).then_inc(s["f_dt"], 1)
                if a + 1 < NC:
                    low(a + 1)

                def gains(c):
                    cs = slice(4 * c, 4 * c + 4)
                    dv.wait_ge(s["f_pow2"], 2 * a + c + 1)
                    dv.wait_ge(s["f_z"], a + 1)
                    link(dv.scalar_tensor_tensor(out=sm1[:, p, YS, cs], in0=sm1[:, p, P2, cs], scalar=RD,
                                                 in1=sm1[:, p, RZ, cs], op0=ALU.mult, op1=ALU.mult))
                    for n in range(4 * c, 4 * c + 4):
                        dv.scalar_tensor_tensor(out=YN[:, 8 * a + n, :], in0=SL[n // 2][:, (n % 2) * D:(n % 2 + 1) * D],
                                                scalar=sm1[:, p, YS, n:n + 1], in1=g2[:], op0=ALU.mult, op1=ALU.mult
                                                ).then_inc(s["f_yn"], 1)

                if a + 1 < NC:
                    max_disp(a + 1)
                for c in range(2):
                    dv.wait_ge(s["f_ssq"], 8 * a + 4 * c + 4)
                    cs = slice(4 * c, 4 * c + 4)
                    dv.tensor_scalar(sm1[:, p, V2, cs], sm1[:, p, SS, cs], EL2, None, ALU.add).then_inc(s["f_v2"], 1)
                gains(0)
                gains(1)
                if a + 1 < NC:
                    max_comb(a + 1)
                for g in range(8):
                    dv.wait_ge(s["f_yte"], 8 * a + g + 1)
                    dv.tensor_copy(meT[:, :, :, 8 * a + g, :],
                                   YT[g % 4][0:DH, 0:2 * (P + 32)].rearrange("p (h n) -> p h n", h=2)[:, :, P:].rearrange(
                                       "p h (e m) -> p h e m", e=E1N)).then_inc(s["f_me"], 1)

            def copy_query(e):
                dv.wait_ge(s["g_tr"], 2 * e + 2)
                dv.tensor_copy(se2T[:, 1, :, e].rearrange("p g q m -> p q g m"),
                               TP[1][0:DH, :].rearrange("p (q g m) -> p q g m", q=E2N, g=NG)).then_inc(s["g_s"], 1)

            for e in range(E1N):
                p, m = e % 2, 2 * (e % 2)
                dv.wait_ge(s["g_ssq"], E2N * (e + 1))
                dv.tensor_scalar(sm2[:, p, 0], sm2[:, p, 2], EL2, None, ALU.add).then_inc(s["g_v"], 1)
                if e:
                    copy_query(e - 1)
                dv.wait_ge(s["g_pow"], e + 1)
                for q in range(E2N):
                    dv.tensor_scalar(se2n[:, p, q, :], MM[m + q // 2][:, (q % 2) * D:(q % 2 + 1) * D],
                                     sm2[:, p, 1, q:q + 1], RD, ALU.mult, ALU.mult).then_inc(s["g_n"], 1)
            copy_query(E1N - 1)

            dv.wait_ge(s["blk_ok"], 3)

            def logits2(q):
                dv.wait_ge(s["h_l2"], q + 1)
                if q >= 2:
                    dv.wait_ge(s["h_c"], GQ * (q - 1))
                    dv.wait_ge(s["h_tr"], q - 1)
                m4 = MM[0][:].rearrange("p (g n) -> p g n", g=GQ)
                dv.tensor_tensor(L2[:, q % 2], m4, blk[:].unsqueeze(1).broadcast_to([P, GQ, NS]), ALU.add).then_inc(s["h_l2m"], 1)
                dv.wait_ge(s["h_l2m"], q + 1)
                if q:
                    dv.wait_ge(s["h_c"], GQ * q)
                link(dv.tensor_reduce(sm3[:, 0, :], L2[:, q % 2], AX.X, ALU.max))
                dv.tensor_scalar(sm3[:, 1, :], sm3[:, 0, :], -1.0, None, ALU.mult).then_inc(s["h_mxc"], 1)
                dv.wait_ge(s["h_tr"], q + 1)
                if q:
                    dv.wait_ge(s["h_d"], GQ * q)
                link(dv.tensor_reduce(sm3[:, 4, :], MM[1][:].rearrange("p (g n) -> p g n", g=GQ), AX.X, ALU.max))
                dv.tensor_scalar(sm3[:, 5, :], sm3[:, 4, :], -1.0, None, ALU.mult).then_inc(s["h_mxd"], 1)

            logits2(0)
            for q in range(NQ):
                dv.wait_ge(s["h_c"], GQ * (q + 1))
                link(dv.reciprocal(sm3[:, 3, :], sm3[:, 2, :]))
                e1 = E1T[:, q * GQ * GT:(q + 1) * GQ * GT].rearrange("p (g t) -> p g t", g=GQ)
                dv.tensor_tensor(e1, e1, bc(sm3[:, 3, :], GT), ALU.mult).then_inc(s["h_cn"], 1)
                dv.wait_ge(s["h_d"], GQ * (q + 1))
                link(dv.reciprocal(sm3[:, 7, :], sm3[:, 6, :]))
                if q:
                    dv.wait_ge(s["h_dtr"], q)
                dv.tensor_tensor(D2n[:], D2T[:], bc(sm3[:, 7, :], NS), ALU.mult).then_inc(s["h_dn"], 1)
                if q + 1 < NQ:
                    logits2(q + 1)
                dv.wait_ge(s["h_sl"], q + 1)
                dv.tensor_copy(sl2T[:, 1, :, :, GQ * q:GQ * (q + 1)],
                               OP[1][0:DH, :].rearrange("p (g k m) -> p k m g", g=GQ, k=KE)).then_inc(s["h_sle"], 1)

            dv.wait_ge(s["ld_b1"], 16)

            def bias2(k, n, edge):
                dv.wait_ge(s["x_down"], k + 1)
                dv.wait_ge(s[f"ld_d{n}"], (k + (NW - n)) * (32 // NW))
                if edge >= 0 or n >= 2:
                    dv.wait_ge(s[f"st_o{n % 2}"], (k - n % 2) * 8)
                dv.tensor_tensor(osb[:, n % 2, :], OP[n % 2][:, 0:D], b2b[n][:], ALU.add).then_inc(s["x_o"], 1)

            def act(k, n, edge):
                dv.wait_ge(s["x_up"], k + 1)
                if edge >= 0 or n >= 2:
                    dv.wait_ge(s["x_down"], k - 1)
                for c in range(HID // P):
                    dv.wait_ge(s["x_gl"], k * (HID // P) + (c + 1))
                    dv.scalar_tensor_tensor(out=ac2[:, n % 2, c, :], in0=MM[2 * (n % 2)][:, c * P:(c + 1) * P],
                                            scalar=b1b[:, bass.ds(k, 1), c],
                                            in1=gl[:, n % 2, c, :], op0=ALU.add, op1=ALU.mult).then_inc(s["x_act"], 1)
                if edge >= 0 or n >= 1:
                    bias2(k - 1, (n - 1) % NW, -1 if edge < 0 else 0)

            experts(dv, act)
            bias2(KE - 1, NW - 1, 0)

            for t in range(NT):
                dv.wait_ge(s["y_o"], t + 1)
                dv.scalar_tensor_tensor(out=X[:, t, :], in0=OP[t % 2][:, 0:D], scalar=rz1[:, t:t + 1], in1=X[:, t, :],
                                        op0=ALU.mult, op1=ALU.add).then_inc(s["y_x"], 1)

        @block.tensor
        def _(pe):

            def turn(a):
                for t in range(TPC):
                    pe.wait_ge(s["f_xg"], TPC * a + t + 1)
                    if a >= 2 and t == 0:
                        pe.wait_ge(s["f_me"], 8 * (a - 1))
                    for h in range(H2):
                        r = pe.transpose(TP[h][0:PH[h], t * P:(t + 1) * P], xg[:, a % 2, t, h * P:h * P + PH[h]], ident[:])
                        if t == TPC - 1:
                            r.then_inc(s["f_tr"], 1)

            def by_slot(a):
                pe.wait_ge(s["f_hlo"], 2 * (a + 1))
                if a:
                    pe.wait_ge(s["f_d"], 8 * a)
                five(pe, MM[0][:], phihi, philo, slice(0, NS), hhi[:, a % 2], hlo[:, a % 2], slice(0, CH)).then_inc(s["f_lt"], 1)

            def by_token(a):
                if a:
                    pe.wait_ge(s["f_e"], TPC * a)
                for t in range(TPC):
                    r = five(pe, MM[1][:, t * NS:(t + 1) * NS], phihi, philo, slice(0, NS), hhi[:, a % 2], hlo[:, a % 2],
                             slice(t * P, (t + 1) * P), rows=True)
                r.then_inc(s["f_l"], 1)

            turn(0)
            by_slot(0)
            by_token(0)
            for a in range(NC):
                pe.wait_ge(s["f_d"], 8 * (a + 1))
                if a:
                    pe.wait_ge(s["f_yn"], 8 * a)
                for t in range(TPC):
                    r = pe.transpose(MM[3][:, t * P:(t + 1) * P], D1[:, t * P:(t + 1) * P], ident[:])
                r.then_inc(s["f_dtr"], 1)
                pe.wait_ge(s["f_e"], TPC * (a + 1))
                for t in range(TPC):
                    r = pe.transpose(MM[2][:, t * P:(t + 1) * P], E1[:, t, :], ident[:])
                r.then_inc(s["f_etr"], 1)
                if a + 1 < NC:
                    turn(a + 1)
                pe.wait_ge(s["f_dt"], 2 * (a + 2))
                if a:
                    pe.wait_ge(s["f_me"], 8 * a)
                for t in range(TPC):
                    if t == 3:
                        pe.wait_ge(s["f_e1t"], a + 1)
                    for g in range(2):
                        r = pe.matmul(SL[t][:, g * D:(g + 1) * D], DT[:, t, g, :], xg[:, a % 2, t, :], start=True, stop=True)
                    r.then_inc(s["f_sl"], 1)
                if a + 1 < NC:
                    by_slot(a + 1)
                    by_token(a + 1)
                for g in range(8):
                    n = 8 * a + g
                    pe.wait_ge(s["f_yn"], n + 1)
                    if g >= 4:
                        pe.wait_ge(s["f_me"], n - 3)
                    for h in range(H2):
                        r = pe.matmul(YT[g % 4][0:DH, h * (P + 32):(h + 1) * (P + 32)], YN[:, n, h * DH:(h + 1) * DH], iavg[:],
                                      start=True, stop=True)
                    r.then_inc(s["f_yt"], 1)

            def queries(e):
                pe.wait_ge(s[f"ld_ws{e % 2}"], 16 * (e // 2 + 1))
                if e == 0:
                    pe.wait_ge(s["f_me"], NG)
                    pe.wait_ge(s["f_e1t"], NC)
                if e >= 2:
                    pe.wait_ge(s["g_n"], E2N * (e - 1))
                for n in range(2):
                    for h in range(H2):
                        r = pe.matmul(MM[2 * (e % 2) + n][:, 0:2 * D], meT[:, h, e].rearrange("p g m -> p (g m)"),
                                      wsl[:, e % 2, h, 2 * n * D:2 * (n + 1) * D], start=(h == 0), stop=(h == 1))
                r.then_inc(s["g_se"], 1)

            queries(0)
            for e in range(E1N):
                if e + 1 < E1N:
                    queries(e + 1)
                pe.wait_ge(s["g_n"], E2N * (e + 1))
                for h in range(H2):
                    if e:
                        pe.wait_ge(s["g_ev"] if h == 0 else s["g_s"], e)
                    for q in range(E2N):
                        r = pe.transpose(TP[h][0:DH, q * P:(q + 1) * P], se2n[:, e % 2, q, h * DH:(h + 1) * DH], ident[:])
                    r.then_inc(s["g_tr"], 1)

            pe.wait_ge(s["g_ev"], E1N)
            pe.wait_ge(s["g_s"], E1N)

            def match(q):
                if q:
                    pe.wait_ge(s["h_l2m"], q)
                for g in range(GQ):
                    n = GQ * q + g
                    for h in range(H2):
                        r = pe.matmul(MM[0][:, g * NS:(g + 1) * NS], ynT[:, n, h, :],
                                      se2T[:, h, n].rearrange("p e q m -> p (e q m)"), start=(h == 0), stop=(h == 1))
                r.then_inc(s["h_l2"], 1)

            def match_turn(q):
                pe.wait_ge(s["h_l2m"], q + 1)
                if q:
                    pe.wait_ge(s["h_d"], GQ * q)
                for g in range(GQ):
                    r = pe.transpose(MM[1][:, g * NS:(g + 1) * NS], L2[:, q % 2, g, :], ident[:])
                r.then_inc(s["h_tr"], 1)

            match(0)
            match_turn(0)
            for q in range(NQ):
                if q + 1 < NQ:
                    match(q + 1)
                pe.wait_ge(s["h_cn"], q + 1)
                if q:
                    pe.wait_ge(s["h_wt"], q)
                for g in range(GQ):
                    n = GQ * q + g
                    r = pe.matmul(MM[3][:, g * GT:(g + 1) * GT], C2[:, q % 2, g, :], E1T[:, n * GT:(n + 1) * GT],
                                  start=True, stop=True)
                r.then_inc(s["h_w"], 1)
                pe.wait_ge(s["h_dn"], q + 1)
                if q:
                    pe.wait_ge(s["h_d2"], q)
                for g in range(GQ):
                    r = pe.transpose(MM[2][:, g * NS:(g + 1) * NS], D2n[:, g, :], ident[:])
                r.then_inc(s["h_dtr"], 1)
                if q + 1 < NQ:
                    match_turn(q + 1)
                pe.wait_ge(s["h_d2"], q + 1)
                if q:
                    pe.wait_ge(s["h_sle"], 2 * q)
                for g in range(GQ):
                    for h in range(H2):
                        r = pe.matmul(OP[h][0:DH, g * NS:(g + 1) * NS], YN[:, GQ * q + g, h * DH:(h + 1) * DH], D2[:, q % 2, g, :],
                                      start=True, stop=True)
                r.then_inc(s["h_sl"], 1)

            def up(k, n, edge):
                pe.wait_ge(s[f"ld_u{n}"], (k + (NW - n)) * (16 // NW))
                if edge >= 0 or n >= 2:
                    pe.wait_ge(s["x_act"], (k - 1) * (HID // P))
                for half in (1, 0):
                    for c in range(HID // P):
                        o = half * HID + c * P
                        for h in range(H2):
                            r = pe.matmul(MM[2 * (n % 2) + half][:, c * P:(c + 1) * P], w1b[n][:, h, o:o + P],
                                          sl2T[:, h, bass.ds(k, 1)].rearrange("p k m g -> p (k m g)"), start=(h == 0), stop=(h == 1))
                r.then_inc(s["x_up"], 1)

            def expert(k, n, edge):
                if edge <= 0 or n < NW - 1:
                    up(k + 1, (n + 1) % NW, 0 if edge >= 0 or n == NW - 1 else -1)
                pe.wait_ge(s["x_act"], (k + 1) * (HID // P))
                pe.wait_ge(s[f"ld_d{n}"], (k + (NW - n)) * (32 // NW))
                if edge >= 0 or n >= 2:
                    pe.wait_ge(s["x_o"], k - 1)
                for c in range(HID // P):
                    r = pe.matmul(OP[n % 2][:, 0:D], ac2[:, n % 2, c, :], w2b[n][:, c, :], start=(c == 0), stop=(c == 3))
                r.then_inc(s["x_down"], 1)

            pe.wait_ge(s["h_sle"], 2 * NQ)
            pe.wait_ge(s["h_wt"], NQ)
            up(0, 0, -1)
            experts(pe, expert)

            pe.wait_ge(s["st_o0"], 8 * KE)
            pe.wait_ge(s["st_o1"], 8 * KE)
            pe.wait_ge(s["x_o"], KE)
            for t in range(NT):
                if t >= 2:
                    pe.wait_ge(s["y_x"], t - 1)
                for g in range(2):
                    r = pe.matmul(OP[t % 2][g * GT:(g + 1) * GT, 0:D], E1T[:, t * P + g * GT:t * P + (g + 1) * GT],
                                  oall[:, 2 * t + g, :], start=True, stop=True)
                r.then_inc(s["y_o"], 1)


def build(nc, A, out):
    with ExitStack() as ctx:
        def ps(name):
            return ctx.enter_context(nc.psum_tensor(name, [P, 512], F32))

        keep = {
            "st_out": ctx.enter_context(nc.semaphore("st_out")),
            "MM": [ps(f"mm{k}") for k in range(4)],
            "TP": [ps(f"tp{h}") for h in range(2)],
            "OP": [ps(f"op{h}") for h in range(2)],
        }
        used = blocks(nc, A, keep)
        nc.all_engine_barrier()
        nc.clear_and_free_semaphores(used)
        nc.all_engine_barrier()
        mixture(nc, A, out, keep)


def layouts(i):
    import numpy as np
    a = {k: np.asarray(v) for k, v in i.items()}
    g = lambda n: a["L0_tok_" + n]
    L = LAYERS
    halves = lambda w: np.ascontiguousarray(w.reshape(w.shape[0], H2, DH, -1).transpose(0, 2, 1, 3))
    stack = lambda w: np.ascontiguousarray(np.stack([w[:, :P], np.concatenate([w[:, P:], w[:, P:]], 1)], 2))
    win = g("Win").transpose(0, 2, 1)
    wd, wb, wc = (g(n).transpose(0, 2, 1) for n in ("Wd", "WB", "WC"))
    uv = [win[:, :, :P], win[:, :, P:D], win[:, :, D + P:], win[:, :, D:D + P]]
    zbc = [wd[:, :, :P], wb[:, :, :P], wc[:, :, :P], wb[:, :, P:], wd[:, :, P:], wc[:, :, P:]]
    one, zero = np.ones((1, D), np.float32), np.zeros((1, D), np.float32)
    cw = g("convw")
    cols = [np.concatenate([g("ln_g"), one]), np.concatenate([g("ln_b"), zero])]
    for v in (g("b_in")[:, :D], cw[..., 0], g("convb"), g("b_in")[:, D:], g("bd"), cw[..., 1], cw[..., 2], cw[..., 3], g("bB"), g("bC")):
        cols.append(np.concatenate([v, zero]))
    pc = stack(np.stack(cols, -1)).transpose(1, 0, 2, 3)
    aw = lambda n: a["L0_attn_" + n]
    attn = np.concatenate([aw("Wq"), aw("Wk"), aw("Wf"), aw("Wf"), aw("Wv"), aw("Wo")], 1)[None]
    ff = lambda n: a["L0_ffn_" + n]
    r = {
        "slots1": np.concatenate([ff("slots1").reshape(NS, D), ff("slots1").reshape(NS, D)[:, P:]], 1),
        "g2": np.repeat(ff("gamma2"), S1N, axis=0),
        "gin": np.broadcast_to(ff("gamma_in"), (P, D)),
        "wsl": halves(ff("w_slot2")),
        "w1": halves(ff("w1").reshape(KE, D, 2 * HID)),
        "w2": ff("w2").reshape(KE, HID // P, P, D).transpose(0, 2, 1, 3),
        "b1": ff("b1").reshape(KE, 2 * HID // P, P).transpose(2, 0, 1),
        "b2": ff("b2").reshape(KE, D),
        "aw": stack(attn)[0],
        "abf": np.concatenate([aw("bf"), aw("bf")])[:, None],
        "agb": stack(np.stack([aw("gamma"), aw("beta")], -1)[None])[0],
        "tok": a["x"].reshape(NT, P).T,
        "pos": g("pos_enc").reshape(S // P, P, D).transpose(1, 0, 2),
        "emb": g("embedding"),
        "pc": pc,
        "wu": stack(np.concatenate(uv, 2)), "wz": stack(np.concatenate(zbc, 2)), "wo": stack(g("Wout").transpose(0, 2, 1)),
        "bout": np.broadcast_to(g("bout")[:, None, :], (L, P, D)),
    }
    return {k: np.ascontiguousarray(v) for k, v in r.items()}
def kernel(**inputs):
    import numpy as np
    import concourse.bacc as bacc
    from concourse.bass_utils import run_bass_kernel_spmd

    nc = bacc.Bacc("TRN2", target_bir_lowering=False, num_devices=1)
    arrays = layouts(inputs)
    aps = {n: nc.dram_tensor(n, v.shape, mybir.dt.from_np(v.dtype), kind="ExternalInput").ap() for n, v in arrays.items()}
    out = nc.dram_tensor("out_0", (P, NT, D), F32, kind="ExternalOutput").ap()
    build(nc, aps, out)
    r = run_bass_kernel_spmd(nc, [arrays], core_ids=[0])
    return np.ascontiguousarray(r.results[0]["out_0"].transpose(1, 0, 2)).reshape(B, S, D)
```
